# Optimizing a Trainium2 kernel written in Bass

```python
import numpy as np
import jax
import jax.numpy as jnp

def _softmax(x, axis=-1):
    return jax.nn.softmax(x, axis=axis)

def _gelu(x):
    return jax.nn.gelu(x, approximate=True)

def _silu(x):
    return jax.nn.silu(x)

def _sigmoid(x):
    return jax.nn.sigmoid(x)

def _layernorm(x, axis=-1, eps=1e-05):
    m = jnp.mean(x, axis=axis, keepdims=True)
    v = jnp.var(x, axis=axis, keepdims=True)
    return (x - m) / jnp.sqrt(v + eps)

def _scatter_add(tgt, idx, src, axis=0):
    return tgt.at[idx].add(src)

def _segment_sum(src, seg, n):
    return jax.ops.segment_sum(src, seg, n)
kernel_name = 'mk_gnn_ffn_d4_gnn_r8_fc1d30'

def setup_inputs(seed: int=0):
    np.random.seed(seed)
    _w = jnp.asarray

    def _rec_inputs():
        import jax
        import jax.numpy as jnp
        _gk = jax.random.key(seed)
        x = -0.0005207 + 1.001 * jax.random.normal(jax.random.fold_in(_gk, 1), (512, 512), jnp.float32)
        _s = jax.random.randint(jax.random.fold_in(_gk, 2), (4096,), 0, 512, jnp.int32)
        _d = jax.random.randint(jax.random.fold_in(_gk, 3), (4096,), 0, 512, jnp.int32)
        _loop = jnp.arange(512, dtype=jnp.int32)
        src = jnp.concatenate([_s, _d, _loop])
        dst = jnp.concatenate([_d, _s, _loop])
        _o = jnp.argsort(dst, stable=True)
        src = src[_o]
        dst = dst[_o]
        edge_attr_2 = 0.00222621 + 0.99962 * jax.random.normal(jax.random.fold_in(_gk, 11), (8704, 2), jnp.float32)
        edge_weight = jax.random.uniform(jax.random.fold_in(_gk, 13), (8704,), jnp.float32, 0.0, 0.999998)
        return (x, src, dst, edge_attr_2, edge_weight)
    x, src, dst, edge_attr_2, edge_weight = _rec_inputs()

    def _L0_gnn_setup():
        import jax, jax.numpy as jnp
        import numpy as np
        N_HEADS = 8
        NEG = -1e+30
        key = jax.random.key(seed)
        ks = jax.random.split(key, 12)
        N, H, E = (512, 512, 16384)
        s = 1.0 / np.sqrt(H)
        x = jax.random.normal(ks[0], (N, H), dtype=jnp.float32)
        edge_index = jax.random.randint(ks[1], (2, E), 0, N, dtype=jnp.int64)
        Wq = jax.random.normal(ks[2], (H, H), dtype=jnp.float32) * s
        Wk = jax.random.normal(ks[3], (H, H), dtype=jnp.float32) * s
        Wv = jax.random.normal(ks[4], (H, H), dtype=jnp.float32) * s
        Wo = jax.random.normal(ks[5], (H, H), dtype=jnp.float32) * s
        bq = jax.random.normal(ks[6], (H,), dtype=jnp.float32) * 0.01
        bk = jax.random.normal(ks[7], (H,), dtype=jnp.float32) * 0.01
        bv = jax.random.normal(ks[8], (H,), dtype=jnp.float32) * 0.01
        bo = jax.random.normal(ks[9], (H,), dtype=jnp.float32) * 0.01
        return {'x': x, 'edge_index': edge_index, 'Wq': Wq, 'bq': bq, 'Wk': Wk, 'bk': bk, 'Wv': Wv, 'bv': bv, 'Wo': Wo, 'bo': bo}
    _L0_gnn_all = _L0_gnn_setup()
    _L0_gnn_in = {k: v for k, v in _L0_gnn_all.items() if k in ('Wq', 'bq', 'Wk', 'bk', 'Wv', 'bv', 'Wo', 'bo')}
    del _L0_gnn_all

    def _L0_ffn_setup():
        import jax, jax.numpy as jnp
        import numpy as np
        B, S, D, H, E = (4, 256, 512, 8, 8)
        FF = 4 * D
        HD = D // H
        EPS = 1e-05

        def _layernorm(x, g, b):
            mu = jnp.mean(x, axis=-1, keepdims=True)
            var = jnp.mean((x - mu) ** 2, axis=-1, keepdims=True)
            return (x - mu) * jax.lax.rsqrt(var + EPS) * g + b
        key = jax.random.key(seed)
        ks = jax.random.split(key, 16)
        s = 0.02
        return {'x': jax.random.normal(ks[0], (B, S, D), dtype=jnp.float32), 'ln1_g': jnp.ones((D,), jnp.float32), 'ln1_b': jnp.zeros((D,), jnp.float32), 'Wq': jax.random.normal(ks[1], (D, D), jnp.float32) * s, 'bq': jnp.zeros((D,), jnp.float32), 'Wk': jax.random.normal(ks[2], (D, D), jnp.float32) * s, 'bk': jnp.zeros((D,), jnp.float32), 'Wv': jax.random.normal(ks[3], (D, D), jnp.float32) * s, 'bv': jnp.zeros((D,), jnp.float32), 'Wo': jax.random.normal(ks[4], (D, D), jnp.float32) * s, 'bo': jnp.zeros((D,), jnp.float32), 'gate_W': jax.random.normal(ks[5], (D, E), jnp.float32) * s, 'gate_b': jnp.zeros((E,), jnp.float32), 'W1': jax.random.normal(ks[6], (E, D, FF), jnp.float32) * s, 'b1': jnp.zeros((E, FF), jnp.float32), 'W2': jax.random.normal(ks[7], (E, FF, D), jnp.float32) * s, 'b2': jnp.zeros((E, D), jnp.float32)}
    _L0_ffn_all = _L0_ffn_setup()
    _L0_ffn_in = {k: v for k, v in _L0_ffn_all.items() if k in ('ln1_g', 'ln1_b', 'Wq', 'bq', 'Wk', 'bk', 'Wv', 'bv', 'Wo', 'bo', 'gate_W', 'gate_b', 'W1', 'b1', 'W2', 'b2')}
    del _L0_ffn_all

    def _L1_gnn_setup():
        import jax, jax.numpy as jnp
        import numpy as np
        N, E, D, ED, L = (2048, 32768, 512, 2, 3)
        EPS = 1e-05
        SLOPE = 0.2

        def _segment_softmax(logits, seg, n):
            m = jax.ops.segment_max(logits, seg, num_segments=n)
            m = jnp.where(jnp.isfinite(m), m, 0.0)
            ex = jnp.exp(logits - m[seg])
            den = jax.ops.segment_sum(ex, seg, num_segments=n)
            return ex / (den[seg] + 1e-16)

        def _forward(x, edge_attr, Wl, bl, Wr, br, We, att, b_out, gamma, beta, edge_index):
            n = x.shape[0]
            src, dst = (edge_index[0], edge_index[1])
            ones = jnp.ones((src.shape[0],), x.dtype)
            cnt = jax.ops.segment_sum(ones, dst, num_segments=n)
            mean_ea = jax.ops.segment_sum(edge_attr, dst, num_segments=n) / jnp.maximum(cnt, 1.0)[:, None]
            loop = jnp.arange(n, dtype=edge_index.dtype)
            src2 = jnp.concatenate([src, loop])
            dst2 = jnp.concatenate([dst, loop])
            ea2 = jnp.concatenate([edge_attr, mean_ea], axis=0)
            for k in range(Wl.shape[0]):
                xl = x @ Wl[k] + bl[k]
                xr = x @ Wr[k] + br[k]
                ef = ea2 @ We[k]
                m = jax.nn.leaky_relu(xl[src2] + xr[dst2] + ef, SLOPE)
                logit = m @ att[k]
                alpha = _segment_softmax(logit, dst2, n)
                out = jax.ops.segment_sum(xl[src2] * alpha[:, None], dst2, num_segments=n) + b_out[k]
                h = out + x
                mu = jnp.mean(h, axis=-1, keepdims=True)
                var = jnp.var(h, axis=-1, keepdims=True)
                h = (h - mu) * jax.lax.rsqrt(var + EPS) * gamma[k] + beta[k]
                x = jax.nn.relu(h)
            return x
        key = jax.random.key(seed)
        ks = jax.random.split(key, 8)
        s = np.float32(1.0 / np.sqrt(D))
        return dict(x=jax.random.normal(ks[0], (N, D), jnp.float32), edge_attr=jax.random.normal(ks[1], (E, ED), jnp.float32), Wl=jax.random.normal(ks[2], (L, D, D), jnp.float32) * s, bl=jnp.zeros((L, D), jnp.float32), Wr=jax.random.normal(ks[3], (L, D, D), jnp.float32) * s, br=jnp.zeros((L, D), jnp.float32), We=jax.random.normal(ks[4], (L, ED, D), jnp.float32) * s, att=jax.random.normal(ks[5], (L, D), jnp.float32) * s, b_out=jnp.zeros((L, D), jnp.float32), gamma=jnp.ones((L, D), jnp.float32), beta=jnp.zeros((L, D), jnp.float32), edge_index=jax.random.randint(ks[6], (2, E), 0, N, dtype=jnp.int32))
    _L1_gnn_all = _L1_gnn_setup()
    _L1_gnn_in = {k: v for k, v in _L1_gnn_all.items() if k in ('Wl', 'bl', 'Wr', 'br', 'We', 'att', 'b_out', 'gamma', 'beta')}
    del _L1_gnn_all

    def _L1_ffn_setup():
        import jax, jax.numpy as jnp
        import numpy as np
        MICRO_BATCHES = 2
        TOP_K = 2
        D = 512
        E = 8
        B, S = (8, 1024)
        key = jax.random.key(seed)
        ks = jax.random.split(key, 12)
        s = 0.02
        return {'x': jax.random.normal(ks[0], (B, S, D), dtype=jnp.float32), 'ln_g': jnp.ones((D,), jnp.float32), 'ln_b': jnp.zeros((D,), jnp.float32), 'attn_w': jax.random.normal(ks[1], (D, D), jnp.float32) * s, 'attn_b': jnp.zeros((D,), jnp.float32), 'gate_w': jax.random.normal(ks[2], (E, D), jnp.float32) * s, 'fc1_w': jax.random.normal(ks[3], (E, 4 * D, D), jnp.float32) * s, 'fc1_b': jnp.zeros((E, 4 * D), jnp.float32), 'fc2_w': jax.random.normal(ks[4], (E, D, 4 * D), jnp.float32) * s, 'fc2_b': jnp.zeros((E, D), jnp.float32), 'next_w': jax.random.normal(ks[5], (D, D), jnp.float32) * s, 'next_b': jnp.zeros((D,), jnp.float32)}
    _L1_ffn_all = _L1_ffn_setup()
    _L1_ffn_in = {k: v for k, v in _L1_ffn_all.items() if k in ('ln_g', 'ln_b', 'attn_w', 'attn_b', 'gate_w', 'fc1_w', 'fc1_b', 'fc2_w', 'fc2_b', 'next_w', 'next_b')}
    del _L1_ffn_all

    def _L2_gnn_setup():
        import jax, jax.numpy as jnp
        import numpy as np
        N_NODES = 6250
        key = jax.random.key(seed)
        k1, k2, k3, k4, k5 = jax.random.split(key, 5)
        N, E, DIN, DOUT = (N_NODES, 200000, 512, 512)
        x = jax.random.normal(k1, (N, DIN), dtype=jnp.float32)
        weight = jax.random.normal(k2, (DIN, DOUT), dtype=jnp.float32) * (1.0 / np.sqrt(DIN))
        bias = jax.random.normal(k3, (DOUT,), dtype=jnp.float32) * 0.02
        edge_index = jax.random.randint(k4, (2, E), 0, N, dtype=jnp.int64)
        edge_vals = jax.random.uniform(k5, (E,), dtype=jnp.float32)
        return {'x': x, 'weight': weight, 'bias': bias, 'edge_index': edge_index, 'edge_vals': edge_vals}
    _L2_gnn_all = _L2_gnn_setup()
    _L2_gnn_in = {k: v for k, v in _L2_gnn_all.items() if k in ('weight', 'bias')}
    del _L2_gnn_all

    def _L2_ffn_setup():
        import jax, jax.numpy as jnp
        import numpy as np
        D, H, E, B, S = (512, 256, 16, 8, 1024)
        MAX_GROUP_SIZE = 512
        MIN_CAPACITY = 8
        CAPACITY_FACTOR = 1.0

        def _group_dims(num_tokens, num_experts):
            num_groups = -(-num_tokens // MAX_GROUP_SIZE)
            while num_tokens % num_groups != 0 or num_groups % num_experts != 0:
                num_groups += 1
            return (num_tokens // num_groups, num_groups)
        key = jax.random.key(seed)
        ks = jax.random.split(key, 6)
        s = 0.02
        return {'x': jax.random.normal(ks[0], (B, S, D), jnp.float32), 'gate_w': jax.random.normal(ks[1], (D, E), jnp.float32) * s, 'w1': jax.random.normal(ks[2], (E, D, H), jnp.float32) * s, 'b1': jnp.zeros((E, H), jnp.float32), 'w2': jax.random.normal(ks[3], (E, H, D), jnp.float32) * s, 'b2': jnp.zeros((E, D), jnp.float32), 'sw1': jax.random.normal(ks[4], (D, H), jnp.float32) * s, 'sb1': jnp.zeros((H,), jnp.float32), 'sw2': jax.random.normal(ks[5], (H, D), jnp.float32) * s, 'sb2': jnp.zeros((D,), jnp.float32)}
    _L2_ffn_all = _L2_ffn_setup()
    _L2_ffn_in = {k: v for k, v in _L2_ffn_all.items() if k in ('gate_w', 'w1', 'b1', 'w2', 'b2', 'sw1', 'sb1', 'sw2', 'sb2')}
    del _L2_ffn_all

    def _L3_gnn_setup():
        import jax, jax.numpy as jnp
        import numpy as np
        N_NODES = 4096
        N_EDGES = 32768
        D = 512
        NUM_EXPERTS = 4
        TOP_K = 2
        LAYERS = 2
        key = jax.random.key(seed)
        ks = jax.random.split(key, 8)
        x = jax.random.normal(ks[0], (N_NODES, D), dtype=jnp.float32)
        edge_index = jax.random.randint(ks[1], (2, N_EDGES), 0, N_NODES, dtype=jnp.int64)
        s = 1.0 / np.sqrt(D)
        gate_W = jax.random.uniform(ks[2], (D, NUM_EXPERTS), jnp.float32, -s, s)
        gate_b = jax.random.uniform(ks[3], (NUM_EXPERTS,), jnp.float32, -s, s)
        Wl = jax.random.uniform(ks[4], (NUM_EXPERTS, LAYERS, D, D), jnp.float32, -s, s)
        bl = jax.random.uniform(ks[5], (NUM_EXPERTS, LAYERS, D), jnp.float32, -s, s)
        Wr = jax.random.uniform(ks[6], (NUM_EXPERTS, LAYERS, D, D), jnp.float32, -s, s)
        return {'x': x, 'gate_W': gate_W, 'gate_b': gate_b, 'Wl': Wl, 'bl': bl, 'Wr': Wr, 'edge_index': edge_index}
    _L3_gnn_all = _L3_gnn_setup()
    _L3_gnn_in = {k: v for k, v in _L3_gnn_all.items() if k in ('gate_W', 'gate_b', 'Wl', 'bl', 'Wr')}
    del _L3_gnn_all

    def _L3_ffn_setup():
        import jax, jax.numpy as jnp
        import numpy as np
        B, S, D, H, E, K = (2, 256, 512, 1024, 8, 2)

        def _moe(x, router_w, w_gate, w_up, w_down):
            bsz, seq, d = x.shape
            flat = x.reshape(-1, d)
            logits = flat @ router_w.T
            topk_vals, topk_idx = jax.lax.top_k(logits, K)
            topk_w = jax.nn.softmax(topk_vals, axis=-1)
            s = flat.shape[0]
            dense_w = jnp.zeros((s, E), dtype=flat.dtype).at[jnp.arange(s)[:, None], topk_idx].add(topk_w)
            g = jnp.einsum('sd,edh->esh', flat, w_gate)
            u = jnp.einsum('sd,edh->esh', flat, w_up)
            y = jnp.einsum('esh,ehd->esd', jax.nn.silu(g) * u, w_down)
            out = jnp.einsum('esd,se->sd', y, dense_w)
            return out.reshape(bsz, seq, d)
        key = jax.random.key(seed)
        k1, k2, k3, k4, k5 = jax.random.split(key, 5)
        return {'x': jax.random.normal(k1, (B, S, D), dtype=jnp.float32), 'router_w': jax.random.normal(k2, (E, D), dtype=jnp.float32) * D ** (-0.5), 'w_gate': jax.random.normal(k3, (E, D, H), dtype=jnp.float32) * D ** (-0.5), 'w_up': jax.random.normal(k4, (E, D, H), dtype=jnp.float32) * D ** (-0.5), 'w_down': jax.random.normal(k5, (E, H, D), dtype=jnp.float32) * H ** (-0.5)}
    _L3_ffn_all = _L3_ffn_setup()
    _L3_ffn_in = {k: v for k, v in _L3_ffn_all.items() if k in ('router_w', 'w_gate', 'w_up', 'w_down')}
    del _L3_ffn_all
    return {'x': x, 'src': src, 'dst': dst, 'edge_attr_2': edge_attr_2, 'edge_weight': edge_weight, 'L0_gnn_Wq': _L0_gnn_in['Wq'], 'L0_gnn_bq': _L0_gnn_in['bq'], 'L0_gnn_Wk': _L0_gnn_in['Wk'], 'L0_gnn_bk': _L0_gnn_in['bk'], 'L0_gnn_Wv': _L0_gnn_in['Wv'], 'L0_gnn_bv': _L0_gnn_in['bv'], 'L0_gnn_Wo': _L0_gnn_in['Wo'], 'L0_gnn_bo': _L0_gnn_in['bo'], 'L0_ffn_ln1_g': _L0_ffn_in['ln1_g'], 'L0_ffn_ln1_b': _L0_ffn_in['ln1_b'], 'L0_ffn_Wq': _L0_ffn_in['Wq'], 'L0_ffn_bq': _L0_ffn_in['bq'], 'L0_ffn_Wk': _L0_ffn_in['Wk'], 'L0_ffn_bk': _L0_ffn_in['bk'], 'L0_ffn_Wv': _L0_ffn_in['Wv'], 'L0_ffn_bv': _L0_ffn_in['bv'], 'L0_ffn_Wo': _L0_ffn_in['Wo'], 'L0_ffn_bo': _L0_ffn_in['bo'], 'L0_ffn_gate_W': _L0_ffn_in['gate_W'], 'L0_ffn_gate_b': _L0_ffn_in['gate_b'], 'L0_ffn_W1': _L0_ffn_in['W1'], 'L0_ffn_b1': _L0_ffn_in['b1'], 'L0_ffn_W2': _L0_ffn_in['W2'], 'L0_ffn_b2': _L0_ffn_in['b2'], 'L1_gnn_Wl': _L1_gnn_in['Wl'], 'L1_gnn_bl': _L1_gnn_in['bl'], 'L1_gnn_Wr': _L1_gnn_in['Wr'], 'L1_gnn_br': _L1_gnn_in['br'], 'L1_gnn_We': _L1_gnn_in['We'], 'L1_gnn_att': _L1_gnn_in['att'], 'L1_gnn_b_out': _L1_gnn_in['b_out'], 'L1_gnn_gamma': _L1_gnn_in['gamma'], 'L1_gnn_beta': _L1_gnn_in['beta'], 'L1_ffn_ln_g': _L1_ffn_in['ln_g'], 'L1_ffn_ln_b': _L1_ffn_in['ln_b'], 'L1_ffn_attn_w': _L1_ffn_in['attn_w'], 'L1_ffn_attn_b': _L1_ffn_in['attn_b'], 'L1_ffn_gate_w': _L1_ffn_in['gate_w'], 'L1_ffn_fc1_w': _L1_ffn_in['fc1_w'], 'L1_ffn_fc1_b': _L1_ffn_in['fc1_b'], 'L1_ffn_fc2_w': _L1_ffn_in['fc2_w'], 'L1_ffn_fc2_b': _L1_ffn_in['fc2_b'], 'L1_ffn_next_w': _L1_ffn_in['next_w'], 'L1_ffn_next_b': _L1_ffn_in['next_b'], 'L2_gnn_weight': _L2_gnn_in['weight'], 'L2_gnn_bias': _L2_gnn_in['bias'], 'L2_ffn_gate_w': _L2_ffn_in['gate_w'], 'L2_ffn_w1': _L2_ffn_in['w1'], 'L2_ffn_b1': _L2_ffn_in['b1'], 'L2_ffn_w2': _L2_ffn_in['w2'], 'L2_ffn_b2': _L2_ffn_in['b2'], 'L2_ffn_sw1': _L2_ffn_in['sw1'], 'L2_ffn_sb1': _L2_ffn_in['sb1'], 'L2_ffn_sw2': _L2_ffn_in['sw2'], 'L2_ffn_sb2': _L2_ffn_in['sb2'], 'L3_gnn_gate_W': _L3_gnn_in['gate_W'], 'L3_gnn_gate_b': _L3_gnn_in['gate_b'], 'L3_gnn_Wl': _L3_gnn_in['Wl'], 'L3_gnn_bl': _L3_gnn_in['bl'], 'L3_gnn_Wr': _L3_gnn_in['Wr'], 'L3_ffn_router_w': _L3_ffn_in['router_w'], 'L3_ffn_w_gate': _L3_ffn_in['w_gate'], 'L3_ffn_w_up': _L3_ffn_in['w_up'], 'L3_ffn_w_down': _L3_ffn_in['w_down']}

def reference(x, src, dst, edge_attr_2, edge_weight, L0_gnn_Wq, L0_gnn_bq, L0_gnn_Wk, L0_gnn_bk, L0_gnn_Wv, L0_gnn_bv, L0_gnn_Wo, L0_gnn_bo, L0_ffn_ln1_g, L0_ffn_ln1_b, L0_ffn_Wq, L0_ffn_bq, L0_ffn_Wk, L0_ffn_bk, L0_ffn_Wv, L0_ffn_bv, L0_ffn_Wo, L0_ffn_bo, L0_ffn_gate_W, L0_ffn_gate_b, L0_ffn_W1, L0_ffn_b1, L0_ffn_W2, L0_ffn_b2, L1_gnn_Wl, L1_gnn_bl, L1_gnn_Wr, L1_gnn_br, L1_gnn_We, L1_gnn_att, L1_gnn_b_out, L1_gnn_gamma, L1_gnn_beta, L1_ffn_ln_g, L1_ffn_ln_b, L1_ffn_attn_w, L1_ffn_attn_b, L1_ffn_gate_w, L1_ffn_fc1_w, L1_ffn_fc1_b, L1_ffn_fc2_w, L1_ffn_fc2_b, L1_ffn_next_w, L1_ffn_next_b, L2_gnn_weight, L2_gnn_bias, L2_ffn_gate_w, L2_ffn_w1, L2_ffn_b1, L2_ffn_w2, L2_ffn_b2, L2_ffn_sw1, L2_ffn_sb1, L2_ffn_sw2, L2_ffn_sb2, L3_gnn_gate_W, L3_gnn_gate_b, L3_gnn_Wl, L3_gnn_bl, L3_gnn_Wr, L3_ffn_router_w, L3_ffn_w_gate, L3_ffn_w_up, L3_ffn_w_down):
    import jax
    import jax.numpy as jnp

    def _L0_gnn_ref(x, edge_index, Wq, bq, Wk, bk, Wv, bv, Wo, bo):
        import jax, jax.numpy as jnp
        import numpy as np
        N_HEADS = 8
        NEG = -1e+30
        N, H = x.shape
        hd = H // N_HEADS
        scale = 1.0 / np.sqrt(hd)
        adj = jnp.zeros((N, N), dtype=bool).at[edge_index[0], edge_index[1]].set(True)
        q = (x @ Wq + bq).reshape(N, N_HEADS, hd)
        k = (x @ Wk + bk).reshape(N, N_HEADS, hd)
        v = (x @ Wv + bv).reshape(N, N_HEADS, hd)
        scores = jnp.einsum('nhd,mhd->hnm', q, k) * scale
        scores = jnp.where(adj[None], scores, NEG)
        attn = jax.nn.softmax(scores, axis=-1)
        out = jnp.einsum('hnm,mhd->nhd', attn, v).reshape(N, H)
        has_edge = adj.any(axis=1)
        out = jnp.where(has_edge[:, None], out, 0.0)
        return out @ Wo + bo

    def _L0_ffn_ref(x, ln1_g, ln1_b, Wq, bq, Wk, bk, Wv, bv, Wo, bo, gate_W, gate_b, W1, b1, W2, b2):
        import jax, jax.numpy as jnp
        import numpy as np
        B, S, D, H, E = (4, 256, 512, 8, 8)
        FF = 4 * D
        HD = D // H
        EPS = 1e-05

        def _layernorm(x, g, b):
            mu = jnp.mean(x, axis=-1, keepdims=True)
            var = jnp.mean((x - mu) ** 2, axis=-1, keepdims=True)
            return (x - mu) * jax.lax.rsqrt(var + EPS) * g + b
        b, s, d = x.shape
        q = (x @ Wq + bq).reshape(b, s, H, HD)
        k = (x @ Wk + bk).reshape(b, s, H, HD)
        v = (x @ Wv + bv).reshape(b, s, H, HD)
        scores = jnp.einsum('bqhd,bkhd->bhqk', q, k) / jnp.sqrt(jnp.float32(HD))
        attn = jax.nn.softmax(scores, axis=-1)
        o = jnp.einsum('bhqk,bkhd->bqhd', attn, v).reshape(b, s, d) @ Wo + bo
        h = _layernorm(x + o, ln1_g, ln1_b)
        t = h.reshape(b * s, d)
        probs = jax.nn.softmax(t @ gate_W + gate_b, axis=-1)
        idx = jnp.argmax(probs, axis=-1)
        gw = jnp.max(probs, axis=-1)
        hid = jax.nn.gelu(jnp.einsum('nd,edf->enf', t, W1) + b1[:, None, :])
        out_all = jnp.einsum('enf,efd->end', hid, W2) + b2[:, None, :]
        onehot = jax.nn.one_hot(idx, E, dtype=t.dtype)
        out = jnp.einsum('ne,end->nd', onehot, out_all)
        out = out * gw[:, None]
        return out.reshape(b, s, d)

    def _L1_gnn_ref(x, edge_attr, Wl, bl, Wr, br, We, att, b_out, gamma, beta, edge_index):
        import jax, jax.numpy as jnp
        import numpy as np
        N, E, D, ED, L = (2048, 32768, 512, 2, 3)
        EPS = 1e-05
        SLOPE = 0.2

        def _segment_softmax(logits, seg, n):
            m = jax.ops.segment_max(logits, seg, num_segments=n)
            m = jnp.where(jnp.isfinite(m), m, 0.0)
            ex = jnp.exp(logits - m[seg])
            den = jax.ops.segment_sum(ex, seg, num_segments=n)
            return ex / (den[seg] + 1e-16)

        def _forward(x, edge_attr, Wl, bl, Wr, br, We, att, b_out, gamma, beta, edge_index):
            n = x.shape[0]
            src, dst = (edge_index[0], edge_index[1])
            ones = jnp.ones((src.shape[0],), x.dtype)
            cnt = jax.ops.segment_sum(ones, dst, num_segments=n)
            mean_ea = jax.ops.segment_sum(edge_attr, dst, num_segments=n) / jnp.maximum(cnt, 1.0)[:, None]
            loop = jnp.arange(n, dtype=edge_index.dtype)
            src2 = jnp.concatenate([src, loop])
            dst2 = jnp.concatenate([dst, loop])
            ea2 = jnp.concatenate([edge_attr, mean_ea], axis=0)
            for k in range(Wl.shape[0]):
                xl = x @ Wl[k] + bl[k]
                xr = x @ Wr[k] + br[k]
                ef = ea2 @ We[k]
                m = jax.nn.leaky_relu(xl[src2] + xr[dst2] + ef, SLOPE)
                logit = m @ att[k]
                alpha = _segment_softmax(logit, dst2, n)
                out = jax.ops.segment_sum(xl[src2] * alpha[:, None], dst2, num_segments=n) + b_out[k]
                h = out + x
                mu = jnp.mean(h, axis=-1, keepdims=True)
                var = jnp.var(h, axis=-1, keepdims=True)
                h = (h - mu) * jax.lax.rsqrt(var + EPS) * gamma[k] + beta[k]
                x = jax.nn.relu(h)
            return x
        return _forward(x, edge_attr, Wl, bl, Wr, br, We, att, b_out, gamma, beta, edge_index)

    def _L1_ffn_ref(x, ln_g, ln_b, attn_w, attn_b, gate_w, fc1_w, fc1_b, fc2_w, fc2_b, next_w, next_b):
        import jax, jax.numpy as jnp
        import numpy as np
        MICRO_BATCHES = 2
        TOP_K = 2
        D = 512
        E = 8
        B, S = (8, 1024)
        b, s, d = x.shape
        xf = x.reshape(b * s, d)
        mu = jnp.mean(xf, axis=-1, keepdims=True)
        var = jnp.var(xf, axis=-1, keepdims=True)
        normed = (xf - mu) / jnp.sqrt(var + 1e-05) * ln_g + ln_b
        x_attn = normed @ attn_w.T + attn_b + xf
        logits = x_attn @ gate_w.T
        _scores, _indices = jax.lax.top_k(logits, TOP_K)
        e = fc1_w.shape[0]
        t = b * s // (MICRO_BATCHES * e)
        tok = x_attn.reshape(MICRO_BATCHES, e, t, d)
        h = jnp.einsum('meti,ehi->meth', tok, fc1_w) + fc1_b[None, :, None, :]
        h = jax.nn.gelu(h, approximate=False)
        y = jnp.einsum('meth,edh->metd', h, fc2_w) + fc2_b[None, :, None, :]
        yf = y.reshape(b * s, d)
        out = jax.nn.gelu(yf @ next_w.T + next_b, approximate=False)
        return out.reshape(b, s, d)

    def _L2_gnn_ref(x, weight, bias, edge_index, edge_vals):
        import jax, jax.numpy as jnp
        import numpy as np
        N_NODES = 6250
        support = x @ weight
        dst, src = (edge_index[0], edge_index[1])
        msgs = support[src] * edge_vals[:, None]
        out = jax.ops.segment_sum(msgs, dst, num_segments=x.shape[0])
        return out + bias

    def _L2_ffn_ref(x, gate_w, w1, b1, w2, b2, sw1, sb1, sw2, sb2):
        import jax, jax.numpy as jnp
        import numpy as np
        D, H, E, B, S = (512, 256, 16, 8, 1024)
        MAX_GROUP_SIZE = 512
        MIN_CAPACITY = 8
        CAPACITY_FACTOR = 1.0

        def _group_dims(num_tokens, num_experts):
            num_groups = -(-num_tokens // MAX_GROUP_SIZE)
            while num_tokens % num_groups != 0 or num_groups % num_experts != 0:
                num_groups += 1
            return (num_tokens // num_groups, num_groups)
        Bn, Sn, Dn = x.shape
        En = gate_w.shape[1]
        T = Bn * Sn
        group_size, num_groups = _group_dims(T, En)
        cap = max(int(round(CAPACITY_FACTOR * group_size * num_groups / En)), MIN_CAPACITY)
        xg = x.reshape(num_groups, group_size, Dn)
        logits = jnp.einsum('gsd,de->gse', xg, gate_w)
        probs = jax.nn.softmax(logits, axis=-1)
        flat_probs = probs.transpose(2, 0, 1).reshape(En, T)
        scores, tok_idx = jax.lax.top_k(flat_probs, cap)
        xf = x.reshape(T, Dn)
        toks = xf[tok_idx]
        h = jax.nn.gelu(jnp.einsum('ecd,edh->ech', toks, w1) + b1[:, None, :])
        y = jnp.einsum('ech,ehd->ecd', h, w2) + b2[:, None, :]
        y = y * scores[..., None]
        routed = jnp.zeros_like(xf).at[tok_idx.reshape(-1)].add(y.reshape(-1, Dn))
        shared = jax.nn.gelu(xf @ sw1 + sb1) @ sw2 + sb2
        out = (routed + shared).reshape(Bn, Sn, Dn)
        return out

    def _L3_gnn_ref(x, gate_W, gate_b, Wl, bl, Wr, edge_index):
        import jax, jax.numpy as jnp
        import numpy as np
        N_NODES = 4096
        N_EDGES = 32768
        D = 512
        NUM_EXPERTS = 4
        TOP_K = 2
        LAYERS = 2
        n = x.shape[0]
        src, dst = (edge_index[0], edge_index[1])
        gates = jax.nn.softmax(x @ gate_W + gate_b, axis=-1)
        top_v, top_i = jax.lax.top_k(gates, TOP_K)
        deg = jax.ops.segment_sum(jnp.ones((src.shape[0],), x.dtype), dst, num_segments=n)
        inv_deg = jnp.where(deg > 0, 1.0 / jnp.maximum(deg, 1.0), 0.0)[:, None]

        def sage_conv(h, W_l, b_l, W_r):
            aggr = jax.ops.segment_sum(h[src], dst, num_segments=n) * inv_deg
            return aggr @ W_l + b_l + h @ W_r
        expert_outs = []
        for e in range(NUM_EXPERTS):
            h = x
            for l in range(LAYERS):
                h = sage_conv(h, Wl[e, l], bl[e, l], Wr[e, l])
                h = jax.nn.relu(h)
            expert_outs.append(h)
        expert_outputs = jnp.stack(expert_outs, axis=1)
        sel = jnp.take_along_axis(expert_outputs, top_i[:, :, None], axis=1)
        out = jnp.sum(sel * top_v[:, :, None], axis=1)
        return out

    def _L3_ffn_ref(x, router_w, w_gate, w_up, w_down):
        import jax, jax.numpy as jnp
        import numpy as np
        B, S, D, H, E, K = (2, 256, 512, 1024, 8, 2)

        def _moe(x, router_w, w_gate, w_up, w_down):
            bsz, seq, d = x.shape
            flat = x.reshape(-1, d)
            logits = flat @ router_w.T
            topk_vals, topk_idx = jax.lax.top_k(logits, K)
            topk_w = jax.nn.softmax(topk_vals, axis=-1)
            s = flat.shape[0]
            dense_w = jnp.zeros((s, E), dtype=flat.dtype).at[jnp.arange(s)[:, None], topk_idx].add(topk_w)
            g = jnp.einsum('sd,edh->esh', flat, w_gate)
            u = jnp.einsum('sd,edh->esh', flat, w_up)
            y = jnp.einsum('esh,ehd->esd', jax.nn.silu(g) * u, w_down)
            out = jnp.einsum('esd,se->sd', y, dense_w)
            return out.reshape(bsz, seq, d)
        return _moe(x, router_w, w_gate, w_up, w_down)
    edge_index = jnp.stack([src, dst])
    x = x + _L0_gnn_ref(_layernorm(x, axis=-1), edge_index, L0_gnn_Wq, L0_gnn_bq, L0_gnn_Wk, L0_gnn_bk, L0_gnn_Wv, L0_gnn_bv, L0_gnn_Wo, L0_gnn_bo)
    x = x + _L0_ffn_ref(_layernorm(x, axis=-1)[None], L0_ffn_ln1_g, L0_ffn_ln1_b, L0_ffn_Wq, L0_ffn_bq, L0_ffn_Wk, L0_ffn_bk, L0_ffn_Wv, L0_ffn_bv, L0_ffn_Wo, L0_ffn_bo, L0_ffn_gate_W, L0_ffn_gate_b, L0_ffn_W1, L0_ffn_b1, L0_ffn_W2, L0_ffn_b2)[0]
    x = x + _L1_gnn_ref(_layernorm(x, axis=-1), edge_attr_2, L1_gnn_Wl, L1_gnn_bl, L1_gnn_Wr, L1_gnn_br, L1_gnn_We, L1_gnn_att, L1_gnn_b_out, L1_gnn_gamma, L1_gnn_beta, edge_index)
    x = x + _L1_ffn_ref(_layernorm(x, axis=-1)[None], L1_ffn_ln_g, L1_ffn_ln_b, L1_ffn_attn_w, L1_ffn_attn_b, L1_ffn_gate_w, L1_ffn_fc1_w, L1_ffn_fc1_b, L1_ffn_fc2_w, L1_ffn_fc2_b, L1_ffn_next_w, L1_ffn_next_b)[0]
    x = x + _L2_gnn_ref(_layernorm(x, axis=-1), L2_gnn_weight, L2_gnn_bias, edge_index, edge_weight)
    x = x + _L2_ffn_ref(_layernorm(x, axis=-1)[None], L2_ffn_gate_w, L2_ffn_w1, L2_ffn_b1, L2_ffn_w2, L2_ffn_b2, L2_ffn_sw1, L2_ffn_sb1, L2_ffn_sw2, L2_ffn_sb2)[0]
    x = x + _L3_gnn_ref(_layernorm(x, axis=-1), L3_gnn_gate_W, L3_gnn_gate_b, L3_gnn_Wl, L3_gnn_bl, L3_gnn_Wr, edge_index)
    x = x + _L3_ffn_ref(_layernorm(x, axis=-1)[None], L3_ffn_router_w, L3_ffn_w_gate, L3_ffn_w_up, L3_ffn_w_down)[0]
    return x

_drawn_inputs = setup_inputs


def setup_inputs(seed=0):
    import zlib

    import numpy as np

    out = dict(_drawn_inputs(seed))
    spreads = {'L0_ffn_ln1_g': (1.0, 0.573),
     'L0_ffn_ln1_b': (0.0, 0.429),
     'L0_ffn_bq': (0.0, 0.8),
     'L0_ffn_bk': (0.0, 2.0),
     'L0_ffn_bv': (0.0, 0.501),
     'L0_ffn_bo': (0.0, 0.404),
     'L0_ffn_gate_b': (0.0, 0.1),
     'L0_ffn_b1': (0.0, 0.406),
     'L0_ffn_b2': (0.0, 0.1),
     'L1_gnn_bl': (0.0, 0.1),
     'L1_gnn_br': (0.0, 0.8),
     'L1_gnn_b_out': (0.0, 0.1),
     'L1_gnn_gamma': (1.0, 0.2),
     'L1_gnn_beta': (0.0, 0.1),
     'L1_ffn_ln_g': (1.0, 0.6),
     'L1_ffn_ln_b': (0.0, 0.8),
     'L1_ffn_attn_b': (0.0, 0.8),
     'L1_ffn_fc1_b': (0.0, 0.629),
     'L1_ffn_fc2_b': (0.0, 0.363),
     'L1_ffn_next_b': (0.0, 0.1),
     'L2_ffn_b1': (0.0, 0.8),
     'L2_ffn_b2': (0.0, 0.8),
     'L2_ffn_sb1': (0.0, 0.8),
     'L2_ffn_sb2': (0.0, 0.403)}
    factors = {'edge_attr_2': 7.874,
     'L0_gnn_bq': 7.744,
     'L0_gnn_bk': 64.0,
     'L0_ffn_Wq': 8.0,
     'L0_ffn_Wk': 8.0,
     'L0_ffn_Wv': 5.538,
     'L0_ffn_Wo': 4.362,
     'L1_gnn_We': 6.433,
     'L1_ffn_attn_w': 2.735,
     'L2_gnn_bias': 6.086,
     'L2_ffn_gate_w': 8.0,
     'L2_ffn_w1': 8.0,
     'L2_ffn_w2': 8.0,
     'L3_gnn_gate_W': 2.896,
     'L3_gnn_gate_b': 50.167,
     'L3_gnn_bl': 22.22,
     'L2_ffn_sw1': 2.959}
    for name, (base, spread) in spreads.items():
        noise = np.random.default_rng([zlib.crc32(name.encode()), seed]).standard_normal(out[name].shape)
        drawn = base * np.exp(spread * noise) if base else spread * noise
        out[name] = jnp.asarray(drawn.astype(out[name].dtype))
    for name, factor in factors.items():
        out[name] = (out[name] * factor).astype(out[name].dtype)
    return out
```

```python
from contextlib import ExitStack

import concourse.bass as bass
import numpy as np
from concourse import mybir

F32 = mybir.dt.float32
F16 = mybir.dt.float16
BF16 = mybir.dt.bfloat16
I32 = mybir.dt.int32
U32 = mybir.dt.uint32
ALU = mybir.AluOpType
ACT = mybir.ActivationFunctionType
AX = mybir.AxisListType

P = 128
N = 512
D = 512
T = N // P
EDGES = 8704
ET = EDGES // P
EA = ET + T
HEADS = 8
HD = D // HEADS
EXPERTS = 8
NEG = -1e30
EPS = 1e-5
EX_SCALE = 16384.0


class Ticker:

    def __init__(self, sem):
        self.sem, self.base = sem, 0

    def at(self, n):
        return self.base + n


class Kernel:

    def __init__(self, nc, inputs):
        self.nc, self.i, self.uid = nc, inputs, 0


class Chain:

    def __init__(self, eng, ticker):
        self.eng, self.t, self.n, self.loop = eng, ticker, 0, 0

    def link(self, ins):
        self.n += 1
        ins.then_inc(self.t.sem, 1)
        self.eng.wait_ge(self.t.sem, self.t.at(self.n) + self.loop)

    def close(self, total=None):
        self.t.base += self.n if total is None else total


def later(step, first):
    return not isinstance(step, int) or step >= first


def rows_of(w):
    return w.rearrange("(k p) n -> p k n", p=P)


def bcast(v, n=P):
    return v.rearrange("(a d) -> a d", a=1).to_broadcast([n, v.shape[0]])


def sb(c, k, name, shape, dt=F32):
    k.uid += 1
    return c.enter_context(k.nc.sbuf_tensor(f"{name}_{k.uid}", shape, dt))


def done(*pairs):
    for ticker, n in pairs:
        ticker.base += n



def constants(k):
    with k.nc.Block() as block:
        @block.gpsimd
        def _(gp):
            ch = Chain(gp, k.pool_step)
            gp.memset(k.ident[:], 0.0)
            gp.memset(k.ones[:], 1.0)
            gp.memset(k.eps[:], EPS)
            ch.link(gp.memset(k.zrow[:], 0.0))
            gp.affine_select(out=k.ident[:], in_=k.ident[:], compare_op=ALU.not_equal, fill=1.0,
                             base=0, pattern=[[-1, P]], channel_multiplier=1)
            gp.affine_select(out=k.before[:], in_=k.ones[:], compare_op=ALU.is_gt, fill=0.0,
                             base=0, pattern=[[1, P]], channel_multiplier=-1)
            gp.iota(k.ramp_i[:], pattern=[[1, N]], base=0, channel_multiplier=0)
            ch.link(gp.iota(k.node_i[:], pattern=[[P, T]], base=0, channel_multiplier=1))
            ch.close()

        @block.sync
        def _(sp):
            for dst, src in ((k.X[:], rows_of(k.i["x"])),
                             (k.src_i[:, 0:ET], k.i["src"].rearrange("(p j) -> p j", p=P)),
                             (k.dst_i[:, 0:ET], k.i["dst"].rearrange("(p j) -> p j", p=P)),
                             (k.ea[:, 0:ET, :], k.i["edge_attr_2"].rearrange("(p j) c -> p j c", p=P))):
                sp.dma_start(dst, src).then_inc(k.loaded.sem, 16)
            sp.wait_ge(k.loaded.sem, k.loaded.at(64))
    done((k.loaded, 64))
    with k.nc.Block() as block:
        @block.vector
        def _(v):
            ch = Chain(v, k.dve_step)
            v.tensor_copy(k.ramp_f[:], k.ramp_i[:])
            v.tensor_copy(k.ramp[:], k.ramp_i[:])
            v.tensor_copy(k.node_f[:], k.node_i[:])
            v.tensor_copy(k.identb[:], k.ident[:])
            v.tensor_copy(k.src_i[:, ET:EA], k.node_i[:])
            ch.link(v.tensor_copy(k.dst_i[:, ET:EA], k.node_i[:]))
            v.tensor_copy(k.src_f[:], k.src_i[:])
            ch.link(v.tensor_copy(k.dst_f[:], k.dst_i[:]))
            ch.close()


def split3(v, ch, parts, value, rest):
    ch.link(v.tensor_copy(parts[0], value))
    ch.link(v.tensor_tensor(rest, value, parts[0], ALU.subtract))
    ch.link(v.tensor_copy(parts[1], rest))
    ch.link(v.tensor_tensor(rest, rest, parts[1], ALU.subtract))
    ch.link(v.tensor_copy(parts[2], rest))


def adjacency(k):
    nc = k.nc
    with ExitStack() as c:
        parts = sb(c, k, "parts", [P, ET, 7], BF16)
        rest = sb(c, k, "rest", [P, ET, 2])
        oh_s = [sb(c, k, "oh_s", [P, N], BF16) for _ in range(2)]
        oh_d = [sb(c, k, "oh_d", [P, N], BF16) for _ in range(2)]
        sums = sb(c, k, "sums", [P, T, 7])
        inv = sb(c, k, "inv", [P, T])
        diag = sb(c, k, "diag", [P, T, P])
        with nc.Block() as block:
            @block.vector
            def _(v):
                ch = Chain(v, k.dve_step)
                v.memset(parts[:, :, 6:7], 1.0)
                split3(v, ch, [parts[:, :, 2 * j:2 * j + 2] for j in range(3)], k.ea[:, 0:ET, :], rest[:])
                ch.close()

                def step(i, u):
                    if later(i, 2):
                        v.wait_ge(k.mm.sem, k.mm.at(i - 1))
                    v.tensor_scalar(oh_s[u][:], k.ramp[:], k.src_f[:, bass.ds(i, 1)], None, ALU.is_equal)
                    v.tensor_scalar(oh_d[u][:], k.ramp[:], k.dst_f[:, bass.ds(i, 1)], None,
                                    ALU.is_equal).then_inc(k.ready.sem, 1)
                for u in range(2):
                    step(u, u)
                with v.Fori(1, ET // 2) as j:
                    for u in range(2):
                        step(j * 2 + u, u)

            @block.tensor
            def _(pe):
                def step(i, u, first=False, last=False):
                    pe.wait_ge(k.ready.sem, k.ready.at(i + 1))
                    for t in range(T):
                        pe.matmul(k.ps[:, t, :], oh_s[u][:, t * P:(t + 1) * P], oh_d[u][:],
                                  start=first, stop=last)
                    for t in range(T):
                        m = pe.matmul(k.ps[:, T + t, 0:7], oh_d[u][:, t * P:(t + 1) * P],
                                      parts[:, bass.ds(i, 1), :].rearrange("p a c -> p (a c)"),
                                      start=first, stop=last)
                    m.then_inc(k.mm.sem, 1)
                step(0, 0, first=True)
                step(1, 1)
                with pe.Fori(1, ET // 2 - 1) as j:
                    for u in range(2):
                        step(j * 2 + u, u)
                step(ET - 2, 0)
                step(ET - 1, 1, last=True)
        done((k.mm, ET), (k.ready, ET))
        with nc.Block() as block:
            @block.scalar
            def _(a):
                for t in range(T):
                    a.activation(k.C[:, t, :], k.ps[:, t, :], ACT.Copy).then_inc(k.copied.sem, 1)

            @block.vector
            def _(v):
                ch = Chain(v, k.dve_step)
                for t in range(T):
                    last = v.tensor_copy(sums[:, t, :], k.ps[:, T + t, 0:7])
                ch.link(last)
                v.tensor_scalar(k.inv_deg[:], sums[:, :, 6], 1.0, None, ALU.min)
                ch.link(v.tensor_scalar(inv[:], sums[:, :, 6], 1.0, None, ALU.max))
                ch.link(v.reciprocal(inv[:], inv[:]))
                ch.link(v.tensor_tensor(k.inv_deg[:], k.inv_deg[:], inv[:], ALU.mult))
                mean = k.ea[:, ET:EA, :]
                ch.link(v.tensor_tensor(mean, sums[:, :, 0:2], sums[:, :, 2:4], ALU.add))
                ch.link(v.tensor_tensor(mean, mean, sums[:, :, 4:6], ALU.add))
                for t in range(T):
                    v.tensor_scalar(k.ea[:, ET + t, :], k.ea[:, ET + t, :], inv[:, t:t + 1], None, ALU.mult)
                for t in range(T):
                    last = v.tensor_scalar(diag[:, t, :], k.ident[:], k.inv_deg[:, t:t + 1], None, ALU.mult)
                last.then_inc(k.ready.sem, 1)
                v.wait_ge(k.mm.sem, k.mm.at(1))
                v.wait_ge(k.copied.sem, k.copied.at(T))
                for t in range(T):
                    v.tensor_tensor(k.Cn[:, t, :], k.C[:, t, :], k.ps[:, T, :], ALU.mult)
                    v.tensor_scalar(k.no_edge[:, t, :], k.C[:, t, :], 0.0, NEG, ALU.is_equal, ALU.mult)
                ch.link(v.tensor_reduce(k.has_out[:], k.C[:], AX.X, ALU.max))
                ch.link(v.tensor_scalar(k.has_out[:], k.has_out[:], 0.0, None, ALU.is_gt))
                ch.close()

            @block.tensor
            def _(pe):
                pe.wait_ge(k.ready.sem, k.ready.at(1))
                for t in range(T):
                    m = pe.matmul(k.ps[:, T, t * P:(t + 1) * P], k.ones[:], diag[:, t, :], start=True, stop=True)
                m.then_inc(k.mm.sem, 1)
        done((k.mm, 1), (k.ready, 1), (k.copied, T))



def layernorm(k, src, rows, cols, passes=(None,), relu=False):
    nc, np_ = k.nc, len(passes)
    with ExitStack() as c:
        stats = sb(c, k, "stats", [P, T, 6])
        mv = sb(c, k, "mv", [P, T, 2])
        rstd = sb(c, k, "rstd", [P, T])
        rows_step = []
        with nc.Block() as block:
            @block.vector
            def _(v):
                ch = Chain(v, k.dve_step)
                for j, gb in enumerate(passes):
                    x = src if j == 0 else rows
                    for t in range(T):
                        last = v.bn_stats(stats[:, t, :], x[:, t, :])
                    ch.link(last)
                    for t in range(T):
                        last = v.bn_aggr(mv[:, t, :], stats[:, t, :])
                    last.then_inc(k.ready.sem, 1)
                    v.wait_ge(k.copied.sem, k.copied.at(j + 1))
                    ch.link(v.reciprocal(rstd[:], rstd[:]))
                    for t in range(T):
                        last = v.tensor_scalar(rows[:, t, :], x[:, t, :], mv[:, t, 0:1], rstd[:, t:t + 1],
                                               ALU.subtract, ALU.mult)
                    ch.link(last)
                    if gb:
                        for op, w in ((ALU.mult, gb[0]), (ALU.add, gb[1])):
                            for t in range(T):
                                last = v.tensor_tensor(rows[:, t, :], rows[:, t, :], w[:], op)
                            ch.link(last)
                if relu:
                    ch.link(v.tensor_scalar(rows[:], rows[:], 0.0, None, ALU.max))
                rows_step.append(k.dve_step.at(ch.n))
                for f in (1, 3):
                    v.wait_ge(k.mm.sem, k.mm.at(f + 1))
                    v.tensor_copy(cols[:, f, :], k.ps[:, f, :])
                ch.close()

            @block.scalar
            def _(a):
                for j in range(np_):
                    a.wait_ge(k.ready.sem, k.ready.at(j + 1))
                    a.activation(rstd[:], mv[:, :, 1], ACT.Sqrt, bias=k.eps[:, 0:1]).then_inc(k.copied.sem, 1)
                for f in (0, 2):
                    a.wait_ge(k.mm.sem, k.mm.at(f + 1))
                    a.activation(cols[:, f, :], k.ps[:, f, :], ACT.Copy)

            @block.tensor
            def _(pe):
                pe.wait_ge(k.dve_step.sem, rows_step[0])
                for f in range(T):
                    for t in range(T):
                        m = pe.transpose(k.ps[:, f, t * P:(t + 1) * P], rows[:, t, f * P:(f + 1) * P], k.ident[:])
                    m.then_inc(k.mm.sem, 1)
        done((k.ready, np_), (k.copied, np_), (k.mm, T))


def mm_rows(pe, k, bank, cols, w, start=True, stop=True):
    for t in range(T):
        for f in range(T):
            m = pe.matmul(k.ps[:, bank + t, :], cols[:, f, t * P:(t + 1) * P], w[:, f, :],
                          start=start and f == 0, stop=stop and f == T - 1)
    return m


def mm_cols(pe, k, bank, w, cols, start=True, stop=True):
    for t in range(T):
        for f in range(T):
            m = pe.matmul(k.ps[:, bank + t, :], w[:, f, t * P:(t + 1) * P], cols[:, f, :],
                          start=start and f == 0, stop=stop and f == T - 1)
    return m



def attention(k, w, mask, base, out):
    nc = k.nc
    with ExitStack() as c:
        W = [sb(c, k, f"w{j}", [P, T, D]) for j in range(4)]
        QT, KT, V, OT = [sb(c, k, n, [P, T, D]) for n in ("qt", "kt", "v", "ot")]
        bq, bk = sb(c, k, "bq", [P, T]), sb(c, k, "bk", [P, T])
        bv, bo = sb(c, k, "bv", [P, D]), sb(c, k, "bo", [P, D])
        E = [sb(c, k, "e", [P, T, N]) for _ in range(2)]
        PT = sb(c, k, "pt", [P, T, N])
        mx, den = sb(c, k, "mx", [P, 2, T]), sb(c, k, "den", [P, 2, T])
        with nc.Block() as block:
            @block.sync
            def _(sp):
                for dst, src in ((bq[:], w["bq"]), (bk[:], w["bk"]), (bv[:], bcast(w["bv"])), (bo[:], bcast(w["bo"]))):
                    sp.dma_start(dst, src).then_inc(k.loaded.sem, 16)
                for j, m in enumerate((w["Wq"], w["Wk"], w["Wv"], w["Wo"])):
                    sp.dma_start(W[j][:], rows_of(m)).then_inc(k.slot[j].sem, 16)

            @block.tensor
            def _(pe):
                pe.wait_ge(k.slot[0].sem, k.slot[0].at(16))
                mm_cols(pe, k, 0, W[0], k.NT).then_inc(k.mm.sem, 1)
                pe.wait_ge(k.slot[1].sem, k.slot[1].at(16))
                mm_cols(pe, k, 4, W[1], k.NT).then_inc(k.mm.sem, 1)
                pe.wait_ge(k.slot[2].sem, k.slot[2].at(16))
                pe.wait_ge(k.copied.sem, k.copied.at(1))
                mm_rows(pe, k, 0, k.NT, W[2]).then_inc(k.mm.sem, 1)

            @block.vector
            def _(v):
                v.wait_ge(k.loaded.sem, k.loaded.at(64))
                v.wait_ge(k.mm.sem, k.mm.at(1))
                for t in range(T):
                    m = v.tensor_scalar(QT[:, t, :], k.ps[:, t, :], bq[:, t:t + 1], HD ** -0.5, ALU.add, ALU.mult)
                m.then_inc(k.copied.sem, 1)
                for t in range(T):
                    v.tensor_tensor(out[:, t, :], base[:, t, :], bo[:], ALU.add)
                v.wait_ge(k.mm.sem, k.mm.at(3))
                for t in range(T):
                    v.tensor_tensor(V[:, t, :], k.ps[:, t, :], bv[:], ALU.add)

            @block.scalar
            def _(a):
                a.wait_ge(k.loaded.sem, k.loaded.at(64))
                a.wait_ge(k.mm.sem, k.mm.at(2))
                for t in range(T):
                    a.activation(KT[:, t, :], k.ps[:, T + t, :], ACT.Identity, bias=bk[:, t:t + 1])
        done((k.loaded, 64), (k.mm, 3), (k.copied, 1), (k.slot[0], 16), (k.slot[1], 16), (k.slot[2], 16))

        with nc.Block() as block:
            @block.tensor
            def _(pe):
                def scores(h):
                    lo, f = (h % 2) * HD, h // 2
                    for t in range(T):
                        if h:
                            pe.wait_ge(k.ready.sem, k.ready.at(T * (h - 1) + t + 1))
                        pe.matmul(k.ps[:, t, :], QT[lo:lo + HD, f, t * P:(t + 1) * P], KT[lo:lo + HD, f, :],
                                  start=True, stop=True).then_inc(k.mm.sem, 1)

                def weigh(h):
                    lo, f = (h % 2) * HD, h // 2
                    pe.wait_ge(k.probs.sem, k.probs.at(h + 1))
                    for m in range(T):
                        if h or m >= 2:
                            n = T * h + m - 2
                            q = k.turned[m % 2]
                            pe.wait_ge(q.sem, q.at(n // 2 + 1))
                        for t in range(T):
                            i = pe.transpose(k.ps[:, 4 + m % 2, t * P:(t + 1) * P],
                                             E[h % 2][:, t, m * P:(m + 1) * P], k.ident[:])
                        i.then_inc(k.tp.sem, 1)
                    if h % 2 == 0 and h >= 4:
                        pe.wait_ge(k.heads.sem, k.heads.at(h // 2 - 1))
                    for m in range(T):
                        q = k.turned[m % 2]
                        pe.wait_ge(q.sem, q.at(2 * h + m // 2 + 1))
                        i = pe.matmul(k.ps[lo:lo + HD, 6 + f % 2, :], V[:, m, h * HD:(h + 1) * HD], PT[:, m, :],
                                      start=(m == 0), stop=(m == T - 1))
                    i.then_inc(k.av.sem, 1)
                scores(0)
                for h in range(HEADS):
                    if h + 1 < HEADS:
                        scores(h + 1)
                    weigh(h)
                pe.wait_ge(k.slot[3].sem, k.slot[3].at(16))
                pe.wait_ge(k.heads.sem, k.heads.at(HEADS // 2))
                mm_rows(pe, k, 0, OT, W[3]).then_inc(k.mm.sem, 1)

            @block.vector
            def _(v):
                ch = Chain(v, k.dve_step)

                def maxima(h):
                    s = h % 2
                    if h >= 2:
                        v.wait_ge(k.tp.sem, k.tp.at(T * (h - 1)))
                    for t in range(T):
                        v.wait_ge(k.mm.sem, k.mm.at(T * h + t + 1))
                        last = v.tensor_tensor_reduce(E[s][:, t, :], k.ps[:, t, :],
                                                      mask[:, t, :] if mask is not None else k.zrow[:],
                                                      1.0, -3e38, ALU.add, ALU.max, mx[:, s, t:t + 1])
                        last.then_inc(k.ready.sem, 1)
                    v.wait_ge(k.ready.sem, k.ready.at(T * (h + 1)))
                    v.tensor_scalar(mx[:, s, :], mx[:, s, :], -1.0, None, ALU.mult).then_inc(k.maxed.sem, 1)

                def norm(h):
                    s = h % 2
                    v.wait_ge(k.exped.sem, k.exped.at(h + 1))
                    ch.link(v.reciprocal(den[:, s, :], den[:, s, :]))
                    if mask is not None:
                        ch.link(v.tensor_tensor(den[:, s, :], den[:, s, :], k.has_out[:], ALU.mult))
                    for t in range(T):
                        last = v.tensor_scalar(E[s][:, t, :], E[s][:, t, :], den[:, s, t:t + 1], None, ALU.mult)
                    last.then_inc(k.probs.sem, 1)
                    for m in (1, 3):
                        v.wait_ge(k.tp.sem, k.tp.at(T * h + m + 1))
                        if h:
                            v.wait_ge(k.av.sem, k.av.at(h))
                        v.tensor_copy(PT[:, m, :], k.ps[:, 5, :]).then_inc(k.turned[1].sem, 1)
                maxima(0)
                for h in range(HEADS):
                    if h + 1 < HEADS:
                        maxima(h + 1)
                    norm(h)
                v.wait_ge(k.mm.sem, k.mm.at(T * HEADS + 1))
                for t in range(T):
                    v.tensor_tensor(out[:, t, :], out[:, t, :], k.ps[:, t, :], ALU.add)
                ch.close()

            @block.scalar
            def _(a):
                for h in range(HEADS):
                    s = h % 2
                    a.wait_ge(k.maxed.sem, k.maxed.at(h + 1))
                    for t in range(T):
                        i = a.activation(E[s][:, t, :], E[s][:, t, :], ACT.Exp, bias=mx[:, s, t:t + 1],
                                         accum_out=den[:, s, t:t + 1])
                    i.then_inc(k.exped.sem, 1)
                    for m in (0, 2):
                        a.wait_ge(k.tp.sem, k.tp.at(T * h + m + 1))
                        if h:
                            a.wait_ge(k.av.sem, k.av.at(h))
                        a.activation(PT[:, m, :], k.ps[:, 4, :], ACT.Copy).then_inc(k.turned[0].sem, 1)
                    if h % 2:
                        a.wait_ge(k.av.sem, k.av.at(h + 1))
                        a.activation(OT[:, h // 2, :], k.ps[:, 6 + (h // 2) % 2, :],
                                     ACT.Copy).then_inc(k.heads.sem, 1)
        done((k.mm, T * HEADS + 1), (k.ready, T * HEADS), (k.maxed, HEADS), (k.exped, HEADS), (k.probs, HEADS),
             (k.tp, T * HEADS), (k.turned[0], 2 * HEADS), (k.turned[1], 2 * HEADS), (k.av, HEADS),
             (k.heads, HEADS // 2), (k.slot[3], 16))



def routing(k, c, cols, gate, bias, width, how, choices):
    nc = k.nc
    g = sb(c, k, "gate", [P, T, width])
    gb = sb(c, k, "gate_b", [P, width])
    lg = sb(c, k, "lg", [P, T, 8])
    mx = sb(c, k, "lmx", [P, T])
    sm = sb(c, k, "lsm", [P, T])
    top = sb(c, k, "top", [P, T, 8])
    at = sb(c, k, "at", [P, T, 8], U32)
    atf = sb(c, k, "atf", [P, T, 8])
    masks = sb(c, k, "masks", [P, T, choices, 8])
    wt = sb(c, k, "wt", [P, T, choices])
    with nc.Block() as block:
        @block.sync
        def _(sp):
            sp.dma_start(g[:], rows_of(gate)).then_inc(k.loaded.sem, 16)
            if bias is not None:
                sp.dma_start(gb[:], bcast(bias)).then_inc(k.loaded.sem, 16)

        @block.tensor
        def _(pe):
            pe.wait_ge(k.loaded.sem, k.loaded.at(32 if bias is not None else 16))
            for t in range(T):
                for f in range(T):
                    m = pe.matmul(k.ps[:, t, 0:width], cols[:, f, t * P:(t + 1) * P], g[:, f, :],
                                  start=(f == 0), stop=(f == T - 1))
            m.then_inc(k.mm.sem, 1)

        @block.vector
        def _(v):
            ch = Chain(v, k.dve_step)
            if width < 8:
                ch.link(v.memset(lg[:], NEG))
            v.wait_ge(k.mm.sem, k.mm.at(1))
            for t in range(T):
                if bias is not None:
                    last = v.tensor_tensor(lg[:, t, 0:width], k.ps[:, t, 0:width], gb[:], ALU.add)
                else:
                    last = v.tensor_copy(lg[:, t, 0:width], k.ps[:, t, 0:width])
            ch.link(last)
            if how != "top2":
                ch.link(v.tensor_reduce(mx[:], lg[:], AX.X, ALU.max))
                ch.link(v.tensor_scalar(mx[:], mx[:], -1.0, None, ALU.mult))
                for t in range(T):
                    last = v.tensor_scalar(lg[:, t, :], lg[:, t, :], mx[:, t:t + 1], None, ALU.add)
                last.then_inc(k.ready.sem, 1)
                v.wait_ge(k.copied.sem, k.copied.at(1))
                ch.link(v.tensor_reduce(sm[:], lg[:], AX.X, ALU.add))
                ch.link(v.reciprocal(sm[:], sm[:]))
                for t in range(T):
                    last = v.tensor_scalar(lg[:, t, :], lg[:, t, :], sm[:, t:t + 1], None, ALU.mult)
                ch.link(last)
            for t in range(T):
                last = v.max(top[:, t, :], lg[:, t, :])
            ch.link(last)
            for t in range(T):
                last = v.max_index(at[:, t, :], top[:, t, :], lg[:, t, :])
            ch.link(last)
            ch.link(v.tensor_copy(atf[:], at[:]))
            for t in range(T):
                for q in range(choices):
                    last = v.tensor_scalar(masks[:, t, q, :], k.ramp_f[:, 0:8], atf[:, t, q:q + 1], None,
                                           ALU.is_equal)
            ch.link(last)
            if how != "top2":
                ch.link(v.tensor_copy(wt[:], top[:, :, 0:choices]))
            else:
                v.tensor_tensor(sm[:], top[:, :, 1], top[:, :, 0], ALU.subtract).then_inc(k.ready.sem, 1)
                v.wait_ge(k.copied.sem, k.copied.at(1))
                ch.link(v.tensor_scalar(sm[:], mx[:], 1.0, None, ALU.add))
                ch.link(v.reciprocal(wt[:, :, 0], sm[:]))
                ch.link(v.tensor_tensor(wt[:, :, 1], wt[:, :, 0], mx[:], ALU.mult))
            ch.close()

        @block.scalar
        def _(a):
            a.wait_ge(k.ready.sem, k.ready.at(1))
            if how != "top2":
                a.activation(lg[:], lg[:], ACT.Exp).then_inc(k.copied.sem, 1)
            else:
                a.activation(mx[:], sm[:], ACT.Exp).then_inc(k.copied.sem, 1)
    done((k.loaded, 32 if bias is not None else 16), (k.mm, 1), (k.ready, 1), (k.copied, 1))
    return masks, wt


def dispatch(k, c, masks, choices, granules, rows, spread):
    nc = k.nc
    m = sb(c, k, "m", [P, T, EXPERTS])
    pos = sb(c, k, "pos", [P, T, EXPERTS])
    n_e = sb(c, k, "n_e", [P, EXPERTS])
    g_e = sb(c, k, "g_e", [P, EXPERTS])
    end = sb(c, k, "end", [P, EXPERTS])
    own = sb(c, k, "own", [P, granules])
    own_i = sb(c, k, "own_i", [P, granules], I32)
    pick = sb(c, k, "pick", [P, T, EXPERTS])
    slot_f = sb(c, k, "slot_f", [P, T, choices])
    slot = sb(c, k, "slot", [P, T, choices], I32)
    zero = sb(c, k, "zero", [P, D])
    with nc.Block() as block:
        @block.sync
        def _(sp):
            sp.wait_ge(k.ready.sem, k.ready.at(1))
            for g in range(granules):
                sp.dma_start(spread[g * P:(g + 1) * P, :], zero[:]).then_inc(k.loaded.sem, 16)

        @block.vector
        def _(v):
            ch = Chain(v, k.dve_step)
            v.memset(zero[:], 0.0).then_inc(k.ready.sem, 1)
            if choices == 1:
                v.tensor_copy(m[:], masks[:, :, 0, :]).then_inc(k.ready.sem, 1)
            else:
                v.tensor_tensor(m[:], masks[:, :, 0, :], masks[:, :, 1, :], ALU.add).then_inc(k.ready.sem, 1)
            v.wait_ge(k.mm.sem, k.mm.at(1))
            for t in range(T):
                v.tensor_copy(pos[:, t, :], k.ps[:, t, 0:EXPERTS])
            ch.link(v.tensor_copy(n_e[:], k.ps[:, T, 0:EXPERTS]))
            ch.link(v.tensor_scalar(g_e[:], n_e[:], 0.0, None, ALU.is_gt))
            for j in range(1, T):
                ch.link(v.scalar_tensor_tensor(g_e[:], n_e[:], float(P * j), g_e[:], ALU.is_gt, ALU.add))
            ch.link(v.tensor_tensor_scan(end[:], k.ones[:, 0:EXPERTS], g_e[:], 0.0, ALU.mult, ALU.add))
            ch.link(v.tensor_tensor(g_e[:], end[:], g_e[:], ALU.subtract))
            for t in range(T):
                last = v.scalar_tensor_tensor(pos[:, t, :], g_e[:], float(P), pos[:, t, :], ALU.mult, ALU.add)
            ch.link(last)
            for q in range(choices):
                ch.link(v.tensor_tensor(pick[:], masks[:, :, q, :], pos[:], ALU.mult))
                ch.link(v.tensor_reduce(slot_f[:, :, q], pick[:], AX.X, ALU.add))
            v.tensor_copy(slot[:], slot_f[:]).then_inc(k.copied.sem, 1)
            ch.link(v.memset(own[:], 0.0))
            for e in range(EXPERTS):
                ch.link(v.scalar_tensor_tensor(own[:], k.ramp_f[:, 0:granules], end[:, e:e + 1], own[:],
                                               ALU.is_ge, ALU.add))
            ch.link(v.tensor_scalar(own[:], own[:], float(EXPERTS - 1), None, ALU.min))
            ch.link(v.tensor_copy(own_i[:], own[:]))
            ch.close()

        @block.tensor
        def _(pe):
            pe.wait_ge(k.ready.sem, k.ready.at(2))
            for t in range(T):
                for s in range(t + 1):
                    pe.matmul(k.ps[:, t, 0:EXPERTS], k.before[:] if s == t else k.ones[:], m[:, s, :],
                              start=(s == 0), stop=(s == t))
            for s in range(T):
                i = pe.matmul(k.ps[:, T, 0:EXPERTS], k.ones[:], m[:, s, :], start=(s == 0), stop=(s == T - 1))
            i.then_inc(k.mm.sem, 1)

        @block.gpsimd
        def _(gp):
            gp.wait_ge(k.loaded.sem, k.loaded.at(16 * granules))
            gp.wait_ge(k.copied.sem, k.copied.at(1))
            for q in range(choices):
                for t in range(T):
                    gp.indirect_dma_start(spread, bass.IndirectOffsetOnAxis(ap=slot[:, t, q:q + 1].bitcast(U32), axis=0),
                                          rows[:, t, :], None).then_inc(k.gathered.sem, 16)
            gp.wait_ge(k.gathered.sem, k.gathered.at(16 * T * choices))
    done((k.ready, 2), (k.mm, 1), (k.copied, 1), (k.loaded, 16 * granules), (k.gathered, 16 * T * choices))
    return slot, own_i


def experts(k, c, granules, own, spread, result, w, hidden, gated):
    nc = k.nc
    HT = hidden // P
    ins = 2 if gated else 1
    W1 = [[sb(c, k, "w1", [P, T, hidden]) for _ in range(ins)] for _ in range(2)]
    W2 = [sb(c, k, "w2", [P, HT, D]) for _ in range(2)]
    b1 = [sb(c, k, "b1", [P, HT]) for _ in range(2)]
    b2 = [sb(c, k, "b2", [P, D]) for _ in range(2)]
    tok = [sb(c, k, "tok", [P, D]) for _ in range(2)]
    tokT = sb(c, k, "tokT", [P, T, P])
    hT = sb(c, k, "hT", [P, HT, P])
    act = sb(c, k, "act", [P, T * P]) if gated else None
    y = [sb(c, k, "y", [P, D]) for _ in range(2)]
    QT_ = HT // T
    loads = 16 * (2 + ins if gated else 4 + ins)

    def walk(eng, step):
        step(0, 0, 0)
        step(1, 1, 0)
        with eng.Fori(1, granules // 2) as j:
            for u in range(2):
                step(j * 2 + u, u, j)
        if granules % 2:
            step(granules - 1, 0, granules // 2)

    with nc.Block() as block:
        @block.sync
        def _(sp):
            def step(g, u, j):
                if later(g, 2):
                    sp.wait_ge(k.heads.sem, k.heads.at(-1) + g)
                e = sp.value_load(own[0:1, bass.ds(g, 1)], min_val=0, max_val=EXPERTS - 1)
                src = ((w["Wg"], w["Wu"]) if gated else (w["W1"],))
                sp.dma_start(tok[u][:], spread[bass.ds(g * P, P), :]).then_inc(k.slot[u].sem, 16)
                for q in range(ins):
                    sp.dma_start(W1[u][q][:], src[q][bass.ds(e, 1)].rearrange("a (k p) n -> p (a k) n", p=P)
                                 ).then_inc(k.slot[u].sem, 16)
                sp.dma_start(W2[u][:], (w["Wd"] if gated else w["W2"])[bass.ds(e, 1)].rearrange(
                    "a (k p) n -> p (a k) n", p=P)).then_inc(k.slot[u].sem, 16)
                if not gated:
                    sp.dma_start(b1[u][:], w["b1"][bass.ds(e, 1)].rearrange("a p m -> p (a m)")
                                 ).then_inc(k.slot[u].sem, 16)
                    sp.dma_start(b2[u][:], w["b2"][bass.ds(e, 1), :].to_broadcast([P, D])
                                 ).then_inc(k.slot[u].sem, 16)
            walk(sp, step)

        @block.tensor
        def _(pe):
            def step(g, u, j):
                pe.wait_ge(k.slot[u].sem, k.slot[u].at(loads) + j * loads)
                for f in range(T):
                    m = pe.transpose(k.ps[:, 0, f * P:(f + 1) * P], tok[u][:, f * P:(f + 1) * P], k.ident[:])
                m.then_inc(k.tp.sem, 1)
                pe.wait_ge(k.turned[0].sem, k.turned[0].at(1) + g)
                for q in range(QT_):
                    for i in range(ins):
                        b = 1 + (q * ins + i) % 4
                        lag = q * ins + i - 4
                        if lag >= 0:
                            pe.wait_ge(k.copied.sem, k.copied.at(lag // ins + 1) + g * QT_)
                        for s in range(T):
                            for f in range(T):
                                m = pe.matmul(k.ps[:, b, s * P:(s + 1) * P],
                                              W1[u][i][:, f, (q * T + s) * P:(q * T + s + 1) * P],
                                              tokT[:, f, :], start=(f == 0), stop=(f == T - 1))
                    m.then_inc(k.mm.sem, 1)
                pe.wait_ge(k.copied.sem, k.copied.at(QT_) + g * QT_)
                if later(g, 2):
                    pe.wait_ge(k.heads.sem, k.heads.at(-1) + g)
                for s in range(HT):
                    m = pe.matmul(k.ps[:, 5 + u, :], hT[:, s, :], W2[u][:, s, :], start=(s == 0), stop=(s == HT - 1))
                m.then_inc(k.out.sem, 1)
            walk(pe, step)

        @block.scalar
        def _(a):
            def step(g, u, j):
                if later(g, 1):
                    a.wait_ge(k.out.sem, k.out.at(0) + g)
                for q in range(QT_):
                    a.wait_ge(k.mm.sem, k.mm.at(q + 1) + g * QT_)
                    if gated:
                        if q or later(g, 1):
                            a.wait_ge(k.copied.sem, k.copied.at(q) + g * QT_)
                        a.activation(act[:], k.ps[:, 1 + (q * 2) % 4, :], ACT.Silu).then_inc(k.exped.sem, 1)
                    else:
                        for s in range(T):
                            i = a.activation(hT[:, q * T + s, :], k.ps[:, 1 + q % 4, s * P:(s + 1) * P],
                                             ACT.Gelu_apprx_tanh, bias=b1[u][:, q * T + s:q * T + s + 1])
                        i.then_inc(k.copied.sem, 1)
            walk(a, step)

        @block.vector
        def _(v):
            def step(g, u, j):
                v.wait_ge(k.tp.sem, k.tp.at(1) + g)
                if later(g, 1):
                    v.wait_ge(k.mm.sem, k.mm.at(0) + g * QT_)
                v.tensor_copy(tokT[:].rearrange("p k n -> p (k n)"), k.ps[:, 0, :]).then_inc(k.turned[0].sem, 1)
                if gated:
                    if later(g, 1):
                        v.wait_ge(k.out.sem, k.out.at(0) + g)
                    for q in range(QT_):
                        v.wait_ge(k.exped.sem, k.exped.at(q + 1) + g * QT_)
                        v.tensor_tensor(hT[:, q * T:(q + 1) * T, :].rearrange("p k n -> p (k n)"), act[:],
                                        k.ps[:, 1 + (q * 2 + 1) % 4, :], ALU.mult).then_inc(k.copied.sem, 1)
                v.wait_ge(k.out.sem, k.out.at(1) + g)
                if later(g, 2):
                    v.wait_ge(k.pool_stored[u].sem, k.pool_stored[u].at(0) + j * 16)
                if gated:
                    v.tensor_copy(y[u][:], k.ps[:, 5 + u, :]).then_inc(k.heads.sem, 1)
                else:
                    v.tensor_tensor(y[u][:], k.ps[:, 5 + u, :], b2[u][:], ALU.add).then_inc(k.heads.sem, 1)
            walk(v, step)

        @block.gpsimd
        def _(gp):
            def step(g, u, j):
                gp.wait_ge(k.heads.sem, k.heads.at(1) + g)
                gp.dma_start(result[bass.ds(g * P, P), :], y[u][:]).then_inc(k.pool_stored[u].sem, 16)
            for g in range(granules):
                step(g, g % 2, g // 2)
            for u in range(2):
                gp.wait_ge(k.pool_stored[u].sem, k.pool_stored[u].at(16 * ((granules + 1 - u) // 2)))
    n0, n1 = (granules + 1) // 2, granules // 2
    done((k.slot[0], loads * n0), (k.slot[1], loads * n1), (k.tp, granules), (k.turned[0], granules),
         (k.mm, QT_ * granules), (k.copied, QT_ * granules), (k.out, granules), (k.heads, granules),
         (k.pool_stored[0], 16 * n0), (k.pool_stored[1], 16 * n1), (k.exped, QT_ * granules if gated else 0))


def combine(k, c, slot, wt, choices, result):
    with k.nc.Block() as block:
        back = [sb(c, k, "back", [P, T, D]) for _ in range(choices)]

        @block.gpsimd
        def _(gp):
            for q in range(choices):
                for t in range(T):
                    gp.indirect_dma_start(back[q][:, t, :], None, result,
                                          bass.IndirectOffsetOnAxis(ap=slot[:, t, q:q + 1].bitcast(U32), axis=0)
                                          ).then_inc(k.gathered.sem, 16)

        @block.vector
        def _(v):
            ch = Chain(v, k.dve_step)
            v.wait_ge(k.gathered.sem, k.gathered.at(16 * T * choices))
            for q in range(choices):
                for t in range(T):
                    last = v.scalar_tensor_tensor(k.X[:, t, :], back[q][:, t, :], wt[:, t, q:q + 1], k.X[:, t, :],
                                                  ALU.mult, ALU.add)
                ch.link(last)
            ch.close()
    done((k.gathered, 16 * T * choices))


def routed_ffn(k, cols, rows, gate, bias, how, choices, granules, w, hidden, gated, spread, result):
    spread, result = spread[0:granules * P, :], result[0:granules * P, :]
    with ExitStack() as c:
        masks, wt = routing(k, c, cols, gate, bias, EXPERTS, how, choices)
        slot, own = dispatch(k, c, masks, choices, granules, rows, spread)
        with ExitStack() as c2:
            experts(k, c2, granules, own, spread, result, w, hidden, gated)
        combine(k, c, slot, wt, choices, result)



def gat_setup(k, c):
    nc = k.nc
    a_part, w_part = (0, 0, 1, 0, 2, 1), (0, 1, 0, 2, 0, 1)
    k.oht = sb(c, k, "oht", [P, T, EA * P], BF16)
    k.eaT = sb(c, k, "eaT", [P, EA * P], BF16)
    k.we = sb(c, k, "we", [P, 3, D], BF16)
    CH = ET // 4 * P
    with ExitStack() as c2:
        dst_row = [sb(c2, k, "dst_row", [P, CH], I32) for _ in range(2)]
        eap = sb(c2, k, "eap", [P, EA, 12], BF16)
        p3 = [sb(c2, k, "p3", [P, EA, 2], BF16) for _ in range(3)]
        rest = sb(c2, k, "rest", [P, EA, 2])
        w_in, w_rest = sb(c2, k, "w_in", [2, 3, D]), sb(c2, k, "w_rest", [2, 3, D])
        w3 = [sb(c2, k, "w3", [2, 3, D], BF16) for _ in range(3)]
        with nc.Block() as block:
            @block.sync
            def _(sp):
                sp.dma_start(w_in[:], k.i["L1_gnn_We"].rearrange("l c n -> c l n")).then_inc(k.loaded.sem, 16)
                for q in range(4):
                    if q >= 2:
                        sp.wait_ge(k.copied.sem, k.copied.at(q - 1))
                    sp.dma_start(dst_row[q % 2][:], bcast(k.i["dst_row"][q * CH:(q + 1) * CH])
                                 ).then_inc(k.slot[q % 2].sem, 16)
                sp.wait_ge(k.ready.sem, k.ready.at(2))
                for j in range(6):
                    sp.dma_start(k.we[2 * j:2 * j + 2, :, :], w3[w_part[j]][:]).then_inc(k.stored[0].sem, 16)
                sp.wait_ge(k.stored[0].sem, k.stored[0].at(96))

            @block.gpsimd
            def _(gp):
                gp.memset(k.we[:], 0.0).then_inc(k.ready.sem, 1)
                gp.memset(k.eaT[:], 0.0).then_inc(k.maxed.sem, 1)

            @block.vector
            def _(v):
                ch = Chain(v, k.dve_step)
                v.wait_ge(k.loaded.sem, k.loaded.at(16))
                split3(v, ch, [w[:] for w in w3], w_in[:], w_rest[:])
                v.tensor_copy(w_rest[:, 0, 0:1], w3[0][:, 0, 0:1]).then_inc(k.ready.sem, 1)
                split3(v, ch, [p[:] for p in p3], k.ea[:], rest[:])
                for j in range(6):
                    last = v.tensor_copy(eap[:, :, 2 * j:2 * j + 2], p3[a_part[j]][:])
                last.then_inc(k.probs.sem, 1)
                for t in range(T):
                    v.memset(k.oht[:, t, ET * P:], 0.0)
                ch.link(v.memset(rest[:], 0.0))
                for t in range(T):
                    v.tensor_copy(k.oht[:, t, (ET + t) * P:(ET + t + 1) * P], k.identb[:])
                for q in range(4):
                    v.wait_ge(k.slot[q % 2].sem, k.slot[q % 2].at(16 * (q // 2 + 1)))
                    for t in range(T):
                        last = v.tensor_scalar(k.oht[:, t, q * CH:(q + 1) * CH], dst_row[q % 2][:],
                                               k.node_f[:, t:t + 1], None, ALU.is_equal)
                    last.then_inc(k.copied.sem, 1)
                ch.close()

            @block.tensor
            def _(pe):
                pe.wait_ge(k.probs.sem, k.probs.at(1))
                for i in range(EA):
                    b = (i // 8) % 2
                    if i % 8 == 0 and i >= 16:
                        pe.wait_ge(k.turned[0].sem, k.turned[0].at(i // 8 - 1))
                    m = pe.transpose(k.psb[0:12, b, (i % 8) * P:(i % 8 + 1) * P], eap[:, i, :], k.identb[:])
                    if i % 8 == 7:
                        m.then_inc(k.mm.sem, 1)

            @block.scalar
            def _(a):
                a.wait_ge(k.maxed.sem, k.maxed.at(1))
                for q in range(EA // 8):
                    a.wait_ge(k.mm.sem, k.mm.at(q + 1))
                    a.activation(k.eaT[0:12, q * 8 * P:(q + 1) * 8 * P], k.psb[0:12, q % 2, :],
                                 ACT.Copy).then_inc(k.turned[0].sem, 1)
        done((k.loaded, 16), (k.copied, 4), (k.slot[0], 32), (k.slot[1], 32), (k.ready, 2), (k.stored[0], 96),
             (k.maxed, 1), (k.probs, 1), (k.mm, EA // 8), (k.turned[0], EA // 8))


def gat_layer(k, l, XL, H2, rows_in, cols_in):
    nc = k.nc
    W1 = D + 1
    with ExitStack() as c:
        att, b_out = sb(c, k, "att", [P, D]), sb(c, k, "b_out", [P, D])
        eac = sb(c, k, "eac", [P, EA])
        L, sdot, lin, me = [sb(c, k, n, [P, EA]) for n in ("L", "sdot", "lin", "me")]
        M = sb(c, k, "M", [P, N])
        mc = sb(c, k, "mc", [P, T])
        mrest = sb(c, k, "mrest", [P, T])
        mp = sb(c, k, "mp", [P, T, 3], BF16)
        hi16 = sb(c, k, "hi16", [P, EA], F16)
        with ExitStack() as c2:
            W = [sb(c2, k, "w", [P, T, D]) for _ in range(2)]
            XR = sb(c2, k, "xr", [P, T, W1])
            bl, br = sb(c2, k, "bl", [P, D]), sb(c2, k, "br", [P, D])
            web = sb(c2, k, "web", [P, 2, D])
            wc = sb(c2, k, "wc", [P, 2])
            junk = sb(c2, k, "junk", [P, D])
            with nc.Block() as block:
                @block.sync
                def _(sp):
                    for dst, src in ((bl[:], bcast(k.i["L1_gnn_bl"][l])), (br[:], bcast(k.i["L1_gnn_br"][l])),
                                     (att[:], bcast(k.i["L1_gnn_att"][l])), (b_out[:], bcast(k.i["L1_gnn_b_out"][l])),
                                     (web[:, 0, :], bcast(k.i["L1_gnn_We"][l, 0])),
                                     (web[:, 1, :], bcast(k.i["L1_gnn_We"][l, 1]))):
                        sp.dma_start(dst, src).then_inc(k.loaded.sem, 16)
                    for j, m in enumerate((k.i["L1_gnn_Wl"], k.i["L1_gnn_Wr"])):
                        sp.dma_start(W[j][:], rows_of(m[l])).then_inc(k.slot[j].sem, 16)
                    for j, (dram, x) in enumerate(((k.xl_d, XL), (k.xr_d, XR))):
                        sp.wait_ge(k.probs.sem, k.probs.at(j + 1))
                        sp.dma_start(dram.rearrange("(k p) n -> p k n", p=P), x[:]).then_inc(k.stored[0].sem, 16)
                    sp.wait_ge(k.stored[0].sem, k.stored[0].at(32))

                @block.tensor
                def _(pe):
                    for j in range(2):
                        pe.wait_ge(k.slot[j].sem, k.slot[j].at(16))
                        mm_rows(pe, k, 4 * j, cols_in, W[j]).then_inc(k.mm.sem, 1)

                @block.vector
                def _(v):
                    ch = Chain(v, k.dve_step)
                    v.wait_ge(k.loaded.sem, k.loaded.at(96))
                    for q in range(2):
                        ch.link(v.scalar_tensor_tensor(junk[:], web[:, q, :], 0.2, att[:], ALU.mult, ALU.mult,
                                                       accum_out=wc[:, q:q + 1]))
                    ch.link(v.tensor_scalar(eac[:], k.ea[:, :, 0], wc[:, 0:1], None, ALU.mult))
                    v.memset(M[:], NEG)
                    ch.link(v.scalar_tensor_tensor(eac[:], k.ea[:, :, 1], wc[:, 1:2], eac[:], ALU.mult, ALU.add))
                    for j, (x, b) in enumerate(((XL, bl), (XR, br))):
                        v.wait_ge(k.mm.sem, k.mm.at(j + 1))
                        for t in range(T):
                            last = v.tensor_tensor(x[:, t, 0:D], k.ps[:, 4 * j + t, :], b[:], ALU.add)
                        ch.link(last)
                        for t in range(T):
                            last = v.scalar_tensor_tensor(junk[:], x[:, t, 0:D], 0.2, att[:], ALU.mult, ALU.mult,
                                                          accum_out=x[:, t, D:W1])
                            if t < T - 1:
                                ch.link(last)
                        last.then_inc(k.probs.sem, 1)
                        v.wait_ge(k.probs.sem, k.probs.at(j + 1))
                    ch.close()
            done((k.loaded, 96), (k.slot[0], 16), (k.slot[1], 16), (k.stored[0], 32), (k.mm, 2), (k.probs, 2))

        with ExitStack() as c2:
            G = [sb(c2, k, "g", [P, W1]) for _ in range(4)]
            r = [sb(c2, k, "r", [P, D]) for _ in range(4)]
            junk = sb(c2, k, "junk", [P, D])
            pen = [sb(c2, k, "pen", [P, N], BF16) for _ in range(2)]
            with nc.Block() as block:
                @block.gpsimd
                def _(gp):
                    def gather(i, dram, idx, **how):
                        gp.indirect_dma_start(G[i % 4][:], None, dram,
                                              bass.IndirectOffsetOnAxis(ap=idx[:, i:i + 1].bitcast(U32), axis=0),
                                              **how).then_inc(k.pool_slot[i % 4].sem, 16)
                    gather(0, k.xl_d, k.src_i)
                    for i in range(EA):
                        if i + 1 < EA:
                            if i + 1 >= 4:
                                gp.wait_ge(k.mm.sem, k.mm.at(i - 2))
                                gp.wait_ge(k.probs.sem, k.probs.at(i - 2))
                            gather(i + 1, k.xl_d, k.src_i)
                        gp.wait_ge(k.pool_slot[i % 4].sem, k.pool_slot[i % 4].at(32 * (i // 4) + 16))
                        gather(i, k.xr_d, k.dst_i, compute_op=ALU.add)

                @block.tensor
                def _(pe):
                    def step(i, u, j):
                        pe.wait_ge(k.pool_slot[u].sem, k.pool_slot[u].at(32) + j * 32)
                        if later(i, 4):
                            pe.wait_ge(k.copied.sem, k.copied.at(-3) + i)
                        pe.matmul(k.ps[:, u, :], k.ident[:], G[u][:, 0:D], start=True, stop=False)
                        pe.matmul(k.ps[:, u, :], k.eaT[:, bass.ds(i * P, P)], k.we[:, l, :],
                                  start=False, stop=True).then_inc(k.mm.sem, 1)
                    for u in range(4):
                        step(u, u, 0)
                    with pe.Fori(1, EA // 4) as j:
                        for u in range(4):
                            step(j * 4 + u, u, j)

                @block.scalar
                def _(a):
                    def step(i, u):
                        a.wait_ge(k.mm.sem, k.mm.at(1) + i)
                        if later(i, 4):
                            a.wait_ge(k.probs.sem, k.probs.at(-3) + i)
                        a.activation(r[u][:], k.ps[:, u, :], ACT.Relu, scale=0.8).then_inc(k.copied.sem, 1)
                    for u in range(4):
                        step(u, u)
                    with a.Fori(1, EA // 4) as j:
                        for u in range(4):
                            step(j * 4 + u, u)

                @block.vector
                def _(v):
                    ch = Chain(v, k.dve_step)
                    with v.Fori(0, EA // 4) as j:
                        ch.loop = j * 8
                        for u in range(4):
                            col = bass.ds(j * 4 + u, 1)
                            v.tensor_scalar(pen[u % 2][:], k.ramp[:], k.dst_f[:, col], NEG, ALU.not_equal, ALU.mult)
                            v.wait_ge(k.copied.sem, k.copied.at(u + 1) + j * 4)
                            v.scalar_tensor_tensor(junk[:], r[u][:], 1.0, att[:], ALU.mult, ALU.mult,
                                                   accum_out=sdot[:, col])
                            v.tensor_tensor(lin[:, col], G[u][:, D:W1], eac[:, col], ALU.add
                                            ).then_inc(k.probs.sem, 1)
                            v.wait_ge(k.probs.sem, k.probs.at(u + 1) + j * 4)
                            ch.link(v.tensor_tensor(L[:, col], sdot[:, col], lin[:, col], ALU.add))
                            ch.link(v.scalar_tensor_tensor(M[:], pen[u % 2][:], L[:, col], M[:], ALU.add, ALU.max))
                    ch.close(EA * 2)
            done((k.pool_slot[0], EA * 8), (k.pool_slot[1], EA * 8), (k.pool_slot[2], EA * 8), (k.pool_slot[3], EA * 8),
                 (k.mm, EA), (k.copied, EA), (k.probs, EA))

        with nc.Block() as block:
            @block.tensor
            def _(pe):
                for t in range(T):
                    m = pe.transpose(k.ps[:, 0, t * P:(t + 1) * P], M[:, t * P:(t + 1) * P], k.ident[:])
                m.then_inc(k.mm.sem, 1)
                pe.wait_ge(k.ready.sem, k.ready.at(1))
                for i in range(EA):
                    for t in range(T):
                        m = pe.matmul(k.ps[:, 1, 3 * i:3 * i + 3], k.oht[:, t, i * P:(i + 1) * P],
                                      mp[:, t, :], start=(t == 0), stop=(t == T - 1))
                m.then_inc(k.mm.sem, 1)

            @block.vector
            def _(v):
                ch = Chain(v, k.dve_step)
                v.wait_ge(k.mm.sem, k.mm.at(1))
                ch.link(v.tensor_reduce(mc[:], k.ps[:, 0, :].rearrange("p (t n) -> p t n", t=T), AX.X, ALU.max))
                split3(v, ch, [mp[:, :, q] for q in range(3)], mc[:], mrest[:])
                v.tensor_copy(mrest[:, 0:1], mc[:, 0:1]).then_inc(k.ready.sem, 1)
                v.wait_ge(k.mm.sem, k.mm.at(2))
                ch.link(v.tensor_reduce(me[:], k.ps[:, 1, 0:3 * EA].rearrange("p (i c) -> p i c", c=3), AX.X, ALU.add))
                v.tensor_tensor(L[:], L[:], me[:], ALU.subtract).then_inc(k.ready.sem, 1)
                v.wait_ge(k.copied.sem, k.copied.at(1))
                ch.link(v.tensor_scalar(me[:], me[:], EX_SCALE, None, ALU.mult))
                ch.link(v.tensor_copy(hi16[:], me[:]))
                ch.link(v.tensor_copy(L[:], hi16[:]))
                ch.link(v.tensor_tensor(me[:], me[:], L[:], ALU.subtract))
                ch.close()

            @block.scalar
            def _(a):
                a.wait_ge(k.ready.sem, k.ready.at(2))
                a.activation(me[:], L[:], ACT.Exp).then_inc(k.copied.sem, 1)
        done((k.mm, 2), (k.ready, 2), (k.copied, 1))

        with ExitStack() as c2:
            oh = [sb(c2, k, "oh", [P, N], F16) for _ in range(3)]
            dh = [sb(c2, k, "dh", [P, N], F16) for _ in range(3)]
            dl = [sb(c2, k, "dl", [P, N], F16) for _ in range(3)]
            A = sb(c2, k, "A", [P, T, N])
            rden = sb(c2, k, "rden", [P, T])
            with nc.Block() as block:
                @block.vector
                def _(v):
                    def step(i, u):
                        if later(i, 3):
                            v.wait_ge(k.mm.sem, k.mm.at(-2) + i)
                        col = bass.ds(i, 1)
                        v.tensor_scalar(oh[u][:], k.ramp[:], k.src_f[:, col], None, ALU.is_equal)
                        v.tensor_scalar(dh[u][:], k.ramp[:], k.dst_f[:, col], L[:, col], ALU.is_equal, ALU.mult)
                        v.tensor_scalar(dl[u][:], k.ramp[:], k.dst_f[:, col], me[:, col], ALU.is_equal,
                                        ALU.mult).then_inc(k.ready.sem, 1)
                    for u in range(3):
                        step(u, u)
                    with v.Fori(1, EA // 3) as j:
                        for u in range(3):
                            step(j * 3 + u, u)

                @block.tensor
                def _(pe):
                    def step(i, u, first=False, last=False):
                        pe.wait_ge(k.ready.sem, k.ready.at(1) + i)
                        for t in range(T):
                            for d in (dh, dl):
                                m = pe.matmul(k.ps[:, t, :], oh[u][:, t * P:(t + 1) * P], d[u][:],
                                              start=first and d is dh, stop=last and d is dl)
                        m.then_inc(k.mm.sem, 1)
                    for u in range(3):
                        step(u, u, first=(u == 0))
                    with pe.Fori(1, EA // 3 - 1) as j:
                        for u in range(3):
                            step(j * 3 + u, u)
                    for u in range(3):
                        step(EA - 3 + u, u, last=(u == 2))
            done((k.mm, EA), (k.ready, EA))
            with nc.Block() as block:
                @block.scalar
                def _(a):
                    for t in range(T):
                        i = a.activation(A[:, t, :], k.ps[:, t, :], ACT.Copy)
                    i.then_inc(k.copied.sem, 1)

                @block.tensor
                def _(pe):
                    pe.wait_ge(k.copied.sem, k.copied.at(1))
                    for t in range(T):
                        for s in range(T):
                            m = pe.matmul(k.ps[:, t, 0:1], A[:, s, t * P:(t + 1) * P], k.ones[:, 0:1],
                                          start=(s == 0), stop=(s == T - 1))
                    m.then_inc(k.mm.sem, 1)
                    for t in range(T):
                        for s in range(T):
                            m = pe.matmul(k.ps[:, T + t, :], A[:, s, t * P:(t + 1) * P], XL[:, s, 0:D],
                                          start=(s == 0), stop=(s == T - 1))
                        m.then_inc(k.mm.sem, 1)

                @block.vector
                def _(v):
                    ch = Chain(v, k.dve_step)
                    for t in range(T):
                        v.tensor_tensor(H2[:, t, :], rows_in[:, t, :], b_out[:], ALU.add)
                    v.wait_ge(k.mm.sem, k.mm.at(1))
                    ch.link(v.tensor_scalar(rden[:], k.ps[:, 0:T, 0], 1e-16 * EX_SCALE, None, ALU.add))
                    ch.link(v.reciprocal(rden[:], rden[:]))
                    for t in range(T):
                        v.wait_ge(k.mm.sem, k.mm.at(t + 2))
                        v.scalar_tensor_tensor(H2[:, t, :], k.ps[:, T + t, :], rden[:, t:t + 1], H2[:, t, :],
                                               ALU.mult, ALU.add)
                    ch.close()
            done((k.copied, 1), (k.mm, 1 + T))


def gat(k):
    nc = k.nc
    with ExitStack() as c:
        gat_setup(k, c)
        XL = sb(c, k, "xl", [P, T, D + 1])
        H2 = sb(c, k, "h2", [P, T, D])
        gb = [sb(c, k, "gb", [P, D]) for _ in range(2)]
        for l in range(3):
            gat_layer(k, l, XL, H2, k.N, k.NT)
            load(k, ((gb[0][:], bcast(k.i["L1_gnn_gamma"][l])), (gb[1][:], bcast(k.i["L1_gnn_beta"][l]))))
            layernorm(k, H2, k.N, k.NT, passes=(gb,), relu=True)
        with nc.Block() as block:
            @block.vector
            def _(v):
                v.tensor_tensor(k.X[:], k.X[:], k.N[:], ALU.add)


def load(k, pairs):
    with k.nc.Block() as block:
        @block.sync
        def _(sp):
            for dst, src in pairs:
                sp.dma_start(dst, src).then_inc(k.loaded.sem, 16)
            sp.wait_ge(k.loaded.sem, k.loaded.at(16 * len(pairs)))
    done((k.loaded, 16 * len(pairs)))



def positional_ffn(k):
    nc, i_ = k.nc, k.i
    FF = 2048
    HT = FF // P
    SL = 64
    with ExitStack() as c:
        XA = sb(c, k, "xa", [P, T, N])
        YT = sb(c, k, "yt", [P, T, N])
        with ExitStack() as c2:
            gb = [sb(c2, k, "gb", [P, D]) for _ in range(2)]
            N2, N2T = sb(c2, k, "n2", [P, T, D]), sb(c2, k, "n2t", [P, T, D])
            W = sb(c2, k, "w", [P, T, D])
            ab = sb(c2, k, "ab", [P, T])
            load(k, ((gb[0][:], bcast(i_["L1_ffn_ln_g"])), (gb[1][:], bcast(i_["L1_ffn_ln_b"])), (ab[:], i_["attn_b"]),
                     (W[:], rows_of(i_["attn_wT"]))))
            layernorm(k, k.N, N2, N2T, passes=(gb,))
            with nc.Block() as block:
                @block.tensor
                def _(pe):
                    mm_cols(pe, k, 0, W, N2T).then_inc(k.mm.sem, 1)

                @block.vector
                def _(v):
                    v.wait_ge(k.mm.sem, k.mm.at(1))
                    for t in range(T):
                        v.scalar_tensor_tensor(XA[:, t, :], k.ps[:, t, :], ab[:, t:t + 1], k.NT[:, t, :],
                                               ALU.add, ALU.add)
            done((k.mm, 1))

        with ExitStack() as c2:
            W1 = [sb(c2, k, "w1", [P, T, FF]) for _ in range(2)]
            W2 = [sb(c2, k, "w2", [P, HT, D]) for _ in range(2)]
            b1 = [sb(c2, k, "b1", [P, HT]) for _ in range(2)]
            b2 = [sb(c2, k, "b2", [P, T]) for _ in range(2)]
            hT = sb(c2, k, "hT", [P, HT, SL])
            own = lambda x, f, e: x[:, f, :].rearrange("p (m e t) -> p m e t", m=2, e=EXPERTS)[:, :, bass.ds(e, 1), :]\
                .rearrange("p m e t -> p m (e t)")
            with nc.Block() as block:
                def walk(eng, step):
                    for u in range(2):
                        step(u, u, 0)
                    with eng.Fori(1, EXPERTS // 2) as j:
                        for u in range(2):
                            step(j * 2 + u, u, j)

                @block.sync
                def _(sp):
                    def step(e, u, j):
                        if later(e, 2):
                            sp.wait_ge(k.heads.sem, k.heads.at(-1) + e)
                        for dst, src in ((W1[u][:], i_["fc1T"][bass.ds(e, 1)].rearrange("a (k p) n -> p (a k) n", p=P)),
                                         (b1[u][:], i_["fc1_b"][bass.ds(e, 1)].rearrange("a p m -> p (a m)")),
                                         (W2[u][:], i_["fc2T"][bass.ds(e, 1)].rearrange("a (k p) n -> p (a k) n", p=P)),
                                         (b2[u][:], i_["fc2_b"][bass.ds(e, 1)].rearrange("a p m -> p (a m)"))):
                            sp.dma_start(dst, src).then_inc(k.slot[u].sem, 16)
                    walk(sp, step)

                @block.tensor
                def _(pe):
                    def step(e, u, j):
                        pe.wait_ge(k.slot[u].sem, k.slot[u].at(64) + j * 64)
                        for s in range(HT):
                            for f in range(T):
                                m = pe.matmul(k.ps[:, s // 8, (s % 8) * SL:(s % 8 + 1) * SL].rearrange(
                                    "p (m t) -> p m t", m=2), W1[u][:, f, s * P:(s + 1) * P], own(XA, f, e),
                                    start=(f == 0), stop=(f == T - 1))
                            if s % 8 == 7:
                                m.then_inc(k.mm.sem, 1)
                        pe.wait_ge(k.copied.sem, k.copied.at(2) + e * 2)
                        if later(e, 2):
                            pe.wait_ge(k.heads.sem, k.heads.at(-1) + e)
                        for t in range(T):
                            for s in range(HT):
                                m = pe.matmul(k.ps[:, 2 + u, t * SL:(t + 1) * SL], W2[u][:, s, t * P:(t + 1) * P],
                                              hT[:, s, :], start=(s == 0), stop=(s == HT - 1))
                        m.then_inc(k.out.sem, 1)
                    walk(pe, step)

                @block.scalar
                def _(a):
                    def step(e, u, j):
                        if later(e, 1):
                            a.wait_ge(k.out.sem, k.out.at(0) + e)
                        for q in range(2):
                            a.wait_ge(k.mm.sem, k.mm.at(q + 1) + e * 2)
                            for s in range(8 * q, 8 * q + 8):
                                m = a.activation(hT[:, s, :], k.ps[:, q, (s % 8) * SL:(s % 8 + 1) * SL], ACT.Gelu,
                                                 bias=b1[u][:, s:s + 1])
                            m.then_inc(k.copied.sem, 1)
                    walk(a, step)

                @block.vector
                def _(v):
                    def step(e, u, j):
                        v.wait_ge(k.out.sem, k.out.at(1) + e)
                        for t in range(T):
                            m = v.tensor_scalar(own(YT, t, e), k.ps[:, 2 + u, t * SL:(t + 1) * SL].rearrange(
                                "p (m t) -> p m t", m=2), b2[u][:, t:t + 1], None, ALU.add)
                        m.then_inc(k.heads.sem, 1)
                    walk(v, step)
            done((k.heads, EXPERTS), (k.slot[0], 32 * EXPERTS), (k.slot[1], 32 * EXPERTS), (k.mm, 2 * EXPERTS),
                 (k.copied, 2 * EXPERTS), (k.out, EXPERTS))

        W, nb, o = sb(c, k, "wn", [P, T, D]), sb(c, k, "nb", [P, D]), sb(c, k, "o", [P, T, D])
        load(k, ((W[:], rows_of(i_["next_wT"])), (nb[:], bcast(i_["L1_ffn_next_b"]))))
        with nc.Block() as block:
            @block.tensor
            def _(pe):
                mm_rows(pe, k, 0, YT, W).then_inc(k.mm.sem, 1)

            @block.vector
            def _(v):
                v.wait_ge(k.mm.sem, k.mm.at(1))
                for t in range(T):
                    v.tensor_tensor(o[:, t, :], k.ps[:, t, :], nb[:], ALU.add).then_inc(k.ready.sem, 1)
                for t in range(T):
                    v.wait_ge(k.copied.sem, k.copied.at(t + 1))
                    v.tensor_tensor(k.X[:, t, :], k.X[:, t, :], o[:, t, :], ALU.add)

            @block.scalar
            def _(a):
                for t in range(T):
                    a.wait_ge(k.ready.sem, k.ready.at(t + 1))
                    a.activation(o[:, t, :], o[:, t, :], ACT.Gelu).then_inc(k.copied.sem, 1)
        done((k.mm, 1), (k.ready, T), (k.copied, T))



def graph_conv(k):
    nc = k.nc
    with ExitStack() as c:
        W, bias = sb(c, k, "w", [P, T, D]), sb(c, k, "bias", [P, D])
        sup = sb(c, k, "sup", [P, T, D])
        AT = sb(c, k, "at", [P, T, N])
        ew, rest = sb(c, k, "ew", [P, ET]), sb(c, k, "rest", [P, ET])
        wp = [sb(c, k, "wp", [P, ET], BF16) for _ in range(3)]
        wf = [sb(c, k, "wf", [P, ET]) for _ in range(3)]
        oh = [sb(c, k, "oh", [P, N], BF16) for _ in range(2)]
        sw = [[sb(c, k, "sw", [P, N], BF16) for _ in range(3)] for _ in range(2)]
        load(k, ((ew[:], k.i["edge_weight"].rearrange("(p j) -> p j", p=P)), (W[:], rows_of(k.i["L2_gnn_weight"])),
                 (bias[:], bcast(k.i["L2_gnn_bias"]))))
        with nc.Block() as block:
            @block.tensor
            def _(pe):
                mm_rows(pe, k, 4, k.NT, W).then_inc(k.mm.sem, 1)

            @block.vector
            def _(v):
                ch = Chain(v, k.dve_step)
                split3(v, ch, [w[:] for w in wp], ew[:], rest[:])
                for q in range(3):
                    v.tensor_copy(wf[q][:], wp[q][:])
                ch.close()

            @block.scalar
            def _(a):
                a.wait_ge(k.mm.sem, k.mm.at(1))
                for t in range(T):
                    a.activation(sup[:, t, :], k.ps[:, T + t, :], ACT.Copy)
        done((k.mm, 1))
        with nc.Block() as block:
            @block.vector
            def _(v):
                def step(i, u):
                    if later(i, 2):
                        v.wait_ge(k.mm.sem, k.mm.at(-1) + i)
                    col = bass.ds(i, 1)
                    v.tensor_scalar(oh[u][:], k.ramp[:], k.dst_f[:, col], None, ALU.is_equal)
                    for q in range(3):
                        m = v.tensor_scalar(sw[u][q][:], k.ramp[:], k.src_f[:, col], wf[q][:, col],
                                            ALU.is_equal, ALU.mult)
                    m.then_inc(k.ready.sem, 1)
                for u in range(2):
                    step(u, u)
                with v.Fori(1, ET // 2) as j:
                    for u in range(2):
                        step(j * 2 + u, u)

            @block.tensor
            def _(pe):
                def step(i, u, first=False, last=False):
                    pe.wait_ge(k.ready.sem, k.ready.at(1) + i)
                    for t in range(T):
                        for q in range(3):
                            m = pe.matmul(k.ps[:, t, :], oh[u][:, t * P:(t + 1) * P], sw[u][q][:],
                                          start=first and q == 0, stop=last and q == 2)
                    m.then_inc(k.mm.sem, 1)
                step(0, 0, first=True)
                step(1, 1)
                with pe.Fori(1, ET // 2 - 1) as j:
                    for u in range(2):
                        step(j * 2 + u, u)
                step(ET - 2, 0)
                step(ET - 1, 1, last=True)
        done((k.mm, ET), (k.ready, ET))
        with nc.Block() as block:
            @block.scalar
            def _(a):
                for t in range(T):
                    m = a.activation(AT[:, t, :], k.ps[:, t, :], ACT.Copy)
                m.then_inc(k.copied.sem, 1)

            @block.tensor
            def _(pe):
                pe.wait_ge(k.copied.sem, k.copied.at(1))
                mm_rows(pe, k, 4, AT, sup).then_inc(k.mm.sem, 1)

            @block.vector
            def _(v):
                ch = Chain(v, k.dve_step)
                for t in range(T):
                    last = v.tensor_tensor(k.X[:, t, :], k.X[:, t, :], bias[:], ALU.add)
                ch.link(last)
                v.wait_ge(k.mm.sem, k.mm.at(1))
                for t in range(T):
                    v.tensor_tensor(k.X[:, t, :], k.X[:, t, :], k.ps[:, T + t, :], ALU.add)
                ch.close()
        done((k.mm, 1), (k.copied, 1))



def expert_choice_ffn(k):
    nc, i_ = k.nc, k.i
    E, CAP, FF = 16, 32, 256
    HT = FF // P
    with ExitStack() as c:
        g = sb(c, k, "g", [P, T, E])
        sw1, sw2 = sb(c, k, "sw1", [P, T, FF]), sb(c, k, "sw2", [P, HT, D])
        sb1, sb2 = sb(c, k, "sb1", [P, HT]), sb(c, k, "sb2", [P, D])
        lg = sb(c, k, "lg", [P, T, E])
        mx, sm = sb(c, k, "mx", [P, T]), sb(c, k, "sm", [P, T])
        pr = sb(c, k, "pr", [E, N])
        val, at = sb(c, k, "val", [E, CAP]), sb(c, k, "at", [E, CAP], U32)
        at_c, atf_c, val_c = sb(c, k, "at_c", [P, T], I32), sb(c, k, "atf_c", [P, T]), sb(c, k, "val_c", [P, T])
        shT = sb(c, k, "shT", [P, HT, N])
        tok, tokT = sb(c, k, "tok", [P, T, D]), sb(c, k, "tokT", [P, T, N])
        yT, y = sb(c, k, "yT", [P, T, N]), sb(c, k, "y", [P, T, D])
        back = sb(c, k, "back", [P, T, N])
        load(k, ((g[:], rows_of(i_["L2_ffn_gate_w"])), (sw1[:], rows_of(i_["L2_ffn_sw1"])),
                 (sw2[:], i_["L2_ffn_sw2"].rearrange("(k p) n -> p k n", p=P)), (sb1[:], i_["sb1"]),
                 (sb2[:], bcast(i_["L2_ffn_sb2"])), (rows_of(k.rows_d), k.N[:])))
        with nc.Block() as block:
            @block.tensor
            def _(pe):
                for t in range(T):
                    for f in range(T):
                        m = pe.matmul(k.ps[:, t, 0:E], k.NT[:, f, t * P:(t + 1) * P], g[:, f, :],
                                      start=(f == 0), stop=(f == T - 1))
                m.then_inc(k.mm.sem, 1)
                for s in range(HT):
                    for f in range(T):
                        m = pe.matmul(k.ps[:, T + s, :], sw1[:, f, s * P:(s + 1) * P], k.NT[:, f, :],
                                      start=(f == 0), stop=(f == T - 1))
                m.then_inc(k.mm.sem, 1)
                pe.wait_ge(k.ready.sem, k.ready.at(2))
                for t in range(T):
                    m = pe.transpose(k.ps[0:E, 6, t * P:(t + 1) * P], lg[:, t, :], k.ident[:])
                m.then_inc(k.mm.sem, 1)

            @block.vector
            def _(v):
                ch = Chain(v, k.dve_step)
                v.wait_ge(k.mm.sem, k.mm.at(1))
                ch.link(v.tensor_reduce(mx[:], k.ps[:, 0:T, 0:E], AX.X, ALU.max))
                for t in range(T):
                    m = v.tensor_scalar(lg[:, t, :], k.ps[:, t, 0:E], mx[:, t:t + 1], None, ALU.subtract)
                m.then_inc(k.ready.sem, 1)
                v.wait_ge(k.copied.sem, k.copied.at(1))
                ch.link(v.tensor_reduce(sm[:], lg[:], AX.X, ALU.add))
                ch.link(v.reciprocal(sm[:], sm[:]))
                for t in range(T):
                    m = v.tensor_scalar(lg[:, t, :], lg[:, t, :], sm[:, t:t + 1], None, ALU.mult)
                m.then_inc(k.ready.sem, 1)
                v.wait_ge(k.mm.sem, k.mm.at(3))
                ch.link(v.tensor_copy(pr[:], k.ps[0:E, 6, :]))
                for q in range(CAP // 8):
                    o = slice(8 * q, 8 * q + 8)
                    ch.link(v.max(val[:, o], pr[:]))
                    ch.link(v.max_index(at[:, o], val[:, o], pr[:]))
                    if q < CAP // 8 - 1:
                        ch.link(v.match_replace(pr[:], val[:, o], pr[:], -1.0))
                v.tensor_copy(sm[0:E, 0:1], val[:, 0:1]).then_inc(k.ready.sem, 1)
                v.wait_ge(k.loaded.sem, k.loaded.at(64))
                ch.link(v.tensor_copy(atf_c[:], at_c[:]))
                for t in range(T):
                    v.tensor_scalar(back[:, t, :], k.ramp_f[:], atf_c[:, t:t + 1], val_c[:, t:t + 1],
                                    ALU.is_equal, ALU.mult)
                ch.close()

            @block.scalar
            def _(a):
                a.wait_ge(k.ready.sem, k.ready.at(1))
                a.activation(lg[:], lg[:], ACT.Exp).then_inc(k.copied.sem, 1)
                a.wait_ge(k.mm.sem, k.mm.at(2))
                for s in range(HT):
                    a.activation(shT[:, s, :], k.ps[:, T + s, :], ACT.Gelu_apprx_tanh, bias=sb1[:, s:s + 1])

            @block.sync
            def _(sp):
                sp.wait_ge(k.ready.sem, k.ready.at(3))
                sp.dma_start(k.at_d.rearrange("(e j) -> e j", e=E), at[:].bitcast(I32)).then_inc(k.loaded.sem, 16)
                sp.dma_start(k.val_d.rearrange("(e j) -> e j", e=E), val[:]).then_inc(k.loaded.sem, 16)
                sp.wait_ge(k.loaded.sem, k.loaded.at(32))
                with nc.allow_non_contiguous_dma(reason="512 words"):
                    sp.dma_start(at_c[:], k.at_d.rearrange("(t p) -> p t", p=P)).then_inc(k.loaded.sem, 16)
                    sp.dma_start(val_c[:], k.val_d.rearrange("(t p) -> p t", p=P)).then_inc(k.loaded.sem, 16)

            @block.gpsimd
            def _(gp):
                gp.wait_ge(k.loaded.sem, k.loaded.at(64))
                for t in range(T):
                    gp.indirect_dma_start(tok[:, t, :], None, k.rows_d,
                                          bass.IndirectOffsetOnAxis(ap=at_c[:, t:t + 1].bitcast(U32), axis=0)
                                          ).then_inc(k.gathered.sem, 16)
                gp.wait_ge(k.gathered.sem, k.gathered.at(16 * T))
        done((k.mm, 3), (k.ready, 3), (k.copied, 1), (k.loaded, 64), (k.gathered, 16 * T))

        def turn(src, dst):
            with nc.Block() as block:
                @block.tensor
                def _(pe):
                    for f in range(T):
                        for t in range(T):
                            m = pe.transpose(k.ps[:, f, t * P:(t + 1) * P], src[:, t, f * P:(f + 1) * P], k.ident[:])
                        m.then_inc(k.mm.sem, 1)

                @block.vector
                def _(v):
                    for f in (0, 2):
                        v.wait_ge(k.mm.sem, k.mm.at(f + 1))
                        v.tensor_copy(dst[:, f, :], k.ps[:, f, :])

                @block.scalar
                def _(a):
                    for f in (1, 3):
                        a.wait_ge(k.mm.sem, k.mm.at(f + 1))
                        a.activation(dst[:, f, :], k.ps[:, f, :], ACT.Copy)
            done((k.mm, T))

        turn(tok, tokT)
        with ExitStack() as c2:
            W1 = [sb(c2, k, "w1", [P, T, FF]) for _ in range(4)]
            W2 = [sb(c2, k, "w2", [P, HT, D]) for _ in range(4)]
            b1 = [sb(c2, k, "b1", [P, HT]) for _ in range(4)]
            b2 = [sb(c2, k, "b2", [P, T]) for _ in range(4)]
            hT = [sb(c2, k, "hT", [P, HT, CAP]) for _ in range(2)]
            with nc.Block() as block:
                def walk(eng, step):
                    for u in range(4):
                        step(u, u, 0)
                    with eng.Fori(1, E // 4) as j:
                        for u in range(4):
                            step(j * 4 + u, u, j)

                @block.sync
                def _(sp):
                    def step(e, u, j):
                        if later(e, 4):
                            sp.wait_ge(k.heads.sem, k.heads.at(-3) + e)
                        for dst, src in ((W1[u][:], i_["L2_ffn_w1"][bass.ds(e, 1)].rearrange("a (k p) n -> p (a k) n", p=P)),
                                         (b1[u][:], i_["l2b1"][bass.ds(e, 1)].rearrange("a p m -> p (a m)")),
                                         (W2[u][:], i_["L2_ffn_w2"][bass.ds(e, 1)].rearrange("a (k p) n -> p (a k) n", p=P)),
                                         (b2[u][:], i_["l2b2"][bass.ds(e, 1)].rearrange("a p m -> p (a m)"))):
                            sp.dma_start(dst, src).then_inc(k.slot[u].sem, 16)
                    walk(sp, step)

                @block.tensor
                def _(pe):
                    def step(e, u, j):
                        pe.wait_ge(k.slot[u].sem, k.slot[u].at(64) + j * 64)
                        for s in range(HT):
                            for f in range(T):
                                m = pe.matmul(k.ps[:, u, s * CAP:(s + 1) * CAP], W1[u][:, f, s * P:(s + 1) * P],
                                              tokT[:, f, bass.ds(e * CAP, CAP)], start=(f == 0), stop=(f == T - 1))
                        m.then_inc(k.mm.sem, 1)
                        pe.wait_ge(k.copied.sem, k.copied.at(1) + e)
                        if later(e, 4):
                            pe.wait_ge(k.heads.sem, k.heads.at(-3) + e)
                        for t in range(T):
                            for s in range(HT):
                                m = pe.matmul(k.ps[:, 4 + u, t * CAP:(t + 1) * CAP], W2[u][:, s, t * P:(t + 1) * P],
                                              hT[u % 2][:, s, :], start=(s == 0), stop=(s == HT - 1))
                        m.then_inc(k.out.sem, 1)
                    walk(pe, step)

                @block.scalar
                def _(a):
                    def step(e, u, j):
                        a.wait_ge(k.mm.sem, k.mm.at(1) + e)
                        if later(e, 2):
                            a.wait_ge(k.out.sem, k.out.at(-1) + e)
                        for s in range(HT):
                            m = a.activation(hT[u % 2][:, s, :], k.ps[:, u, s * CAP:(s + 1) * CAP],
                                             ACT.Gelu_apprx_tanh, bias=b1[u][:, s:s + 1])
                        m.then_inc(k.copied.sem, 1)
                    walk(a, step)

                @block.vector
                def _(v):
                    def step(e, u, j):
                        v.wait_ge(k.out.sem, k.out.at(1) + e)
                        for t in range(T):
                            m = v.tensor_scalar(yT[:, t, bass.ds(e * CAP, CAP)], k.ps[:, 4 + u, t * CAP:(t + 1) * CAP],
                                                b2[u][:, t:t + 1], None, ALU.add)
                        m.then_inc(k.heads.sem, 1)
                    walk(v, step)
            done((k.heads, E), (k.mm, E), (k.copied, E), (k.out, E), *[(k.slot[u], 16 * E) for u in range(4)])
        turn(yT, y)
        with nc.Block() as block:
            @block.tensor
            def _(pe):
                for t in range(T):
                    for s in range(HT):
                        pe.matmul(k.ps[:, T + t, :], shT[:, s, t * P:(t + 1) * P], sw2[:, s, :],
                                  start=(s == 0), stop=False)
                    for s in range(T):
                        m = pe.matmul(k.ps[:, T + t, :], back[:, s, t * P:(t + 1) * P], y[:, s, :],
                                      start=False, stop=(s == T - 1))
                    m.then_inc(k.mm.sem, 1)

            @block.vector
            def _(v):
                ch = Chain(v, k.dve_step)
                for t in range(T):
                    last = v.tensor_tensor(k.X[:, t, :], k.X[:, t, :], sb2[:], ALU.add)
                ch.link(last)
                for t in range(T):
                    v.wait_ge(k.mm.sem, k.mm.at(t + 1))
                    v.tensor_tensor(k.X[:, t, :], k.X[:, t, :], k.ps[:, T + t, :], ALU.add)
                ch.close()
        done((k.mm, T))



def sage(k):
    nc, i_ = k.nc, k.i
    E = 4
    with ExitStack() as c:
        masks, wt = routing(k, c, k.NT, i_["L3_gnn_gate_W"], i_["L3_gnn_gate_b"], E, "gates", 2)
        wE = sb(c, k, "wE", [P, T, 8])
        A0 = sb(c, k, "A0", [P, T, N])
        H1, PR, o = [sb(c, k, n, [P, T, D]) for n in ("H1", "PR", "o")]
        W = [[sb(c, k, "w", [P, T, D]) for _ in range(4)] for _ in range(2)]
        b0 = [sb(c, k, "b0", [P, T]) for _ in range(2)]
        b1 = [sb(c, k, "b1", [P, D]) for _ in range(2)]
        with nc.Block() as block:
            @block.tensor
            def _(pe):
                mm_cols(pe, k, 0, k.N, k.Cn).then_inc(k.mm.sem, 1)

            @block.scalar
            def _(a):
                a.wait_ge(k.mm.sem, k.mm.at(1))
                for t in range(T):
                    a.activation(A0[:, t, :], k.ps[:, t, :], ACT.Copy)

            @block.vector
            def _(v):
                ch = Chain(v, k.dve_step)
                for t in range(T):
                    ch.link(v.tensor_scalar(wE[:, t, :], masks[:, t, 0, :], wt[:, t, 0:1], None, ALU.mult))
                    ch.link(v.scalar_tensor_tensor(wE[:, t, :], masks[:, t, 1, :], wt[:, t, 1:2], wE[:, t, :],
                                                   ALU.mult, ALU.add))
                ch.close()
        done((k.mm, 1))
        with nc.Block() as block:
            def walk(eng, step):
                for u in range(2):
                    step(u, u, 0)
                with eng.Fori(1, E // 2) as j:
                    for u in range(2):
                        step(j * 2 + u, u, j)

            @block.sync
            def _(sp):
                def step(e, u, j):
                    if later(e, 2):
                        sp.wait_ge(k.heads.sem, k.heads.at(-1) + e)
                    for q, m in enumerate((i_["L3_gnn_Wl"], i_["L3_gnn_Wr"])):
                        for l in range(2):
                            sp.dma_start(W[u][2 * l + q][:], m[bass.ds(e, 1), l].rearrange(
                                "a (k p) n -> p (a k) n", p=P)).then_inc(k.slot[u].sem, 16)
                    sp.dma_start(b0[u][:], i_["sage_b0"][bass.ds(e, 1)].rearrange("a p m -> p (a m)")
                                 ).then_inc(k.slot[u].sem, 16)
                    sp.dma_start(b1[u][:], i_["sage_b1"][bass.ds(e, 1), :].to_broadcast([P, D])
                                 ).then_inc(k.slot[u].sem, 16)
                walk(sp, step)

            @block.tensor
            def _(pe):
                def step(e, u, j):
                    pe.wait_ge(k.slot[u].sem, k.slot[u].at(96) + j * 96)
                    if later(e, 1):
                        pe.wait_ge(k.heads.sem, k.heads.at(0) + e)
                    for t in range(T):
                        for w, x in ((W[u][0], A0), (W[u][1], k.NT)):
                            for f in range(T):
                                m = pe.matmul(k.ps[:, t, :], w[:, f, t * P:(t + 1) * P], x[:, f, :],
                                              start=(f == 0 and x is A0), stop=(f == T - 1 and x is not A0))
                        m.then_inc(k.mm.sem, 1)
                    pe.wait_ge(k.copied.sem, k.copied.at(1) + e)
                    for t in range(T):
                        for f in range(T):
                            m = pe.matmul(k.ps[:, T + t, :], H1[:, f, t * P:(t + 1) * P], W[u][2][:, f, :],
                                          start=(f == 0), stop=(f == T - 1))
                        m.then_inc(k.tp.sem, 1)
                    mm_rows(pe, k, 0, H1, W[u][3], stop=False)
                    pe.wait_ge(k.ready.sem, k.ready.at(1) + e)
                    for t in range(T):
                        for s in range(T):
                            m = pe.matmul(k.ps[:, t, :], k.Cn[:, s, t * P:(t + 1) * P], PR[:, s, :],
                                          start=False, stop=(s == T - 1))
                        m.then_inc(k.out.sem, 1)
                walk(pe, step)

            @block.scalar
            def _(a):
                def step(e, u, j):
                    for t in range(T):
                        a.wait_ge(k.mm.sem, k.mm.at(t + 1) + e * T)
                        m = a.activation(H1[:, t, :], k.ps[:, t, :], ACT.Relu, bias=b0[u][:, t:t + 1])
                    m.then_inc(k.copied.sem, 1)
                walk(a, step)

            @block.vector
            def _(v):
                ch = Chain(v, k.dve_step)

                def step(e, u, j):
                    ch.n, ch.loop = 2 * T * u, j * (4 * T)
                    for t in range(T):
                        v.wait_ge(k.tp.sem, k.tp.at(t + 1) + e * T)
                        m = v.tensor_copy(PR[:, t, :], k.ps[:, T + t, :])
                    m.then_inc(k.ready.sem, 1)
                    for t in range(T):
                        v.wait_ge(k.out.sem, k.out.at(t + 1) + e * T)
                        ch.link(v.tensor_tensor(o[:, t, :], k.ps[:, t, :], b1[u][:], ALU.add))
                        ch.link(v.tensor_scalar(o[:, t, :], o[:, t, :], 0.0, wE[:, t, bass.ds(e, 1)],
                                                ALU.max, ALU.mult))
                        m = v.tensor_tensor(k.X[:, t, :], k.X[:, t, :], o[:, t, :], ALU.add)
                    m.then_inc(k.heads.sem, 1)
                    v.wait_ge(k.heads.sem, k.heads.at(1) + e)
                walk(v, step)
                ch.close(2 * T * E)
        done((k.heads, E), (k.slot[0], 48 * E), (k.slot[1], 48 * E), (k.mm, T * E), (k.copied, E), (k.ready, E),
             (k.tp, T * E), (k.out, T * E))



def program(nc, i, y):
    with ExitStack() as c:
        k = Kernel(nc, i)
        (k.loaded, k.mm, k.ready, k.copied, k.maxed, k.exped, k.probs, k.tp, k.av, k.heads, k.out, k.gathered,
         k.dve_step, k.pool_step) = [Ticker(c.enter_context(nc.semaphore(n))) for n in (
             "loaded", "mm", "ready", "copied", "maxed", "exped", "probs", "tp", "av", "heads", "out", "gathered",
             "dve_step", "pool_step")]
        k.slot = [Ticker(c.enter_context(nc.semaphore(f"slot{j}"))) for j in range(4)]
        k.pool_slot = [Ticker(c.enter_context(nc.semaphore(f"pool_slot{j}"))) for j in range(4)]
        k.pool_stored = [Ticker(c.enter_context(nc.semaphore(f"pool_stored{j}"))) for j in range(2)]
        k.turned = [Ticker(c.enter_context(nc.semaphore(f"turned{j}"))) for j in range(2)]
        k.stored = [Ticker(c.enter_context(nc.semaphore(f"stored{j}"))) for j in range(2)]
        k.ps = c.enter_context(nc.psum_tensor("ps", [P, 8, 512], F32))
        k.psb = k.ps[:].bitcast(BF16)
        k.X, k.N, k.NT, k.Cn = [sb(c, k, n, [P, T, D]) for n in ("X", "N", "NT", "Cn")]
        k.ident, k.ones, k.before = [sb(c, k, n, [P, P]) for n in ("ident", "ones", "before")]
        k.identb = sb(c, k, "identb", [P, P], BF16)
        k.zrow, k.ramp_f = sb(c, k, "zrow", [P, N]), sb(c, k, "ramp_f", [P, N])
        k.ramp, k.ramp_i = sb(c, k, "ramp", [P, N], F16), sb(c, k, "ramp_i", [P, N], I32)
        k.node_i, k.node_f = sb(c, k, "node_i", [P, T], I32), sb(c, k, "node_f", [P, T])
        k.src_i, k.dst_i = sb(c, k, "src_i", [P, EA], I32), sb(c, k, "dst_i", [P, EA], I32)
        k.src_f, k.dst_f = sb(c, k, "src_f", [P, EA]), sb(c, k, "dst_f", [P, EA])
        k.ea = sb(c, k, "ea", [P, EA, 2])
        k.inv_deg, k.has_out = sb(c, k, "inv_deg", [P, T]), sb(c, k, "has_out", [P, T])
        k.eps = sb(c, k, "eps", [P, 1])
        G0, G3 = (N + EXPERTS * (P - 1)) // P, (2 * N + EXPERTS * (P - 1)) // P
        k.xl_d, k.xr_d = [nc.dram_tensor(n, (N, D + 1), F32).ap() for n in ("xl_d", "xr_d")]
        k.rows_d = nc.dram_tensor("rows_d", (N, D), F32).ap()
        k.at_d, k.val_d = nc.dram_tensor("at_d", (N,), I32).ap(), nc.dram_tensor("val_d", (N,), F32).ap()
        spread, result = [nc.dram_tensor(n, (G3 * P, D), F32).ap() for n in ("spread_d", "result_d")]

        with ExitStack() as c0:
            k.C, k.no_edge = [sb(c0, k, n, [P, T, D]) for n in ("C", "no_edge")]
            constants(k)
            adjacency(k)

            layernorm(k, k.X, k.N, k.NT)
            attention(k, dict(Wq=i["L0_gnn_Wq"], Wk=i["L0_gnn_Wk"], Wv=i["L0_gnn_Wv"], Wo=i["L0_gnn_Wo"], bq=i["g_bq"],
                                         bk=i["g_bk"], bv=i["L0_gnn_bv"], bo=i["L0_gnn_bo"]), k.no_edge, k.X, k.X)
        layernorm(k, k.X, k.N, k.NT)
        with ExitStack() as c1:
            O = sb(c1, k, "O", [P, T, D])
            attention(k, dict(Wq=i["L0_ffn_Wq"], Wk=i["L0_ffn_Wk"], Wv=i["L0_ffn_Wv"], Wo=i["L0_ffn_Wo"], bq=i["f_bq"],
                                         bk=i["f_bk"], bv=i["L0_ffn_bv"], bo=i["L0_ffn_bo"]), None, k.N, O)
            with ExitStack() as c2:
                gb = [sb(c2, k, "gb", [P, D]) for _ in range(2)]
                load(k, ((gb[0][:], bcast(i["L0_ffn_ln1_g"])), (gb[1][:], bcast(i["L0_ffn_ln1_b"]))))
                layernorm(k, O, k.N, k.NT, passes=(gb,))
        routed_ffn(k, k.NT, k.N, i["L0_ffn_gate_W"], i["L0_ffn_gate_b"], "top1", 1, G0,
                   dict(W1=i["L0_ffn_W1"], W2=i["L0_ffn_W2"], b1=i["l0b1"], b2=i["L0_ffn_b2"]),
                   2048, False, spread, result)

        layernorm(k, k.X, k.N, k.NT)
        gat(k)
        layernorm(k, k.X, k.N, k.NT)
        positional_ffn(k)

        layernorm(k, k.X, k.N, k.NT)
        graph_conv(k)
        layernorm(k, k.X, k.N, k.NT)
        expert_choice_ffn(k)

        layernorm(k, k.X, k.N, k.NT)
        sage(k)
        layernorm(k, k.X, k.N, k.NT)
        routed_ffn(k, k.NT, k.N, i["router_wT"], None, "top2", 2, G3,
                   dict(Wg=i["L3_ffn_w_gate"], Wu=i["L3_ffn_w_up"], Wd=i["L3_ffn_w_down"]), 1024, True,
                   spread, result)
        store(k, y)


def store(k, y):
    with k.nc.Block() as block:
        @block.sync
        def _(sp):
            sp.dma_start(rows_of(y), k.X[:]).then_inc(k.stored[0].sem, 16)
            sp.wait_ge(k.stored[0].sem, k.stored[0].at(16))



def kernel(**inputs):
    import concourse.bacc as bacc
    from concourse.bass_utils import run_bass_kernel_spmd

    given = {n: np.asarray(a) for n, a in inputs.items()}

    def columns(v, tiles):
        return np.ascontiguousarray(np.swapaxes(v.reshape(*v.shape[:-1], tiles, P), -1, -2))

    def turned(w):
        return np.ascontiguousarray(np.swapaxes(w, -1, -2))

    laid = {
        "g_bq": columns(given["L0_gnn_bq"], T), "g_bk": columns(given["L0_gnn_bk"], T),
        "f_bq": columns(given["L0_ffn_bq"], T), "f_bk": columns(given["L0_ffn_bk"], T),
        "l0b1": columns(given["L0_ffn_b1"], 16), "attn_b": columns(given["L1_ffn_attn_b"], T),
        "attn_wT": turned(given["L1_ffn_attn_w"]), "next_wT": turned(given["L1_ffn_next_w"]),
        "fc1T": turned(given["L1_ffn_fc1_w"]), "fc2T": turned(given["L1_ffn_fc2_w"]),
        "fc1_b": columns(given["L1_ffn_fc1_b"], 16), "fc2_b": columns(given["L1_ffn_fc2_b"], T),
        "l2b1": columns(given["L2_ffn_b1"], 2), "l2b2": columns(given["L2_ffn_b2"], T),
        "sb1": columns(given["L2_ffn_sb1"], 2),
        "sage_b0": columns(given["L3_gnn_bl"][:, 0], T), "sage_b1": np.ascontiguousarray(given["L3_gnn_bl"][:, 1]),
        "router_wT": turned(given["L3_ffn_router_w"]),
        "dst_row": np.ascontiguousarray(given["dst"].reshape(P, ET).T).reshape(-1),
    }
    unused = {"L0_gnn_bq", "L0_gnn_bk", "L0_ffn_bq", "L0_ffn_bk", "L0_ffn_b1", "L1_ffn_attn_b", "L1_ffn_attn_w",
              "L1_ffn_next_w", "L1_ffn_fc1_w", "L1_ffn_fc2_w", "L1_ffn_fc1_b", "L1_ffn_fc2_b", "L2_ffn_b1",
              "L2_ffn_b2", "L2_ffn_sb1", "L3_gnn_bl", "L3_ffn_router_w", "L1_ffn_gate_w"}
    laid.update({n: np.ascontiguousarray(a) for n, a in given.items() if n not in unused})
    nc = bacc.Bacc("TRN2", target_bir_lowering=False, num_devices=1)
    i = {n: nc.dram_tensor(n, a.shape, mybir.dt.from_np(a.dtype), kind="ExternalInput").ap()
         for n, a in laid.items()}
    y = nc.dram_tensor("y", (N, D), F32, kind="ExternalOutput").ap()
    program(nc, i, y)
    return run_bass_kernel_spmd(nc, [laid], core_ids=[0]).results[0]["y"]
```

```python
from contextlib import ExitStack

import concourse.bass as bass
import numpy as np
from concourse import mybir

F32 = mybir.dt.float32
F16 = mybir.dt.float16
BF16 = mybir.dt.bfloat16
I32 = mybir.dt.int32
U32 = mybir.dt.uint32
ALU = mybir.AluOpType
ACT = mybir.ActivationFunctionType
AX = mybir.AxisListType

P = 128
N = 512
D = 512
T = N // P
EDGES = 8704
ET = EDGES // P
EB = ET + T
EA = EB + T
WORDS = 8
HEADS = 8
HD = D // HEADS
EXPERTS = 8
NEG = -1e30
EPS = 1e-5
EX_SCALE = 16384.0


class Ticker:

    def __init__(self, sem):
        self.sem, self.base = sem, 0

    def at(self, n):
        return self.base + n


class Kernel:

    def __init__(self, nc, inputs):
        self.nc, self.i, self.uid = nc, inputs, 0


class Chain:

    def __init__(self, eng, ticker):
        self.eng, self.t, self.n, self.loop = eng, ticker, 0, 0

    def link(self, ins):
        self.n += 1
        ins.then_inc(self.t.sem, 1)
        self.eng.wait_ge(self.t.sem, self.t.at(self.n) + self.loop)

    def close(self, total=None):
        self.t.base += self.n if total is None else total


def later(step, first):
    return not isinstance(step, int) or step >= first


def rows_of(w):
    return w.rearrange("(k p) n -> p k n", p=P)


def bcast(v, n=P):
    return v.rearrange("(a d) -> a d", a=1).to_broadcast([n, v.shape[0]])


def sb(c, k, name, shape, dt=F32):
    k.uid += 1
    return c.enter_context(k.nc.sbuf_tensor(f"{name}_{k.uid}", shape, dt))


def done(*pairs):
    for ticker, n in pairs:
        ticker.base += n



def constants(k):
    with k.nc.Block() as block:
        @block.gpsimd
        def _(gp):
            ch = Chain(gp, k.pool_step)
            gp.memset(k.ident[:], 0.0)
            gp.memset(k.ones[:], 1.0)
            gp.memset(k.eps[:], EPS)
            ch.link(gp.memset(k.zrow[:], 0.0))
            gp.affine_select(out=k.ident[:], in_=k.ident[:], compare_op=ALU.not_equal, fill=1.0,
                             base=0, pattern=[[-1, P]], channel_multiplier=1)
            gp.affine_select(out=k.before[:], in_=k.ones[:], compare_op=ALU.is_gt, fill=0.0,
                             base=0, pattern=[[1, P]], channel_multiplier=-1)
            gp.iota(k.ramp_i[:], pattern=[[1, N]], base=0, channel_multiplier=0)
            ch.link(gp.iota(k.node_i[:], pattern=[[P, T]], base=0, channel_multiplier=1))
            ch.close()

        @block.sync
        def _(sp):
            sp.dma_start(k.X[:], rows_of(k.i["x"])).then_inc(k.loaded.sem, 16)
            sp.wait_ge(k.loaded.sem, k.loaded.at(16))
    done((k.loaded, 16))
    with k.nc.Block() as block:
        @block.vector
        def _(v):
            v.tensor_copy(k.ramp_f[:], k.ramp_i[:])
            v.tensor_copy(k.ramp[:], k.ramp_i[:])
            v.tensor_copy(k.node_f[:], k.node_i[:])
            v.tensor_copy(k.identb[:], k.ident[:])
            v.memset(k.zero16[:], 0.0)


def edge_slots(k, c0):
    nc = k.nc
    k.drawn_src, k.drawn_dst = sb(c0, k, "drawn_src", [P, ET]), sb(c0, k, "drawn_dst", [P, ET])
    k.drawn_ea = ea = sb(c0, k, "drawn_ea", [P, ET, 2])
    k.slots = slot = sb(c0, k, "slots", [P, ET], I32)
    k.payload = pay = sb(c0, k, "payload", [P, ET, WORDS])
    with ExitStack() as c:
        src_i, dst_i = sb(c, k, "src_r", [P, ET], I32), sb(c, k, "dst_r", [P, ET], I32)
        ew = sb(c, k, "ew_r", [P, ET])
        dst = sb(c, k, "dst", [P, ET])
        ge = sb(c, k, "ge", [P, T + 1, ET])
        m, rank = sb(c, k, "m", [P, T, ET]), sb(c, k, "rank", [P, T, ET])
        tot, off, n_b, tiles, end = [sb(c, k, n, [P, T]) for n in ("tot", "off", "n_b", "tiles", "end")]
        junk, starts = sb(c, k, "junk", [P, ET]), sb(c, k, "starts", [P, ET])
        slot_f = sb(c, k, "slot_f", [P, ET])
        own = sb(c, k, "own", [P, EA])
        zero = sb(c, k, "zero", [P, EB * WORDS])
        with nc.Block() as block:
            @block.sync
            def _(sp):
                for to, frm in ((src_i[:], k.i["src"].rearrange("(p j) -> p j", p=P)),
                                (dst_i[:], k.i["dst"].rearrange("(p j) -> p j", p=P)),
                                (ea[:], k.i["edge_attr_2"].rearrange("(p j) c -> p j c", p=P)),
                                (ew[:], k.i["edge_weight"].rearrange("(p j) -> p j", p=P))):
                    sp.dma_start(to, frm).then_inc(k.loaded.sem, 16)
                sp.wait_ge(k.ready.sem, k.ready.at(1))
                sp.dma_start(k.edges_d.rearrange("(p j) c -> p (j c)", p=P), zero[:]).then_inc(k.stored[0].sem, 16)
                sp.wait_ge(k.stored[0].sem, k.stored[0].at(16))

            @block.tensor
            def _(pe):
                pe.wait_ge(k.ready.sem, k.ready.at(2))
                pe.matmul(k.ps[:, 0, 0:T], k.before[:], tot[:], start=True, stop=True)
                pe.matmul(k.ps[:, 1, 0:T], k.ones[:], tot[:], start=True, stop=True).then_inc(k.mm.sem, 1)

            @block.vector
            def _(v):
                ch = Chain(v, k.dve_step)
                v.memset(zero[:], 0.0).then_inc(k.ready.sem, 1)
                v.memset(pay[:], 0.0)
                ch.link(v.tensor_scalar(starts[:], k.ramp_f[:, 0:ET], float(P), None, ALU.mult))
                v.wait_ge(k.loaded.sem, k.loaded.at(64))
                v.tensor_copy(k.drawn_src[:], src_i[:])
                v.tensor_copy(k.drawn_dst[:], dst_i[:])
                ch.link(v.tensor_copy(dst[:], dst_i[:]))
                for b in range(T + 1):
                    last = v.tensor_scalar(ge[:, b, :], dst[:], float(P * b), None, ALU.is_ge)
                ch.link(last)
                ch.link(v.tensor_tensor(m[:], ge[:, 0:T, :], ge[:, 1:T + 1, :], ALU.subtract))
                v.tensor_reduce(tot[:], m[:], AX.X, ALU.add).then_inc(k.ready.sem, 1)
                for b in range(T):
                    last = v.tensor_tensor_scan(rank[:, b, :], k.ones[:, 0:ET], m[:, b, :], 0.0, ALU.mult, ALU.add)
                ch.link(last)
                v.wait_ge(k.mm.sem, k.mm.at(1))
                v.tensor_copy(off[:], k.ps[:, 0, 0:T])
                ch.link(v.tensor_copy(n_b[:], k.ps[:, 1, 0:T]))
                for b in range(T):
                    last = v.tensor_scalar(junk[:], starts[:], n_b[:, b:b + 1], None, ALU.is_lt, ALU.add,
                                           accum_out=tiles[:, b:b + 1])
                    ch.link(last)
                ch.link(v.tensor_tensor_scan(end[:], k.ones[:, 0:T], tiles[:], 0.0, ALU.mult, ALU.add))
                ch.link(v.tensor_tensor(tiles[:], end[:], tiles[:], ALU.subtract))
                ch.link(v.scalar_tensor_tensor(off[:], tiles[:], float(P), off[:], ALU.mult, ALU.add))
                ch.link(v.tensor_tensor(rank[:], rank[:], m[:], ALU.subtract))
                for b in range(T):
                    ch.link(v.scalar_tensor_tensor(rank[:, b, :], rank[:, b, :], off[:, b:b + 1], m[:, b, :],
                                                   ALU.add, ALU.mult))
                ch.link(v.tensor_tensor(slot_f[:], rank[:, 0, :], rank[:, 1, :], ALU.add))
                ch.link(v.tensor_tensor(slot_f[:], slot_f[:], rank[:, 2, :], ALU.add))
                ch.link(v.tensor_tensor(slot_f[:], slot_f[:], rank[:, 3, :], ALU.add))
                ch.link(v.tensor_copy(slot[:], slot_f[:]))
                ch.link(v.tensor_scalar(dst[:], dst[:], 1.0, None, ALU.add))
                for b in range(1, T):
                    ch.link(v.scalar_tensor_tensor(dst[:], ge[:, b, :], -float(P), dst[:], ALU.mult, ALU.add))
                v.tensor_copy(pay[:, :, 0], src_i[:])
                v.tensor_copy(pay[:, :, 1], dst[:])
                v.tensor_copy(pay[:, :, 2:4], ea[:])
                v.tensor_copy(pay[:, :, 4], ew[:])
                ch.link(v.memset(own[:], 0.0))
                for b in range(T - 1):
                    ch.link(v.scalar_tensor_tensor(own[:, 0:EB], k.ramp_f[:, 0:EB], end[:, b:b + 1], own[:, 0:EB],
                                                   ALU.is_ge, ALU.add))
                ch.link(v.tensor_copy(own[:, EB:EA], k.ramp_f[:, 0:T]))
                v.tensor_copy(k.own[:], own[:])
                v.tensor_copy(k.src_f[:, EB:EA], k.node_f[:])
                for t in range(T):
                    v.tensor_copy(k.dst_f[:, EB + t:EB + t + 1], k.node_f[:, 0:1])
                ch.close()
        done((k.loaded, 64), (k.stored[0], 16), (k.ready, 2), (k.mm, 1))


def split3(v, ch, parts, value, rest):
    ch.link(v.tensor_copy(parts[0], value))
    ch.link(v.tensor_tensor(rest, value, parts[0], ALU.subtract))
    ch.link(v.tensor_copy(parts[1], rest))
    ch.link(v.tensor_tensor(rest, rest, parts[1], ALU.subtract))
    ch.link(v.tensor_copy(parts[2], rest))


def clear_banks(pe, k, banks):
    for b in banks:
        m = pe.matmul(k.ps[:, b, :], k.zero16[:, 0:P], k.zero16[:], start=True, stop=True)
    return m


def dst_tiles(eng, k, i):
    return k.nc.values_load_multi_w_load_instructions(
        k.own[0:1, bass.ds(i, 4)], engines=(eng.engine,), min_val=0, max_val=T - 1,
        skip_runtime_bounds_check_because="a sum of three comparisons, and 0..3 for the self loops")[1]


def adjacency(k):
    nc = k.nc
    with ExitStack() as c:
        parts = sb(c, k, "parts", [P, ET, 7], BF16)
        rest = sb(c, k, "rest", [P, ET, 2])
        oh_s = [sb(c, k, "oh_s", [P, N], BF16) for _ in range(2)]
        oh_d = [sb(c, k, "oh_d", [P, N], BF16) for _ in range(2)]
        sums = sb(c, k, "sums", [P, T, 7])
        inv = sb(c, k, "inv", [P, T])
        diag = sb(c, k, "diag", [P, T, P])
        back = sb(c, k, "back", [P, EB, WORDS])
        with nc.Block() as block:
            @block.gpsimd
            def _(gp):
                for j in range(ET):
                    gp.indirect_dma_start(k.edges_d,
                                          bass.IndirectOffsetOnAxis(ap=k.slots[:, j:j + 1].bitcast(U32), axis=0),
                                          k.payload[:, j, :], None).then_inc(k.gathered.sem, 16)

            @block.vector
            def _(v):
                ch = Chain(v, k.dve_step)
                v.memset(parts[:, :, 6:7], 1.0)
                split3(v, ch, [parts[:, :, 2 * j:2 * j + 2] for j in range(3)], k.drawn_ea[:], rest[:])
                ch.close()

                def step(i, u):
                    if later(i, 2):
                        v.wait_ge(k.mm.sem, k.mm.at(i - 1))
                    v.tensor_scalar(oh_s[u][:], k.ramp[:], k.drawn_src[:, bass.ds(i, 1)], None, ALU.is_equal)
                    v.tensor_scalar(oh_d[u][:], k.ramp[:], k.drawn_dst[:, bass.ds(i, 1)], None,
                                    ALU.is_equal).then_inc(k.ready.sem, 1)
                for u in range(2):
                    step(u, u)
                with v.Fori(1, ET // 2) as j:
                    for u in range(2):
                        step(j * 2 + u, u)

            @block.tensor
            def _(pe):
                def step(i, u, first=False, last=False):
                    pe.wait_ge(k.ready.sem, k.ready.at(i + 1))
                    for t in range(T):
                        pe.matmul(k.ps[:, t, :], oh_s[u][:, t * P:(t + 1) * P], oh_d[u][:],
                                  start=first, stop=last)
                    for t in range(T):
                        m = pe.matmul(k.ps[:, T + t, 0:7], oh_d[u][:, t * P:(t + 1) * P],
                                      parts[:, bass.ds(i, 1), :].rearrange("p a c -> p (a c)"),
                                      start=first, stop=last)
                    m.then_inc(k.mm.sem, 1)
                step(0, 0, first=True)
                step(1, 1)
                with pe.Fori(1, ET // 2 - 1) as j:
                    for u in range(2):
                        step(j * 2 + u, u)
                step(ET - 2, 0)
                step(ET - 1, 1, last=True)
        done((k.mm, ET), (k.ready, ET))
        with nc.Block() as block:
            @block.sync
            def _(sp):
                sp.wait_ge(k.gathered.sem, k.gathered.at(16 * ET))
                sp.dma_start(back[:], k.edges_d.rearrange("(j p) c -> p j c", p=P)).then_inc(k.loaded.sem, 16)

            @block.scalar
            def _(a):
                for t in range(T):
                    a.activation(k.C[:, t, :], k.ps[:, t, :], ACT.Copy).then_inc(k.copied.sem, 1)

            @block.vector
            def _(v):
                ch = Chain(v, k.dve_step)
                for t in range(T):
                    last = v.tensor_copy(sums[:, t, :], k.ps[:, T + t, 0:7])
                ch.link(last)
                v.tensor_scalar(k.inv_deg[:], sums[:, :, 6], 1.0, None, ALU.min)
                ch.link(v.tensor_scalar(inv[:], sums[:, :, 6], 1.0, None, ALU.max))
                ch.link(v.reciprocal(inv[:], inv[:]))
                ch.link(v.tensor_tensor(k.inv_deg[:], k.inv_deg[:], inv[:], ALU.mult))
                mean = k.ea[:, EB:EA, :]
                ch.link(v.tensor_tensor(mean, sums[:, :, 0:2], sums[:, :, 2:4], ALU.add))
                ch.link(v.tensor_tensor(mean, mean, sums[:, :, 4:6], ALU.add))
                for t in range(T):
                    v.tensor_scalar(k.ea[:, EB + t, :], k.ea[:, EB + t, :], inv[:, t:t + 1], None, ALU.mult)
                for t in range(T):
                    last = v.tensor_scalar(diag[:, t, :], k.ident[:], k.inv_deg[:, t:t + 1], None, ALU.mult)
                last.then_inc(k.ready.sem, 1)
                v.wait_ge(k.mm.sem, k.mm.at(1))
                v.wait_ge(k.copied.sem, k.copied.at(T))
                for t in range(T):
                    v.tensor_tensor(k.Cn[:, t, :], k.C[:, t, :], k.ps[:, T, :], ALU.mult)
                    v.tensor_scalar(k.no_edge[:, t, :], k.C[:, t, :], 0.0, NEG, ALU.is_equal, ALU.mult)
                ch.link(v.tensor_reduce(k.has_out[:], k.C[:], AX.X, ALU.max))
                ch.link(v.tensor_scalar(k.has_out[:], k.has_out[:], 0.0, None, ALU.is_gt))
                v.wait_ge(k.loaded.sem, k.loaded.at(16))
                v.tensor_copy(k.src_f[:, 0:EB], back[:, :, 0])
                v.tensor_scalar(k.dst_f[:, 0:EB], back[:, :, 1], -1.0, None, ALU.add)
                v.tensor_copy(k.ea[:, 0:EB, :], back[:, :, 2:4])
                ch.link(v.tensor_copy(k.ew[:], back[:, :, 4]))
                ch.link(v.tensor_copy(k.src_i[:], k.src_f[:]))
                ch.close()

            @block.tensor
            def _(pe):
                pe.wait_ge(k.ready.sem, k.ready.at(1))
                for t in range(T):
                    m = pe.matmul(k.ps[:, T, t * P:(t + 1) * P], k.ones[:], diag[:, t, :], start=True, stop=True)
                m.then_inc(k.mm.sem, 1)
        done((k.mm, 1), (k.ready, 1), (k.copied, T), (k.loaded, 16), (k.gathered, 16 * ET))



def layernorm(k, src, rows, cols, passes=(None,), relu=False):
    nc, np_ = k.nc, len(passes)
    with ExitStack() as c:
        stats = sb(c, k, "stats", [P, T, 6])
        mv = sb(c, k, "mv", [P, T, 2])
        rstd = sb(c, k, "rstd", [P, T])
        rows_step = []
        with nc.Block() as block:
            @block.vector
            def _(v):
                ch = Chain(v, k.dve_step)
                for j, gb in enumerate(passes):
                    x = src if j == 0 else rows
                    for t in range(T):
                        last = v.bn_stats(stats[:, t, :], x[:, t, :])
                    ch.link(last)
                    for t in range(T):
                        last = v.bn_aggr(mv[:, t, :], stats[:, t, :])
                    last.then_inc(k.ready.sem, 1)
                    v.wait_ge(k.copied.sem, k.copied.at(j + 1))
                    ch.link(v.reciprocal(rstd[:], rstd[:]))
                    for t in range(T):
                        last = v.tensor_scalar(rows[:, t, :], x[:, t, :], mv[:, t, 0:1], rstd[:, t:t + 1],
                                               ALU.subtract, ALU.mult)
                    ch.link(last)
                    if gb:
                        for op, w in ((ALU.mult, gb[0]), (ALU.add, gb[1])):
                            for t in range(T):
                                last = v.tensor_tensor(rows[:, t, :], rows[:, t, :], w[:], op)
                            ch.link(last)
                if relu:
                    ch.link(v.tensor_scalar(rows[:], rows[:], 0.0, None, ALU.max))
                rows_step.append(k.dve_step.at(ch.n))
                for f in (1, 3):
                    v.wait_ge(k.mm.sem, k.mm.at(f + 1))
                    v.tensor_copy(cols[:, f, :], k.ps[:, f, :])
                ch.close()

            @block.scalar
            def _(a):
                for j in range(np_):
                    a.wait_ge(k.ready.sem, k.ready.at(j + 1))
                    a.activation(rstd[:], mv[:, :, 1], ACT.Sqrt, bias=k.eps[:, 0:1]).then_inc(k.copied.sem, 1)
                for f in (0, 2):
                    a.wait_ge(k.mm.sem, k.mm.at(f + 1))
                    a.activation(cols[:, f, :], k.ps[:, f, :], ACT.Copy)

            @block.tensor
            def _(pe):
                pe.wait_ge(k.dve_step.sem, rows_step[0])
                for f in range(T):
                    for t in range(T):
                        m = pe.transpose(k.ps[:, f, t * P:(t + 1) * P], rows[:, t, f * P:(f + 1) * P], k.ident[:])
                    m.then_inc(k.mm.sem, 1)
        done((k.ready, np_), (k.copied, np_), (k.mm, T))


def mm_rows(pe, k, bank, cols, w, start=True, stop=True):
    for t in range(T):
        for f in range(T):
            m = pe.matmul(k.ps[:, bank + t, :], cols[:, f, t * P:(t + 1) * P], w[:, f, :],
                          start=start and f == 0, stop=stop and f == T - 1)
    return m


def mm_cols(pe, k, bank, w, cols, start=True, stop=True):
    for t in range(T):
        for f in range(T):
            m = pe.matmul(k.ps[:, bank + t, :], w[:, f, t * P:(t + 1) * P], cols[:, f, :],
                          start=start and f == 0, stop=stop and f == T - 1)
    return m



def attention(k, w, mask, base, out):
    nc = k.nc
    with ExitStack() as c:
        W = [sb(c, k, f"w{j}", [P, T, D]) for j in range(4)]
        QT, KT, V, OT = [sb(c, k, n, [P, T, D]) for n in ("qt", "kt", "v", "ot")]
        bq, bk = sb(c, k, "bq", [P, T]), sb(c, k, "bk", [P, T])
        bv, bo = sb(c, k, "bv", [P, D]), sb(c, k, "bo", [P, D])
        E = [sb(c, k, "e", [P, T, N]) for _ in range(2)]
        PT = sb(c, k, "pt", [P, T, N])
        mx, den = sb(c, k, "mx", [P, 2, T]), sb(c, k, "den", [P, 2, T])
        with nc.Block() as block:
            @block.sync
            def _(sp):
                for dst, src in ((bq[:], w["bq"]), (bk[:], w["bk"]), (bv[:], bcast(w["bv"])), (bo[:], bcast(w["bo"]))):
                    sp.dma_start(dst, src).then_inc(k.loaded.sem, 16)
                for j, m in enumerate((w["Wq"], w["Wk"], w["Wv"], w["Wo"])):
                    sp.dma_start(W[j][:], rows_of(m)).then_inc(k.slot[j].sem, 16)

            @block.tensor
            def _(pe):
                pe.wait_ge(k.slot[0].sem, k.slot[0].at(16))
                mm_cols(pe, k, 0, W[0], k.NT).then_inc(k.mm.sem, 1)
                pe.wait_ge(k.slot[1].sem, k.slot[1].at(16))
                mm_cols(pe, k, 4, W[1], k.NT).then_inc(k.mm.sem, 1)
                pe.wait_ge(k.slot[2].sem, k.slot[2].at(16))
                pe.wait_ge(k.copied.sem, k.copied.at(1))
                mm_rows(pe, k, 0, k.NT, W[2]).then_inc(k.mm.sem, 1)

            @block.vector
            def _(v):
                v.wait_ge(k.loaded.sem, k.loaded.at(64))
                v.wait_ge(k.mm.sem, k.mm.at(1))
                for t in range(T):
                    m = v.tensor_scalar(QT[:, t, :], k.ps[:, t, :], bq[:, t:t + 1], HD ** -0.5, ALU.add, ALU.mult)
                m.then_inc(k.copied.sem, 1)
                for t in range(T):
                    v.tensor_tensor(out[:, t, :], base[:, t, :], bo[:], ALU.add)
                v.wait_ge(k.mm.sem, k.mm.at(3))
                for t in range(T):
                    v.tensor_tensor(V[:, t, :], k.ps[:, t, :], bv[:], ALU.add)

            @block.scalar
            def _(a):
                a.wait_ge(k.loaded.sem, k.loaded.at(64))
                a.wait_ge(k.mm.sem, k.mm.at(2))
                for t in range(T):
                    a.activation(KT[:, t, :], k.ps[:, T + t, :], ACT.Identity, bias=bk[:, t:t + 1])
        done((k.loaded, 64), (k.mm, 3), (k.copied, 1), (k.slot[0], 16), (k.slot[1], 16), (k.slot[2], 16))

        with nc.Block() as block:
            @block.tensor
            def _(pe):
                def scores(h):
                    lo, f = (h % 2) * HD, h // 2
                    for t in range(T):
                        if h:
                            pe.wait_ge(k.ready.sem, k.ready.at(T * (h - 1) + t + 1))
                        pe.matmul(k.ps[:, t, :], QT[lo:lo + HD, f, t * P:(t + 1) * P], KT[lo:lo + HD, f, :],
                                  start=True, stop=True).then_inc(k.mm.sem, 1)

                def weigh(h):
                    lo, f = (h % 2) * HD, h // 2
                    pe.wait_ge(k.probs.sem, k.probs.at(h + 1))
                    for m in range(T):
                        if h or m >= 2:
                            n = T * h + m - 2
                            q = k.turned[m % 2]
                            pe.wait_ge(q.sem, q.at(n // 2 + 1))
                        for t in range(T):
                            i = pe.transpose(k.ps[:, 4 + m % 2, t * P:(t + 1) * P],
                                             E[h % 2][:, t, m * P:(m + 1) * P], k.ident[:])
                        i.then_inc(k.tp.sem, 1)
                    if h % 2 == 0 and h >= 4:
                        pe.wait_ge(k.heads.sem, k.heads.at(h // 2 - 1))
                    for m in range(T):
                        q = k.turned[m % 2]
                        pe.wait_ge(q.sem, q.at(2 * h + m // 2 + 1))
                        i = pe.matmul(k.ps[lo:lo + HD, 6 + f % 2, :], V[:, m, h * HD:(h + 1) * HD], PT[:, m, :],
                                      start=(m == 0), stop=(m == T - 1))
                    i.then_inc(k.av.sem, 1)
                scores(0)
                for h in range(HEADS):
                    if h + 1 < HEADS:
                        scores(h + 1)
                    weigh(h)
                pe.wait_ge(k.slot[3].sem, k.slot[3].at(16))
                pe.wait_ge(k.heads.sem, k.heads.at(HEADS // 2))
                mm_rows(pe, k, 0, OT, W[3]).then_inc(k.mm.sem, 1)

            @block.vector
            def _(v):
                ch = Chain(v, k.dve_step)

                def maxima(h):
                    s = h % 2
                    if h >= 2:
                        v.wait_ge(k.tp.sem, k.tp.at(T * (h - 1)))
                    for t in range(T):
                        v.wait_ge(k.mm.sem, k.mm.at(T * h + t + 1))
                        last = v.tensor_tensor_reduce(E[s][:, t, :], k.ps[:, t, :],
                                                      mask[:, t, :] if mask is not None else k.zrow[:],
                                                      1.0, -3e38, ALU.add, ALU.max, mx[:, s, t:t + 1])
                        last.then_inc(k.ready.sem, 1)
                    v.wait_ge(k.ready.sem, k.ready.at(T * (h + 1)))
                    v.tensor_scalar(mx[:, s, :], mx[:, s, :], -1.0, None, ALU.mult).then_inc(k.maxed.sem, 1)

                def norm(h):
                    s = h % 2
                    v.wait_ge(k.exped.sem, k.exped.at(h + 1))
                    ch.link(v.reciprocal(den[:, s, :], den[:, s, :]))
                    if mask is not None:
                        ch.link(v.tensor_tensor(den[:, s, :], den[:, s, :], k.has_out[:], ALU.mult))
                    for t in range(T):
                        last = v.tensor_scalar(E[s][:, t, :], E[s][:, t, :], den[:, s, t:t + 1], None, ALU.mult)
                    last.then_inc(k.probs.sem, 1)
                    for m in (1, 3):
                        v.wait_ge(k.tp.sem, k.tp.at(T * h + m + 1))
                        if h:
                            v.wait_ge(k.av.sem, k.av.at(h))
                        v.tensor_copy(PT[:, m, :], k.ps[:, 5, :]).then_inc(k.turned[1].sem, 1)
                maxima(0)
                for h in range(HEADS):
                    if h + 1 < HEADS:
                        maxima(h + 1)
                    norm(h)
                v.wait_ge(k.mm.sem, k.mm.at(T * HEADS + 1))
                for t in range(T):
                    v.tensor_tensor(out[:, t, :], out[:, t, :], k.ps[:, t, :], ALU.add)
                ch.close()

            @block.scalar
            def _(a):
                for h in range(HEADS):
                    s = h % 2
                    a.wait_ge(k.maxed.sem, k.maxed.at(h + 1))
                    for t in range(T):
                        i = a.activation(E[s][:, t, :], E[s][:, t, :], ACT.Exp, bias=mx[:, s, t:t + 1],
                                         accum_out=den[:, s, t:t + 1])
                    i.then_inc(k.exped.sem, 1)
                    for m in (0, 2):
                        a.wait_ge(k.tp.sem, k.tp.at(T * h + m + 1))
                        if h:
                            a.wait_ge(k.av.sem, k.av.at(h))
                        a.activation(PT[:, m, :], k.ps[:, 4, :], ACT.Copy).then_inc(k.turned[0].sem, 1)
                    if h % 2:
                        a.wait_ge(k.av.sem, k.av.at(h + 1))
                        a.activation(OT[:, h // 2, :], k.ps[:, 6 + (h // 2) % 2, :],
                                     ACT.Copy).then_inc(k.heads.sem, 1)
        done((k.mm, T * HEADS + 1), (k.ready, T * HEADS), (k.maxed, HEADS), (k.exped, HEADS), (k.probs, HEADS),
             (k.tp, T * HEADS), (k.turned[0], 2 * HEADS), (k.turned[1], 2 * HEADS), (k.av, HEADS),
             (k.heads, HEADS // 2), (k.slot[3], 16))



def routing(k, c, cols, gate, bias, width, how, choices):
    nc = k.nc
    g = sb(c, k, "gate", [P, T, width])
    gb = sb(c, k, "gate_b", [P, width])
    lg = sb(c, k, "lg", [P, T, 8])
    mx = sb(c, k, "lmx", [P, T])
    sm = sb(c, k, "lsm", [P, T])
    top = sb(c, k, "top", [P, T, 8])
    at = sb(c, k, "at", [P, T, 8], U32)
    atf = sb(c, k, "atf", [P, T, 8])
    masks = sb(c, k, "masks", [P, T, choices, 8])
    wt = sb(c, k, "wt", [P, T, choices])
    with nc.Block() as block:
        @block.sync
        def _(sp):
            sp.dma_start(g[:], rows_of(gate)).then_inc(k.loaded.sem, 16)
            if bias is not None:
                sp.dma_start(gb[:], bcast(bias)).then_inc(k.loaded.sem, 16)

        @block.tensor
        def _(pe):
            pe.wait_ge(k.loaded.sem, k.loaded.at(32 if bias is not None else 16))
            for t in range(T):
                for f in range(T):
                    m = pe.matmul(k.ps[:, t, 0:width], cols[:, f, t * P:(t + 1) * P], g[:, f, :],
                                  start=(f == 0), stop=(f == T - 1))
            m.then_inc(k.mm.sem, 1)

        @block.vector
        def _(v):
            ch = Chain(v, k.dve_step)
            if width < 8:
                ch.link(v.memset(lg[:], NEG))
            v.wait_ge(k.mm.sem, k.mm.at(1))
            for t in range(T):
                if bias is not None:
                    last = v.tensor_tensor(lg[:, t, 0:width], k.ps[:, t, 0:width], gb[:], ALU.add)
                else:
                    last = v.tensor_copy(lg[:, t, 0:width], k.ps[:, t, 0:width])
            ch.link(last)
            if how != "top2":
                ch.link(v.tensor_reduce(mx[:], lg[:], AX.X, ALU.max))
                ch.link(v.tensor_scalar(mx[:], mx[:], -1.0, None, ALU.mult))
                for t in range(T):
                    last = v.tensor_scalar(lg[:, t, :], lg[:, t, :], mx[:, t:t + 1], None, ALU.add)
                last.then_inc(k.ready.sem, 1)
                v.wait_ge(k.copied.sem, k.copied.at(1))
                ch.link(v.tensor_reduce(sm[:], lg[:], AX.X, ALU.add))
                ch.link(v.reciprocal(sm[:], sm[:]))
                for t in range(T):
                    last = v.tensor_scalar(lg[:, t, :], lg[:, t, :], sm[:, t:t + 1], None, ALU.mult)
                ch.link(last)
            for t in range(T):
                last = v.max(top[:, t, :], lg[:, t, :])
            ch.link(last)
            for t in range(T):
                last = v.max_index(at[:, t, :], top[:, t, :], lg[:, t, :])
            ch.link(last)
            ch.link(v.tensor_copy(atf[:], at[:]))
            for t in range(T):
                for q in range(choices):
                    last = v.tensor_scalar(masks[:, t, q, :], k.ramp_f[:, 0:8], atf[:, t, q:q + 1], None,
                                           ALU.is_equal)
            ch.link(last)
            if how != "top2":
                ch.link(v.tensor_copy(wt[:], top[:, :, 0:choices]))
            else:
                v.tensor_tensor(sm[:], top[:, :, 1], top[:, :, 0], ALU.subtract).then_inc(k.ready.sem, 1)
                v.wait_ge(k.copied.sem, k.copied.at(1))
                ch.link(v.tensor_scalar(sm[:], mx[:], 1.0, None, ALU.add))
                ch.link(v.reciprocal(wt[:, :, 0], sm[:]))
                ch.link(v.tensor_tensor(wt[:, :, 1], wt[:, :, 0], mx[:], ALU.mult))
            ch.close()

        @block.scalar
        def _(a):
            a.wait_ge(k.ready.sem, k.ready.at(1))
            if how != "top2":
                a.activation(lg[:], lg[:], ACT.Exp).then_inc(k.copied.sem, 1)
            else:
                a.activation(mx[:], sm[:], ACT.Exp).then_inc(k.copied.sem, 1)
    done((k.loaded, 32 if bias is not None else 16), (k.mm, 1), (k.ready, 1), (k.copied, 1))
    return masks, wt


def dispatch(k, c, masks, choices, granules, rows, spread):
    nc = k.nc
    m = sb(c, k, "m", [P, T, EXPERTS])
    pos = sb(c, k, "pos", [P, T, EXPERTS])
    n_e = sb(c, k, "n_e", [P, EXPERTS])
    g_e = sb(c, k, "g_e", [P, EXPERTS])
    end = sb(c, k, "end", [P, EXPERTS])
    own = sb(c, k, "own", [P, granules])
    own_i = sb(c, k, "own_i", [P, granules], I32)
    pick = sb(c, k, "pick", [P, T, EXPERTS])
    slot_f = sb(c, k, "slot_f", [P, T, choices])
    slot = sb(c, k, "slot", [P, T, choices], I32)
    zero = sb(c, k, "zero", [P, D])
    with nc.Block() as block:
        @block.sync
        def _(sp):
            sp.wait_ge(k.ready.sem, k.ready.at(1))
            for g in range(granules):
                sp.dma_start(spread[g * P:(g + 1) * P, :], zero[:]).then_inc(k.loaded.sem, 16)

        @block.vector
        def _(v):
            ch = Chain(v, k.dve_step)
            v.memset(zero[:], 0.0).then_inc(k.ready.sem, 1)
            if choices == 1:
                v.tensor_copy(m[:], masks[:, :, 0, :]).then_inc(k.ready.sem, 1)
            else:
                v.tensor_tensor(m[:], masks[:, :, 0, :], masks[:, :, 1, :], ALU.add).then_inc(k.ready.sem, 1)
            v.wait_ge(k.mm.sem, k.mm.at(1))
            for t in range(T):
                v.tensor_copy(pos[:, t, :], k.ps[:, t, 0:EXPERTS])
            ch.link(v.tensor_copy(n_e[:], k.ps[:, T, 0:EXPERTS]))
            ch.link(v.tensor_scalar(g_e[:], n_e[:], 0.0, None, ALU.is_gt))
            for j in range(1, T):
                ch.link(v.scalar_tensor_tensor(g_e[:], n_e[:], float(P * j), g_e[:], ALU.is_gt, ALU.add))
            ch.link(v.tensor_tensor_scan(end[:], k.ones[:, 0:EXPERTS], g_e[:], 0.0, ALU.mult, ALU.add))
            ch.link(v.tensor_tensor(g_e[:], end[:], g_e[:], ALU.subtract))
            for t in range(T):
                last = v.scalar_tensor_tensor(pos[:, t, :], g_e[:], float(P), pos[:, t, :], ALU.mult, ALU.add)
            ch.link(last)
            for q in range(choices):
                ch.link(v.tensor_tensor(pick[:], masks[:, :, q, :], pos[:], ALU.mult))
                ch.link(v.tensor_reduce(slot_f[:, :, q], pick[:], AX.X, ALU.add))
            v.tensor_copy(slot[:], slot_f[:]).then_inc(k.copied.sem, 1)
            ch.link(v.memset(own[:], 0.0))
            for e in range(EXPERTS):
                ch.link(v.scalar_tensor_tensor(own[:], k.ramp_f[:, 0:granules], end[:, e:e + 1], own[:],
                                               ALU.is_ge, ALU.add))
            ch.link(v.tensor_scalar(own[:], own[:], float(EXPERTS - 1), None, ALU.min))
            ch.link(v.tensor_copy(own_i[:], own[:]))
            ch.close()

        @block.tensor
        def _(pe):
            pe.wait_ge(k.ready.sem, k.ready.at(2))
            for t in range(T):
                for s in range(t + 1):
                    pe.matmul(k.ps[:, t, 0:EXPERTS], k.before[:] if s == t else k.ones[:], m[:, s, :],
                              start=(s == 0), stop=(s == t))
            for s in range(T):
                i = pe.matmul(k.ps[:, T, 0:EXPERTS], k.ones[:], m[:, s, :], start=(s == 0), stop=(s == T - 1))
            i.then_inc(k.mm.sem, 1)

        @block.gpsimd
        def _(gp):
            gp.wait_ge(k.loaded.sem, k.loaded.at(16 * granules))
            gp.wait_ge(k.copied.sem, k.copied.at(1))
            for q in range(choices):
                for t in range(T):
                    gp.indirect_dma_start(spread, bass.IndirectOffsetOnAxis(ap=slot[:, t, q:q + 1].bitcast(U32), axis=0),
                                          rows[:, t, :], None).then_inc(k.gathered.sem, 16)
            gp.wait_ge(k.gathered.sem, k.gathered.at(16 * T * choices))
    done((k.ready, 2), (k.mm, 1), (k.copied, 1), (k.loaded, 16 * granules), (k.gathered, 16 * T * choices))
    return slot, own_i


def experts(k, c, granules, own, spread, result, w, hidden, gated):
    nc = k.nc
    HT = hidden // P
    ins = 2 if gated else 1
    W1 = [[sb(c, k, "w1", [P, T, hidden]) for _ in range(ins)] for _ in range(2)]
    W2 = [sb(c, k, "w2", [P, HT, D]) for _ in range(2)]
    b1 = [sb(c, k, "b1", [P, HT]) for _ in range(2)]
    b2 = [sb(c, k, "b2", [P, D]) for _ in range(2)]
    tok = [sb(c, k, "tok", [P, D]) for _ in range(2)]
    tokT = sb(c, k, "tokT", [P, T, P])
    hT = sb(c, k, "hT", [P, HT, P])
    act = sb(c, k, "act", [P, T * P]) if gated else None
    y = [sb(c, k, "y", [P, D]) for _ in range(2)]
    QT_ = HT // T
    loads = 16 * (2 + ins if gated else 4 + ins)

    def walk(eng, step):
        step(0, 0, 0)
        step(1, 1, 0)
        with eng.Fori(1, granules // 2) as j:
            for u in range(2):
                step(j * 2 + u, u, j)
        if granules % 2:
            step(granules - 1, 0, granules // 2)

    with nc.Block() as block:
        @block.sync
        def _(sp):
            def step(g, u, j):
                if later(g, 2):
                    sp.wait_ge(k.heads.sem, k.heads.at(-1) + g)
                e = sp.value_load(own[0:1, bass.ds(g, 1)], min_val=0, max_val=EXPERTS - 1)
                src = ((w["Wg"], w["Wu"]) if gated else (w["W1"],))
                sp.dma_start(tok[u][:], spread[bass.ds(g * P, P), :]).then_inc(k.slot[u].sem, 16)
                for q in range(ins):
                    sp.dma_start(W1[u][q][:], src[q][bass.ds(e, 1)].rearrange("a (k p) n -> p (a k) n", p=P)
                                 ).then_inc(k.slot[u].sem, 16)
                sp.dma_start(W2[u][:], (w["Wd"] if gated else w["W2"])[bass.ds(e, 1)].rearrange(
                    "a (k p) n -> p (a k) n", p=P)).then_inc(k.slot[u].sem, 16)
                if not gated:
                    sp.dma_start(b1[u][:], w["b1"][bass.ds(e, 1)].rearrange("a p m -> p (a m)")
                                 ).then_inc(k.slot[u].sem, 16)
                    sp.dma_start(b2[u][:], w["b2"][bass.ds(e, 1), :].to_broadcast([P, D])
                                 ).then_inc(k.slot[u].sem, 16)
            walk(sp, step)

        @block.tensor
        def _(pe):
            def step(g, u, j):
                pe.wait_ge(k.slot[u].sem, k.slot[u].at(loads) + j * loads)
                for f in range(T):
                    m = pe.transpose(k.ps[:, 0, f * P:(f + 1) * P], tok[u][:, f * P:(f + 1) * P], k.ident[:])
                m.then_inc(k.tp.sem, 1)
                pe.wait_ge(k.turned[0].sem, k.turned[0].at(1) + g)
                for q in range(QT_):
                    for i in range(ins):
                        b = 1 + (q * ins + i) % 4
                        lag = q * ins + i - 4
                        if lag >= 0:
                            pe.wait_ge(k.copied.sem, k.copied.at(lag // ins + 1) + g * QT_)
                        for s in range(T):
                            for f in range(T):
                                m = pe.matmul(k.ps[:, b, s * P:(s + 1) * P],
                                              W1[u][i][:, f, (q * T + s) * P:(q * T + s + 1) * P],
                                              tokT[:, f, :], start=(f == 0), stop=(f == T - 1))
                    m.then_inc(k.mm.sem, 1)
                pe.wait_ge(k.copied.sem, k.copied.at(QT_) + g * QT_)
                if later(g, 2):
                    pe.wait_ge(k.heads.sem, k.heads.at(-1) + g)
                for s in range(HT):
                    m = pe.matmul(k.ps[:, 5 + u, :], hT[:, s, :], W2[u][:, s, :], start=(s == 0), stop=(s == HT - 1))
                m.then_inc(k.out.sem, 1)
            walk(pe, step)

        @block.scalar
        def _(a):
            def step(g, u, j):
                if later(g, 1):
                    a.wait_ge(k.out.sem, k.out.at(0) + g)
                for q in range(QT_):
                    a.wait_ge(k.mm.sem, k.mm.at(q + 1) + g * QT_)
                    if gated:
                        if q or later(g, 1):
                            a.wait_ge(k.copied.sem, k.copied.at(q) + g * QT_)
                        a.activation(act[:], k.ps[:, 1 + (q * 2) % 4, :], ACT.Silu).then_inc(k.exped.sem, 1)
                    else:
                        for s in range(T):
                            i = a.activation(hT[:, q * T + s, :], k.ps[:, 1 + q % 4, s * P:(s + 1) * P],
                                             ACT.Gelu_apprx_tanh, bias=b1[u][:, q * T + s:q * T + s + 1])
                        i.then_inc(k.copied.sem, 1)
            walk(a, step)

        @block.vector
        def _(v):
            def step(g, u, j):
                v.wait_ge(k.tp.sem, k.tp.at(1) + g)
                if later(g, 1):
                    v.wait_ge(k.mm.sem, k.mm.at(0) + g * QT_)
                v.tensor_copy(tokT[:].rearrange("p k n -> p (k n)"), k.ps[:, 0, :]).then_inc(k.turned[0].sem, 1)
                if gated:
                    if later(g, 1):
                        v.wait_ge(k.out.sem, k.out.at(0) + g)
                    for q in range(QT_):
                        v.wait_ge(k.exped.sem, k.exped.at(q + 1) + g * QT_)
                        v.tensor_tensor(hT[:, q * T:(q + 1) * T, :].rearrange("p k n -> p (k n)"), act[:],
                                        k.ps[:, 1 + (q * 2 + 1) % 4, :], ALU.mult).then_inc(k.copied.sem, 1)
                v.wait_ge(k.out.sem, k.out.at(1) + g)
                if later(g, 2):
                    v.wait_ge(k.pool_stored[u].sem, k.pool_stored[u].at(0) + j * 16)
                if gated:
                    v.tensor_copy(y[u][:], k.ps[:, 5 + u, :]).then_inc(k.heads.sem, 1)
                else:
                    v.tensor_tensor(y[u][:], k.ps[:, 5 + u, :], b2[u][:], ALU.add).then_inc(k.heads.sem, 1)
            walk(v, step)

        @block.gpsimd
        def _(gp):
            def step(g, u, j):
                gp.wait_ge(k.heads.sem, k.heads.at(1) + g)
                gp.dma_start(result[bass.ds(g * P, P), :], y[u][:]).then_inc(k.pool_stored[u].sem, 16)
            for g in range(granules):
                step(g, g % 2, g // 2)
            for u in range(2):
                gp.wait_ge(k.pool_stored[u].sem, k.pool_stored[u].at(16 * ((granules + 1 - u) // 2)))
    n0, n1 = (granules + 1) // 2, granules // 2
    done((k.slot[0], loads * n0), (k.slot[1], loads * n1), (k.tp, granules), (k.turned[0], granules),
         (k.mm, QT_ * granules), (k.copied, QT_ * granules), (k.out, granules), (k.heads, granules),
         (k.pool_stored[0], 16 * n0), (k.pool_stored[1], 16 * n1), (k.exped, QT_ * granules if gated else 0))


def combine(k, c, slot, wt, choices, result):
    with k.nc.Block() as block:
        back = [sb(c, k, "back", [P, T, D]) for _ in range(choices)]

        @block.gpsimd
        def _(gp):
            for q in range(choices):
                for t in range(T):
                    gp.indirect_dma_start(back[q][:, t, :], None, result,
                                          bass.IndirectOffsetOnAxis(ap=slot[:, t, q:q + 1].bitcast(U32), axis=0)
                                          ).then_inc(k.gathered.sem, 16)

        @block.vector
        def _(v):
            ch = Chain(v, k.dve_step)
            v.wait_ge(k.gathered.sem, k.gathered.at(16 * T * choices))
            for q in range(choices):
                for t in range(T):
                    last = v.scalar_tensor_tensor(k.X[:, t, :], back[q][:, t, :], wt[:, t, q:q + 1], k.X[:, t, :],
                                                  ALU.mult, ALU.add)
                ch.link(last)
            ch.close()
    done((k.gathered, 16 * T * choices))


def routed_ffn(k, cols, rows, gate, bias, how, choices, granules, w, hidden, gated, spread, result):
    spread, result = spread[0:granules * P, :], result[0:granules * P, :]
    with ExitStack() as c:
        masks, wt = routing(k, c, cols, gate, bias, EXPERTS, how, choices)
        slot, own = dispatch(k, c, masks, choices, granules, rows, spread)
        with ExitStack() as c2:
            experts(k, c2, granules, own, spread, result, w, hidden, gated)
        combine(k, c, slot, wt, choices, result)



def gat_setup(k, c):
    nc = k.nc
    a_part, w_part = (0, 0, 1, 0, 2, 1), (0, 1, 0, 2, 0, 1)
    G4 = 4 * P
    k.oht = sb(c, k, "oht", [P, EA * P], BF16)
    k.eaT = sb(c, k, "eaT", [P, EA * P], BF16)
    k.we = sb(c, k, "we", [P, 3, D], BF16)
    k.pick = sb(c, k, "pick", [P, EA, 3 * T])
    with ExitStack() as c2:
        oh = sb(c2, k, "oh", [P, EA, P], BF16)
        eap = sb(c2, k, "eap", [P, EA, 12], BF16)
        p3 = [sb(c2, k, "p3", [P, EA, 2], BF16) for _ in range(3)]
        rest, own_f = sb(c2, k, "rest", [P, EA, 2]), sb(c2, k, "own_f", [P, EA])
        w_in, w_rest = sb(c2, k, "w_in", [2, 3, D]), sb(c2, k, "w_rest", [2, 3, D])
        w3 = [sb(c2, k, "w3", [2, 3, D], BF16) for _ in range(3)]
        with nc.Block() as block:
            @block.sync
            def _(sp):
                sp.dma_start(w_in[:], k.i["L1_gnn_We"].rearrange("l c n -> c l n")).then_inc(k.loaded.sem, 16)
                sp.wait_ge(k.ready.sem, k.ready.at(2))
                for j in range(6):
                    sp.dma_start(k.we[2 * j:2 * j + 2, :, :], w3[w_part[j]][:]).then_inc(k.stored[0].sem, 16)
                sp.wait_ge(k.stored[0].sem, k.stored[0].at(96))

            @block.gpsimd
            def _(gp):
                gp.memset(k.we[:], 0.0).then_inc(k.ready.sem, 1)
                gp.memset(k.eaT[:], 0.0).then_inc(k.maxed.sem, 1)

            @block.vector
            def _(v):
                ch = Chain(v, k.dve_step)
                split3(v, ch, [p[:] for p in p3], k.ea[:], rest[:])
                for j in range(6):
                    last = v.tensor_copy(eap[:, :, 2 * j:2 * j + 2], p3[a_part[j]][:])
                last.then_inc(k.probs.sem, 1)
                with v.Fori(0, EA // 4) as j:
                    for u in range(4):
                        i = j * 4 + u
                        m = v.tensor_scalar(oh[:, bass.ds(i, 1), :].rearrange("p a n -> p (a n)"), k.ramp[:, 0:P],
                                            k.dst_f[:, bass.ds(i, 1)], None, ALU.is_equal)
                    m.then_inc(k.copied.sem, 1)
                v.wait_ge(k.loaded.sem, k.loaded.at(16))
                split3(v, ch, [w[:] for w in w3], w_in[:], w_rest[:])
                v.tensor_copy(w_rest[:, 0, 0:1], w3[0][:, 0, 0:1]).then_inc(k.ready.sem, 1)
                ch.link(v.tensor_copy(own_f[:], k.own[:]))
                for b in range(T):
                    for q in range(3):
                        v.tensor_scalar(k.pick[:, :, 3 * b + q], own_f[:], float(b), None, ALU.is_equal)
                ch.close()

            @block.tensor
            def _(pe):
                pe.wait_ge(k.probs.sem, k.probs.at(1))
                for q in range(EA // 4):
                    if q >= 2:
                        pe.wait_ge(k.turned[0].sem, k.turned[0].at(q - 1))
                        pe.wait_ge(k.turned[1].sem, k.turned[1].at(q - 1))
                    for u in range(4):
                        m = pe.transpose(k.psb[0:12, q % 2, u * P:(u + 1) * P], eap[:, 4 * q + u, :], k.identb[:])
                    m.then_inc(k.mm.sem, 1)
                    pe.wait_ge(k.copied.sem, k.copied.at(q + 1))
                    for u in range(4):
                        m = pe.transpose(k.psb[:, 2 + q % 2, u * P:(u + 1) * P], oh[:, 4 * q + u, :], k.identb[:])
                    m.then_inc(k.tp.sem, 1)

            @block.scalar
            def _(a):
                a.wait_ge(k.maxed.sem, k.maxed.at(1))
                for q in range(EA // 4):
                    a.wait_ge(k.mm.sem, k.mm.at(q + 1))
                    a.activation(k.eaT[0:12, q * G4:(q + 1) * G4], k.psb[0:12, q % 2, 0:G4],
                                 ACT.Copy).then_inc(k.turned[0].sem, 1)
                    a.wait_ge(k.tp.sem, k.tp.at(q + 1))
                    a.activation(k.oht[:, q * G4:(q + 1) * G4], k.psb[:, 2 + q % 2, 0:G4],
                                 ACT.Copy).then_inc(k.turned[1].sem, 1)
        done((k.loaded, 16), (k.copied, EA // 4), (k.ready, 2), (k.stored[0], 96), (k.maxed, 1), (k.probs, 1),
             (k.mm, EA // 4), (k.tp, EA // 4), (k.turned[0], EA // 4), (k.turned[1], EA // 4))


def per_edge(pe, k, bank, table):
    h = EA // 2
    for i in range(EA):
        m = pe.matmul(k.ps[:, bank + i // h, i % h * 12:(i % h + 1) * 12], k.oht[:, i * P:(i + 1) * P],
                      table[:].rearrange("p a c -> p (a c)"), start=True, stop=True)
        if i % h == h - 1:
            m.then_inc(k.tp.sem, 1)


def pick_own(v, ch, k, bank, me, prod):
    h = EA // 2
    for half in range(2):
        v.wait_ge(k.tp.sem, k.tp.at(half + 1))
        ch.link(v.tensor_tensor(prod[:, half * h:(half + 1) * h, :], k.ps[:, bank + half, 0:h * 12].rearrange(
            "p (i c) -> p i c", c=12), k.pick[:, half * h:(half + 1) * h, :], ALU.mult))
    ch.link(v.tensor_reduce(me[:], prod[:], AX.X, ALU.add))


def gat_layer(k, l, XL, H2, rows_in, cols_in):
    nc = k.nc
    W1 = D + 1
    with ExitStack() as c:
        att, b_out = sb(c, k, "att", [P, D]), sb(c, k, "b_out", [P, D])
        eac = sb(c, k, "eac", [P, EA])
        L, sdot, me = [sb(c, k, n, [P, EA]) for n in ("L", "sdot", "me")]
        M = sb(c, k, "M", [P, N])
        prod = sb(c, k, "prod", [P, EA, 12])
        mc = sb(c, k, "mc", [P, T])
        mrest = sb(c, k, "mrest", [P, T])
        mp = sb(c, k, "mp", [P, T, 3], BF16)
        hi16 = sb(c, k, "hi16", [P, EA], F16)
        XP = sb(c, k, "xp", [P, 3, T, D], BF16)
        ap = sb(c, k, "ap", [P, T, 3], BF16)
        with ExitStack() as c2:
            W = [sb(c2, k, "w", [P, T, D]) for _ in range(2)]
            XR = sb(c2, k, "xr", [P, T, W1])
            bl, br = sb(c2, k, "bl", [P, D]), sb(c2, k, "br", [P, D])
            web = sb(c2, k, "web", [P, 2, D])
            wc = sb(c2, k, "wc", [P, 2])
            junk = sb(c2, k, "junk", [P, D])
            with nc.Block() as block:
                @block.sync
                def _(sp):
                    for dst, src in ((bl[:], bcast(k.i["L1_gnn_bl"][l])), (br[:], bcast(k.i["L1_gnn_br"][l])),
                                     (att[:], bcast(k.i["L1_gnn_att"][l])), (b_out[:], bcast(k.i["L1_gnn_b_out"][l])),
                                     (web[:, 0, :], bcast(k.i["L1_gnn_We"][l, 0])),
                                     (web[:, 1, :], bcast(k.i["L1_gnn_We"][l, 1]))):
                        sp.dma_start(dst, src).then_inc(k.loaded.sem, 16)
                    for j, m in enumerate((k.i["L1_gnn_Wl"], k.i["L1_gnn_Wr"])):
                        sp.dma_start(W[j][:], rows_of(m[l])).then_inc(k.slot[j].sem, 16)
                    sp.wait_ge(k.probs.sem, k.probs.at(1))
                    sp.dma_start(k.xl_d.rearrange("(k p) n -> p k n", p=P), XL[:]).then_inc(k.stored[0].sem, 16)
                    sp.wait_ge(k.stored[0].sem, k.stored[0].at(16))

                @block.tensor
                def _(pe):
                    for j in range(2):
                        pe.wait_ge(k.slot[j].sem, k.slot[j].at(16))
                        mm_rows(pe, k, 4 * j, cols_in, W[j]).then_inc(k.mm.sem, 1)
                    pe.wait_ge(k.ready.sem, k.ready.at(1))
                    per_edge(pe, k, 0, ap)

                @block.vector
                def _(v):
                    ch = Chain(v, k.dve_step)
                    v.wait_ge(k.loaded.sem, k.loaded.at(96))
                    for q in range(2):
                        ch.link(v.scalar_tensor_tensor(junk[:], web[:, q, :], 0.2, att[:], ALU.mult, ALU.mult,
                                                       accum_out=wc[:, q:q + 1]))
                    ch.link(v.tensor_scalar(eac[:], k.ea[:, :, 0], wc[:, 0:1], None, ALU.mult))
                    v.memset(M[:], NEG)
                    ch.link(v.scalar_tensor_tensor(eac[:], k.ea[:, :, 1], wc[:, 1:2], eac[:], ALU.mult, ALU.add))
                    for j, (x, b) in enumerate(((XL, bl), (XR, br))):
                        v.wait_ge(k.mm.sem, k.mm.at(j + 1))
                        for t in range(T):
                            last = v.tensor_tensor(x[:, t, 0:D], k.ps[:, 4 * j + t, :], b[:], ALU.add)
                        ch.link(last)
                        for t in range(T):
                            last = v.scalar_tensor_tensor(junk[:], x[:, t, 0:D], 0.2, att[:], ALU.mult, ALU.mult,
                                                          accum_out=x[:, t, D:W1])
                            if t < T - 1:
                                ch.link(last)
                        last.then_inc(k.probs.sem, 1)
                        v.wait_ge(k.probs.sem, k.probs.at(j + 1))
                    split3(v, ch, [ap[:, :, q] for q in range(3)], XR[:, :, D], mrest[:])
                    v.tensor_copy(mrest[:, 0:1], ap[:, 0, 0:1]).then_inc(k.ready.sem, 1)
                    split3(v, ch, [XP[:, q] for q in range(3)], XR[:, :, 0:D], XR[:, :, 0:D])
                    pick_own(v, ch, k, 0, me, prod)
                    ch.link(v.tensor_tensor(eac[:], eac[:], me[:], ALU.add))
                    ch.close()
            done((k.loaded, 96), (k.slot[0], 16), (k.slot[1], 16), (k.stored[0], 16), (k.mm, 2), (k.probs, 2),
                 (k.ready, 1), (k.tp, 2))

        with ExitStack() as c2:
            G = [sb(c2, k, "g", [P, W1]) for _ in range(4)]
            r = [sb(c2, k, "r", [P, D]) for _ in range(4)]
            junk = sb(c2, k, "junk", [P, D])
            pen = [sb(c2, k, "pen", [P, P], BF16) for _ in range(2)]
            with nc.Block() as block:
                @block.gpsimd
                def _(gp):
                    for i in range(EA):
                        if i >= 4:
                            gp.wait_ge(k.mm.sem, k.mm.at(i - 3))
                            gp.wait_ge(k.probs.sem, k.probs.at(i - 3))
                        gp.indirect_dma_start(G[i % 4][:], None, k.xl_d,
                                              bass.IndirectOffsetOnAxis(ap=k.src_i[:, i:i + 1].bitcast(U32), axis=0)
                                              ).then_inc(k.pool_slot[i % 4].sem, 16)

                @block.tensor
                def _(pe):
                    def step(i, u, j, b):
                        if later(i, 4):
                            pe.wait_ge(k.copied.sem, k.copied.at(-3) + i)
                        pe.matmul(k.ps[:, u, :], k.eaT[:, bass.ds(i * P, P)], k.we[:, l, :],
                                  start=True, stop=False)
                        for q in range(3):
                            pe.matmul(k.ps[:, u, :], k.oht[:, bass.ds(i * P, P)],
                                      XP[:, q, bass.ds(b, 1), :].rearrange("p a n -> p (a n)"),
                                      start=False, stop=False)
                        pe.wait_ge(k.pool_slot[u].sem, k.pool_slot[u].at(16) + j * 16)
                        pe.matmul(k.ps[:, u, :], k.ident[:], G[u][:, 0:D], start=False, stop=True
                                  ).then_inc(k.mm.sem, 1)
                    own = dst_tiles(pe, k, 0)
                    for u in range(4):
                        step(u, u, 0, own[u])
                    with pe.Fori(1, EA // 4) as j:
                        own = dst_tiles(pe, k, j * 4)
                        for u in range(4):
                            step(j * 4 + u, u, j, own[u])

                @block.scalar
                def _(a):
                    def step(i, u):
                        a.wait_ge(k.mm.sem, k.mm.at(1) + i)
                        if later(i, 4):
                            a.wait_ge(k.probs.sem, k.probs.at(-3) + i)
                        a.activation(r[u][:], k.ps[:, u, :], ACT.Relu, scale=0.8).then_inc(k.copied.sem, 1)
                    for u in range(4):
                        step(u, u)
                    with a.Fori(1, EA // 4) as j:
                        for u in range(4):
                            step(j * 4 + u, u)

                @block.vector
                def _(v):
                    ch = Chain(v, k.dve_step)
                    with v.Fori(0, EA // 4) as j:
                        ch.loop = j * 8
                        own = dst_tiles(v, k, j * 4)
                        for u in range(4):
                            b = own[u]
                            col = bass.ds(j * 4 + u, 1)
                            v.tensor_scalar(pen[u % 2][:], k.ramp[:, 0:P], k.dst_f[:, col], NEG,
                                            ALU.not_equal, ALU.mult)
                            v.wait_ge(k.copied.sem, k.copied.at(u + 1) + j * 4)
                            ch.link(v.scalar_tensor_tensor(junk[:], r[u][:], 1.0, att[:], ALU.mult, ALU.mult,
                                                           accum_out=sdot[:, col]))
                            v.scalar_tensor_tensor(L[:, col], G[u][:, D:W1], eac[:, col], sdot[:, col],
                                                   ALU.add, ALU.add).then_inc(k.probs.sem, 1)
                            v.wait_ge(k.probs.sem, k.probs.at(u + 1) + j * 4)
                            top = M[:, bass.ds(b * P, P)]
                            ch.link(v.scalar_tensor_tensor(top, pen[u % 2][:], L[:, col], top, ALU.add, ALU.max))
                    ch.close(EA * 2)
            done(*[(k.pool_slot[u], EA * 4) for u in range(4)], (k.mm, EA), (k.copied, EA), (k.probs, EA))

        with nc.Block() as block:
            @block.tensor
            def _(pe):
                for t in range(T):
                    m = pe.transpose(k.ps[:, 0, t * P:(t + 1) * P], M[:, t * P:(t + 1) * P], k.ident[:])
                m.then_inc(k.mm.sem, 1)
                pe.wait_ge(k.ready.sem, k.ready.at(1))
                per_edge(pe, k, 1, mp)

            @block.vector
            def _(v):
                ch = Chain(v, k.dve_step)
                v.wait_ge(k.mm.sem, k.mm.at(1))
                ch.link(v.tensor_reduce(mc[:], k.ps[:, 0, :].rearrange("p (t n) -> p t n", t=T), AX.X, ALU.max))
                split3(v, ch, [mp[:, :, q] for q in range(3)], mc[:], mrest[:])
                v.tensor_copy(mrest[:, 0:1], mc[:, 0:1]).then_inc(k.ready.sem, 1)
                pick_own(v, ch, k, 1, me, prod)
                ch.link(v.tensor_tensor(L[:], L[:], me[:], ALU.subtract))
                v.tensor_scalar(L[:], L[:], 0.0, None, ALU.min).then_inc(k.ready.sem, 1)
                v.wait_ge(k.copied.sem, k.copied.at(1))
                ch.link(v.tensor_scalar(me[:], me[:], EX_SCALE, None, ALU.mult))
                ch.link(v.tensor_copy(hi16[:], me[:]))
                ch.link(v.tensor_copy(L[:], hi16[:]))
                ch.link(v.tensor_tensor(me[:], me[:], L[:], ALU.subtract))
                ch.close()

            @block.scalar
            def _(a):
                a.wait_ge(k.ready.sem, k.ready.at(2))
                a.activation(me[:], L[:], ACT.Exp).then_inc(k.copied.sem, 1)
        done((k.mm, 1), (k.tp, 2), (k.ready, 2), (k.copied, 1))

        with ExitStack() as c2:
            os_ = [sb(c2, k, "os", [P, N], F16) for _ in range(4)]
            dh = [sb(c2, k, "dh", [P, P], F16) for _ in range(4)]
            dl = [sb(c2, k, "dl", [P, P], F16) for _ in range(4)]
            A, AT = sb(c2, k, "A", [P, T, N]), sb(c2, k, "AT", [P, T, N])
            den = sb(c2, k, "den", [P, T])
            with nc.Block() as block:
                @block.vector
                def _(v):
                    def step(i, u):
                        if later(i, 4):
                            v.wait_ge(k.mm.sem, k.mm.at(-3) + i)
                        col = bass.ds(i, 1)
                        v.tensor_scalar(os_[u][:], k.ramp[:], k.src_f[:, col], None, ALU.is_equal)
                        v.tensor_scalar(dh[u][:], k.ramp[:, 0:P], k.dst_f[:, col], L[:, col], ALU.is_equal, ALU.mult)
                        v.tensor_scalar(dl[u][:], k.ramp[:, 0:P], k.dst_f[:, col], me[:, col], ALU.is_equal,
                                        ALU.mult).then_inc(k.ready.sem, 1)
                    for u in range(4):
                        step(u, u)
                    with v.Fori(1, EA // 4) as j:
                        for u in range(4):
                            step(j * 4 + u, u)

                @block.tensor
                def _(pe):
                    clear_banks(pe, k, range(T))
                    with pe.Fori(0, EA // 4) as j:
                        own = dst_tiles(pe, k, j * 4)
                        for u in range(4):
                            i, b = j * 4 + u, own[u]
                            pe.wait_ge(k.ready.sem, k.ready.at(1) + i)
                            for half in (dh, dl):
                                m = pe.matmul(k.ps[:, bass.ds(b, 1), :].rearrange("p a n -> p (a n)"), half[u][:],
                                              os_[u][:], start=False, stop=True, skip_group_check=True)
                            m.then_inc(k.mm.sem, 1)
            done((k.mm, EA), (k.ready, EA))
            with nc.Block() as block:
                @block.scalar
                def _(a):
                    for t in range(T):
                        i = a.activation(A[:, t, :], k.ps[:, t, :], ACT.Copy, accum_out=den[:, t:t + 1])
                    i.then_inc(k.copied.sem, 1)
                    for f in (0, 2):
                        a.wait_ge(k.tp.sem, k.tp.at(f + 1))
                        i = a.activation(AT[:, f, :], k.ps[:, f, :], ACT.Copy)
                    i.then_inc(k.copied.sem, 1)

                @block.tensor
                def _(pe):
                    pe.wait_ge(k.copied.sem, k.copied.at(1))
                    for f in range(T):
                        for t in range(T):
                            m = pe.transpose(k.ps[:, f, t * P:(t + 1) * P], A[:, t, f * P:(f + 1) * P], k.ident[:])
                        m.then_inc(k.tp.sem, 1)
                    pe.wait_ge(k.copied.sem, k.copied.at(2))
                    pe.wait_ge(k.ready.sem, k.ready.at(1))
                    for t in range(T):
                        for s in range(T):
                            m = pe.matmul(k.ps[:, T + t, :], AT[:, s, t * P:(t + 1) * P], XL[:, s, 0:D],
                                          start=(s == 0), stop=(s == T - 1))
                        m.then_inc(k.mm.sem, 1)

                @block.vector
                def _(v):
                    ch = Chain(v, k.dve_step)
                    for t in range(T):
                        v.tensor_tensor(H2[:, t, :], rows_in[:, t, :], b_out[:], ALU.add)
                    v.wait_ge(k.copied.sem, k.copied.at(1))
                    ch.link(v.tensor_scalar(den[:], den[:], 1e-16 * EX_SCALE, None, ALU.add))
                    ch.link(v.reciprocal(den[:], den[:]))
                    for f in (1, 3):
                        v.wait_ge(k.tp.sem, k.tp.at(f + 1))
                        m = v.tensor_copy(AT[:, f, :], k.ps[:, f, :])
                    m.then_inc(k.ready.sem, 1)
                    for t in range(T):
                        v.wait_ge(k.mm.sem, k.mm.at(t + 1))
                        v.scalar_tensor_tensor(H2[:, t, :], k.ps[:, T + t, :], den[:, t:t + 1], H2[:, t, :],
                                               ALU.mult, ALU.add)
                    ch.close()
            done((k.copied, 2), (k.mm, T), (k.tp, T), (k.ready, 1))


def gat(k):
    nc = k.nc
    with ExitStack() as c:
        gat_setup(k, c)
        XL = sb(c, k, "xl", [P, T, D + 1])
        H2 = sb(c, k, "h2", [P, T, D])
        gb = [sb(c, k, "gb", [P, D]) for _ in range(2)]
        for l in range(3):
            gat_layer(k, l, XL, H2, k.N, k.NT)
            load(k, ((gb[0][:], bcast(k.i["L1_gnn_gamma"][l])), (gb[1][:], bcast(k.i["L1_gnn_beta"][l]))))
            layernorm(k, H2, k.N, k.NT, passes=(gb,), relu=True)
        with nc.Block() as block:
            @block.vector
            def _(v):
                v.tensor_tensor(k.X[:], k.X[:], k.N[:], ALU.add)


def load(k, pairs):
    with k.nc.Block() as block:
        @block.sync
        def _(sp):
            for dst, src in pairs:
                sp.dma_start(dst, src).then_inc(k.loaded.sem, 16)
            sp.wait_ge(k.loaded.sem, k.loaded.at(16 * len(pairs)))
    done((k.loaded, 16 * len(pairs)))



def positional_ffn(k):
    nc, i_ = k.nc, k.i
    FF = 2048
    HT = FF // P
    SL = 64

    def by_expert(x, m):
        return x.rearrange("p (e m t) -> p e m t", e=EXPERTS, m=2)[:, :, m, :]

    def by_token(x, m):
        return x.rearrange("p (m e t) -> p e m t", e=EXPERTS, m=2)[:, :, m, :]

    with ExitStack() as c:
        XA = sb(c, k, "xa", [P, T, N])
        YT = k.NT
        with ExitStack() as c2:
            gb = [sb(c2, k, "gb", [P, D]) for _ in range(2)]
            N2, N2T = sb(c2, k, "n2", [P, T, D]), sb(c2, k, "n2t", [P, T, D])
            W = sb(c2, k, "w", [P, T, D])
            ab = sb(c2, k, "ab", [P, T])
            load(k, ((gb[0][:], bcast(i_["L1_ffn_ln_g"])), (gb[1][:], bcast(i_["L1_ffn_ln_b"])), (ab[:], i_["attn_b"]),
                     (W[:], rows_of(i_["attn_wT"]))))
            layernorm(k, k.N, N2, N2T, passes=(gb,))
            with nc.Block() as block:
                @block.tensor
                def _(pe):
                    mm_cols(pe, k, 0, W, N2T).then_inc(k.mm.sem, 1)

                @block.vector
                def _(v):
                    v.wait_ge(k.mm.sem, k.mm.at(1))
                    for t in range(T):
                        for m in range(2):
                            v.scalar_tensor_tensor(by_expert(XA[:, t, :], m), by_token(k.ps[:, t, :], m),
                                                   ab[:, t:t + 1], by_token(k.NT[:, t, :], m), ALU.add, ALU.add)
            done((k.mm, 1))

        with ExitStack() as c2:
            W1 = [sb(c2, k, "w1", [P, T, FF]) for _ in range(2)]
            W2 = [sb(c2, k, "w2", [P, HT, D]) for _ in range(2)]
            b1, b2 = sb(c2, k, "b1", [P, FF]), sb(c2, k, "b2", [P, D])
            h = sb(c2, k, "h", [P, FF])
            hT = k.N[:].rearrange("p a (b n) -> p (a b) n", n=P)
            yb = sb(c2, k, "yb", [P, D])
            PAIRS = EXPERTS // 2
            with nc.Block() as block:
                @block.sync
                def _(sp):
                    for j in range(PAIRS):
                        for u in range(2):
                            if j:
                                sp.wait_ge(k.mm.sem, k.mm.at(2 * j - 1 + u))
                            sp.dma_start(W1[u][:], rows_of(i_["fc1T"][2 * j + u])).then_inc(k.slot[u].sem, 16)
                        for u in range(2):
                            if j:
                                sp.wait_ge(k.out.sem, k.out.at(2 * j - 1 + u))
                            sp.dma_start(W2[u][:], rows_of(i_["fc2T"][2 * j + u])).then_inc(k.slot[2 + u].sem, 16)

                @block.gpsimd
                def _(gp):
                    for j in range(PAIRS):
                        if j:
                            gp.wait_ge(k.heads.sem, k.heads.at(j))
                        for u in range(2):
                            o = slice(u * SL, (u + 1) * SL)
                            gp.dma_start(b1[o, :], bcast(i_["L1_ffn_fc1_b"][2 * j + u], SL)
                                         ).then_inc(k.gathered.sem, 16)
                            gp.dma_start(b2[o, :], bcast(i_["L1_ffn_fc2_b"][2 * j + u], SL)
                                         ).then_inc(k.gathered.sem, 16)

                @block.tensor
                def _(pe):
                    def turn_y(j):
                        pe.wait_ge(k.heads.sem, k.heads.at(j + 1))
                        if j:
                            pe.wait_ge(k.probs.sem, k.probs.at(j))
                        for f in range(T):
                            m = pe.transpose(k.ps[:, 7, f * P:(f + 1) * P], yb[:, f * P:(f + 1) * P], k.ident[:])
                        m.then_inc(k.av.sem, 1)

                    for j in range(PAIRS):
                        for u in range(2):
                            e = 2 * j + u
                            pe.wait_ge(k.slot[u].sem, k.slot[u].at(16 * (j + 1)))
                            for q in range(T):
                                for f in range(T):
                                    m = pe.matmul(k.ps[u * SL:(u + 1) * SL, q, :], XA[:, f, e * SL:(e + 1) * SL],
                                                  W1[u][:, f, q * 512:(q + 1) * 512],
                                                  start=(f == 0), stop=(f == T - 1))
                            m.then_inc(k.mm.sem, 1)
                        if j:
                            turn_y(j - 1)
                        for q in range(T):
                            n = T * j + q
                            pe.wait_ge(k.ready.sem, k.ready.at(n + 1))
                            if n >= 2:
                                pe.wait_ge(k.copied.sem, k.copied.at(n - 1))
                            for s in range(T):
                                m = pe.transpose(k.ps[:, 4 + q % 2, s * P:(s + 1) * P],
                                                 h[:, (T * q + s) * P:(T * q + s + 1) * P], k.ident[:])
                            m.then_inc(k.tp.sem, 1)
                        pe.wait_ge(k.copied.sem, k.copied.at(T * (j + 1)))
                        for u in range(2):
                            pe.wait_ge(k.slot[2 + u].sem, k.slot[2 + u].at(16 * (j + 1)))
                            for s in range(HT):
                                m = pe.matmul(k.ps[u * SL:(u + 1) * SL, 6, :], hT[:, s, u * SL:(u + 1) * SL],
                                              W2[u][:, s, :], start=(s == 0), stop=(s == HT - 1))
                            m.then_inc(k.out.sem, 1)
                    turn_y(PAIRS - 1)

                @block.scalar
                def _(a):
                    for n in range(T * PAIRS):
                        q = n % T
                        a.wait_ge(k.tp.sem, k.tp.at(n + 1))
                        if n >= T:
                            a.wait_ge(k.out.sem, k.out.at(2 * (n // T)))
                        a.activation(hT[:, T * q:T * q + T, :].rearrange("p s n -> p (s n)"), k.ps[:, 4 + q % 2, :],
                                     ACT.Gelu).then_inc(k.copied.sem, 1)

                @block.vector
                def _(v):
                    def spread_y(j):
                        v.wait_ge(k.av.sem, k.av.at(j + 1))
                        for u in range(2):
                            for m in range(2):
                                at = m * 256 + (2 * j + u) * 32
                                i = v.tensor_copy(YT[:, :, at:at + 32], k.ps[:, 7, :].rearrange(
                                    "p (f u m t) -> p u m f t", f=T, u=2, m=2)[:, u, m])
                        i.then_inc(k.probs.sem, 1)

                    for j in range(PAIRS):
                        v.wait_ge(k.mm.sem, k.mm.at(2 * j + 2))
                        v.wait_ge(k.gathered.sem, k.gathered.at(64 * (j + 1)))
                        for q in range(T):
                            if j:
                                v.wait_ge(k.tp.sem, k.tp.at(T * (j - 1) + q + 1))
                            v.tensor_tensor(h[:, q * 512:(q + 1) * 512], k.ps[:, q, :], b1[:, q * 512:(q + 1) * 512],
                                            ALU.add).then_inc(k.ready.sem, 1)
                        if j:
                            spread_y(j - 1)
                        v.wait_ge(k.out.sem, k.out.at(2 * j + 2))
                        v.tensor_tensor(yb[:], k.ps[:, 6, :], b2[:], ALU.add).then_inc(k.heads.sem, 1)
                    spread_y(PAIRS - 1)
            done((k.slot[0], 16 * PAIRS), (k.slot[1], 16 * PAIRS), (k.slot[2], 16 * PAIRS), (k.slot[3], 16 * PAIRS),
                 (k.gathered, 64 * PAIRS), (k.mm, 2 * PAIRS), (k.tp, T * PAIRS), (k.ready, T * PAIRS),
                 (k.copied, T * PAIRS), (k.out, 2 * PAIRS), (k.heads, PAIRS), (k.av, PAIRS), (k.probs, PAIRS))

        W, nb, o = sb(c, k, "wn", [P, T, D]), sb(c, k, "nb", [P, D]), sb(c, k, "o", [P, T, D])
        load(k, ((W[:], rows_of(i_["next_wT"])), (nb[:], bcast(i_["L1_ffn_next_b"]))))
        with nc.Block() as block:
            @block.tensor
            def _(pe):
                mm_rows(pe, k, 0, YT, W).then_inc(k.mm.sem, 1)

            @block.vector
            def _(v):
                v.wait_ge(k.mm.sem, k.mm.at(1))
                for t in range(T):
                    v.tensor_tensor(o[:, t, :], k.ps[:, t, :], nb[:], ALU.add).then_inc(k.ready.sem, 1)
                for t in range(T):
                    v.wait_ge(k.copied.sem, k.copied.at(t + 1))
                    v.tensor_tensor(k.X[:, t, :], k.X[:, t, :], o[:, t, :], ALU.add)

            @block.scalar
            def _(a):
                for t in range(T):
                    a.wait_ge(k.ready.sem, k.ready.at(t + 1))
                    a.activation(o[:, t, :], o[:, t, :], ACT.Gelu).then_inc(k.copied.sem, 1)
        done((k.mm, 1), (k.ready, T), (k.copied, T))



def graph_conv(k):
    nc = k.nc
    with ExitStack() as c:
        W, bias = sb(c, k, "w", [P, T, D]), sb(c, k, "bias", [P, D])
        sup = sb(c, k, "sup", [P, T, D])
        AT = sb(c, k, "at", [P, T, N])
        rest = sb(c, k, "rest", [P, EB])
        wp = [sb(c, k, "wp", [P, EB], BF16) for _ in range(3)]
        wf = [sb(c, k, "wf", [P, EB]) for _ in range(3)]
        os_ = [sb(c, k, "os", [P, N], BF16) for _ in range(4)]
        dw = [[sb(c, k, "dw", [P, P], BF16) for _ in range(3)] for _ in range(4)]
        load(k, ((W[:], rows_of(k.i["L2_gnn_weight"])),
                 (bias[:], bcast(k.i["L2_gnn_bias"]))))
        with nc.Block() as block:
            @block.tensor
            def _(pe):
                mm_rows(pe, k, 4, k.NT, W).then_inc(k.mm.sem, 1)

            @block.vector
            def _(v):
                ch = Chain(v, k.dve_step)
                split3(v, ch, [w[:] for w in wp], k.ew[:], rest[:])
                for q in range(3):
                    v.tensor_copy(wf[q][:], wp[q][:])
                ch.close()

            @block.scalar
            def _(a):
                a.wait_ge(k.mm.sem, k.mm.at(1))
                for t in range(T):
                    a.activation(sup[:, t, :], k.ps[:, T + t, :], ACT.Copy)
        done((k.mm, 1))
        with nc.Block() as block:
            @block.vector
            def _(v):
                def step(i, u):
                    if later(i, 4):
                        v.wait_ge(k.mm.sem, k.mm.at(-3) + i)
                    col = bass.ds(i, 1)
                    v.tensor_scalar(os_[u][:], k.ramp[:], k.src_f[:, col], None, ALU.is_equal)
                    for q in range(3):
                        m = v.tensor_scalar(dw[u][q][:], k.ramp[:, 0:P], k.dst_f[:, col], wf[q][:, col],
                                            ALU.is_equal, ALU.mult)
                    m.then_inc(k.ready.sem, 1)
                for u in range(4):
                    step(u, u)
                with v.Fori(1, EB // 4) as j:
                    for u in range(4):
                        step(j * 4 + u, u)

            @block.tensor
            def _(pe):
                clear_banks(pe, k, range(T))
                with pe.Fori(0, EB // 4) as j:
                    own = dst_tiles(pe, k, j * 4)
                    for u in range(4):
                        i, b = j * 4 + u, own[u]
                        pe.wait_ge(k.ready.sem, k.ready.at(1) + i)
                        for q in range(3):
                            m = pe.matmul(k.ps[:, bass.ds(b, 1), :].rearrange("p a n -> p (a n)"), dw[u][q][:],
                                          os_[u][:], start=False, stop=True, skip_group_check=True)
                        m.then_inc(k.mm.sem, 1)
        done((k.mm, EB), (k.ready, EB))
        with nc.Block() as block:
            @block.scalar
            def _(a):
                for t in range(T):
                    m = a.activation(AT[:, t, :], k.ps[:, t, :], ACT.Copy)
                m.then_inc(k.copied.sem, 1)

            @block.tensor
            def _(pe):
                pe.wait_ge(k.copied.sem, k.copied.at(1))
                mm_rows(pe, k, 4, AT, sup).then_inc(k.mm.sem, 1)

            @block.vector
            def _(v):
                ch = Chain(v, k.dve_step)
                for t in range(T):
                    last = v.tensor_tensor(k.X[:, t, :], k.X[:, t, :], bias[:], ALU.add)
                ch.link(last)
                v.wait_ge(k.mm.sem, k.mm.at(1))
                for t in range(T):
                    v.tensor_tensor(k.X[:, t, :], k.X[:, t, :], k.ps[:, T + t, :], ALU.add)
                ch.close()
        done((k.mm, 1), (k.copied, 1))



def expert_choice_ffn(k):
    nc, i_ = k.nc, k.i
    E, CAP, FF = 16, 32, 256
    HT = FF // P
    with ExitStack() as c:
        g = sb(c, k, "g", [P, T, E])
        sw1, sw2 = sb(c, k, "sw1", [P, T, FF]), sb(c, k, "sw2", [P, HT, D])
        sb1, sb2 = sb(c, k, "sb1", [P, HT]), sb(c, k, "sb2", [P, D])
        lg = sb(c, k, "lg", [P, T, E])
        mx, sm = sb(c, k, "mx", [P, T]), sb(c, k, "sm", [P, T])
        pr = sb(c, k, "pr", [E, N])
        val, at = sb(c, k, "val", [E, CAP]), sb(c, k, "at", [E, CAP], U32)
        at_c, atf_c, val_c = sb(c, k, "at_c", [P, T], I32), sb(c, k, "atf_c", [P, T]), sb(c, k, "val_c", [P, T])
        shT = sb(c, k, "shT", [P, HT, N])
        tok, tokT = sb(c, k, "tok", [P, T, D]), sb(c, k, "tokT", [P, T, N])
        yT, y = sb(c, k, "yT", [P, T, N]), sb(c, k, "y", [P, T, D])
        back = sb(c, k, "back", [P, T, N])
        load(k, ((g[:], rows_of(i_["L2_ffn_gate_w"])), (sw1[:], rows_of(i_["L2_ffn_sw1"])),
                 (sw2[:], i_["L2_ffn_sw2"].rearrange("(k p) n -> p k n", p=P)), (sb1[:], i_["sb1"]),
                 (sb2[:], bcast(i_["L2_ffn_sb2"])), (rows_of(k.rows_d), k.N[:])))
        with nc.Block() as block:
            @block.tensor
            def _(pe):
                for t in range(T):
                    for f in range(T):
                        m = pe.matmul(k.ps[:, t, 0:E], k.NT[:, f, t * P:(t + 1) * P], g[:, f, :],
                                      start=(f == 0), stop=(f == T - 1))
                m.then_inc(k.mm.sem, 1)
                for s in range(HT):
                    for f in range(T):
                        m = pe.matmul(k.ps[:, T + s, :], sw1[:, f, s * P:(s + 1) * P], k.NT[:, f, :],
                                      start=(f == 0), stop=(f == T - 1))
                m.then_inc(k.mm.sem, 1)
                pe.wait_ge(k.ready.sem, k.ready.at(2))
                for t in range(T):
                    m = pe.transpose(k.ps[0:E, 6, t * P:(t + 1) * P], lg[:, t, :], k.ident[:])
                m.then_inc(k.mm.sem, 1)

            @block.vector
            def _(v):
                ch = Chain(v, k.dve_step)
                v.wait_ge(k.mm.sem, k.mm.at(1))
                ch.link(v.tensor_reduce(mx[:], k.ps[:, 0:T, 0:E], AX.X, ALU.max))
                for t in range(T):
                    m = v.tensor_scalar(lg[:, t, :], k.ps[:, t, 0:E], mx[:, t:t + 1], None, ALU.subtract)
                m.then_inc(k.ready.sem, 1)
                v.wait_ge(k.copied.sem, k.copied.at(1))
                ch.link(v.tensor_reduce(sm[:], lg[:], AX.X, ALU.add))
                ch.link(v.reciprocal(sm[:], sm[:]))
                for t in range(T):
                    m = v.tensor_scalar(lg[:, t, :], lg[:, t, :], sm[:, t:t + 1], None, ALU.mult)
                m.then_inc(k.ready.sem, 1)
                v.wait_ge(k.mm.sem, k.mm.at(3))
                ch.link(v.tensor_copy(pr[:], k.ps[0:E, 6, :]))
                for q in range(CAP // 8):
                    o = slice(8 * q, 8 * q + 8)
                    ch.link(v.max(val[:, o], pr[:]))
                    ch.link(v.max_index(at[:, o], val[:, o], pr[:]))
                    if q < CAP // 8 - 1:
                        ch.link(v.match_replace(pr[:], val[:, o], pr[:], -1.0))
                v.tensor_copy(sm[0:E, 0:1], val[:, 0:1]).then_inc(k.ready.sem, 1)
                v.wait_ge(k.loaded.sem, k.loaded.at(64))
                ch.link(v.tensor_copy(atf_c[:], at_c[:]))
                for t in range(T):
                    v.tensor_scalar(back[:, t, :], k.ramp_f[:], atf_c[:, t:t + 1], val_c[:, t:t + 1],
                                    ALU.is_equal, ALU.mult)
                ch.close()

            @block.scalar
            def _(a):
                a.wait_ge(k.ready.sem, k.ready.at(1))
                a.activation(lg[:], lg[:], ACT.Exp).then_inc(k.copied.sem, 1)
                a.wait_ge(k.mm.sem, k.mm.at(2))
                for s in range(HT):
                    a.activation(shT[:, s, :], k.ps[:, T + s, :], ACT.Gelu_apprx_tanh, bias=sb1[:, s:s + 1])

            @block.sync
            def _(sp):
                sp.wait_ge(k.ready.sem, k.ready.at(3))
                sp.dma_start(k.at_d.rearrange("(e j) -> e j", e=E), at[:].bitcast(I32)).then_inc(k.loaded.sem, 16)
                sp.dma_start(k.val_d.rearrange("(e j) -> e j", e=E), val[:]).then_inc(k.loaded.sem, 16)
                sp.wait_ge(k.loaded.sem, k.loaded.at(32))
                with nc.allow_non_contiguous_dma(reason="512 words"):
                    sp.dma_start(at_c[:], k.at_d.rearrange("(t p) -> p t", p=P)).then_inc(k.loaded.sem, 16)
                    sp.dma_start(val_c[:], k.val_d.rearrange("(t p) -> p t", p=P)).then_inc(k.loaded.sem, 16)

            @block.gpsimd
            def _(gp):
                gp.wait_ge(k.loaded.sem, k.loaded.at(64))
                for t in range(T):
                    gp.indirect_dma_start(tok[:, t, :], None, k.rows_d,
                                          bass.IndirectOffsetOnAxis(ap=at_c[:, t:t + 1].bitcast(U32), axis=0)
                                          ).then_inc(k.gathered.sem, 16)
                gp.wait_ge(k.gathered.sem, k.gathered.at(16 * T))
        done((k.mm, 3), (k.ready, 3), (k.copied, 1), (k.loaded, 64), (k.gathered, 16 * T))

        def turn(src, dst):
            with nc.Block() as block:
                @block.tensor
                def _(pe):
                    for f in range(T):
                        for t in range(T):
                            m = pe.transpose(k.ps[:, f, t * P:(t + 1) * P], src[:, t, f * P:(f + 1) * P], k.ident[:])
                        m.then_inc(k.mm.sem, 1)

                @block.vector
                def _(v):
                    for f in (0, 2):
                        v.wait_ge(k.mm.sem, k.mm.at(f + 1))
                        v.tensor_copy(dst[:, f, :], k.ps[:, f, :])

                @block.scalar
                def _(a):
                    for f in (1, 3):
                        a.wait_ge(k.mm.sem, k.mm.at(f + 1))
                        a.activation(dst[:, f, :], k.ps[:, f, :], ACT.Copy)
            done((k.mm, T))

        turn(tok, tokT)
        with ExitStack() as c2:
            W1 = [sb(c2, k, "w1", [P, T, FF]) for _ in range(4)]
            W2 = [sb(c2, k, "w2", [P, HT, D]) for _ in range(4)]
            b1 = [sb(c2, k, "b1", [P, HT]) for _ in range(4)]
            b2 = [sb(c2, k, "b2", [P, T]) for _ in range(4)]
            hT = [sb(c2, k, "hT", [P, HT, CAP]) for _ in range(2)]
            with nc.Block() as block:
                def walk(eng, step):
                    for u in range(4):
                        step(u, u, 0)
                    with eng.Fori(1, E // 4) as j:
                        for u in range(4):
                            step(j * 4 + u, u, j)

                @block.sync
                def _(sp):
                    def step(e, u, j):
                        if later(e, 4):
                            sp.wait_ge(k.heads.sem, k.heads.at(-3) + e)
                        for dst, src in ((W1[u][:], i_["L2_ffn_w1"][bass.ds(e, 1)].rearrange("a (k p) n -> p (a k) n", p=P)),
                                         (b1[u][:], i_["l2b1"][bass.ds(e, 1)].rearrange("a p m -> p (a m)")),
                                         (W2[u][:], i_["L2_ffn_w2"][bass.ds(e, 1)].rearrange("a (k p) n -> p (a k) n", p=P)),
                                         (b2[u][:], i_["l2b2"][bass.ds(e, 1)].rearrange("a p m -> p (a m)"))):
                            sp.dma_start(dst, src).then_inc(k.slot[u].sem, 16)
                    walk(sp, step)

                @block.tensor
                def _(pe):
                    def step(e, u, j):
                        pe.wait_ge(k.slot[u].sem, k.slot[u].at(64) + j * 64)
                        for s in range(HT):
                            for f in range(T):
                                m = pe.matmul(k.ps[:, u, s * CAP:(s + 1) * CAP], W1[u][:, f, s * P:(s + 1) * P],
                                              tokT[:, f, bass.ds(e * CAP, CAP)], start=(f == 0), stop=(f == T - 1))
                        m.then_inc(k.mm.sem, 1)
                        pe.wait_ge(k.copied.sem, k.copied.at(1) + e)
                        if later(e, 4):
                            pe.wait_ge(k.heads.sem, k.heads.at(-3) + e)
                        for t in range(T):
                            for s in range(HT):
                                m = pe.matmul(k.ps[:, 4 + u, t * CAP:(t + 1) * CAP], W2[u][:, s, t * P:(t + 1) * P],
                                              hT[u % 2][:, s, :], start=(s == 0), stop=(s == HT - 1))
                        m.then_inc(k.out.sem, 1)
                    walk(pe, step)

                @block.scalar
                def _(a):
                    def step(e, u, j):
                        a.wait_ge(k.mm.sem, k.mm.at(1) + e)
                        if later(e, 2):
                            a.wait_ge(k.out.sem, k.out.at(-1) + e)
                        for s in range(HT):
                            m = a.activation(hT[u % 2][:, s, :], k.ps[:, u, s * CAP:(s + 1) * CAP],
                                             ACT.Gelu_apprx_tanh, bias=b1[u][:, s:s + 1])
                        m.then_inc(k.copied.sem, 1)
                    walk(a, step)

                @block.vector
                def _(v):
                    def step(e, u, j):
                        v.wait_ge(k.out.sem, k.out.at(1) + e)
                        for t in range(T):
                            m = v.tensor_scalar(yT[:, t, bass.ds(e * CAP, CAP)], k.ps[:, 4 + u, t * CAP:(t + 1) * CAP],
                                                b2[u][:, t:t + 1], None, ALU.add)
                        m.then_inc(k.heads.sem, 1)
                    walk(v, step)
            done((k.heads, E), (k.mm, E), (k.copied, E), (k.out, E), *[(k.slot[u], 16 * E) for u in range(4)])
        turn(yT, y)
        with nc.Block() as block:
            @block.tensor
            def _(pe):
                for t in range(T):
                    for s in range(HT):
                        pe.matmul(k.ps[:, T + t, :], shT[:, s, t * P:(t + 1) * P], sw2[:, s, :],
                                  start=(s == 0), stop=False)
                    for s in range(T):
                        m = pe.matmul(k.ps[:, T + t, :], back[:, s, t * P:(t + 1) * P], y[:, s, :],
                                      start=False, stop=(s == T - 1))
                    m.then_inc(k.mm.sem, 1)

            @block.vector
            def _(v):
                ch = Chain(v, k.dve_step)
                for t in range(T):
                    last = v.tensor_tensor(k.X[:, t, :], k.X[:, t, :], sb2[:], ALU.add)
                ch.link(last)
                for t in range(T):
                    v.wait_ge(k.mm.sem, k.mm.at(t + 1))
                    v.tensor_tensor(k.X[:, t, :], k.X[:, t, :], k.ps[:, T + t, :], ALU.add)
                ch.close()
        done((k.mm, T))



def sage(k):
    nc, i_ = k.nc, k.i
    E = 4
    with ExitStack() as c:
        masks, wt = routing(k, c, k.NT, i_["L3_gnn_gate_W"], i_["L3_gnn_gate_b"], E, "gates", 2)
        wE = sb(c, k, "wE", [P, T, 8])
        A0 = sb(c, k, "A0", [P, T, N])
        H1, PR, o = [sb(c, k, n, [P, T, D]) for n in ("H1", "PR", "o")]
        W = [[sb(c, k, "w", [P, T, D]) for _ in range(4)] for _ in range(2)]
        b0 = [sb(c, k, "b0", [P, T]) for _ in range(2)]
        b1 = [sb(c, k, "b1", [P, D]) for _ in range(2)]
        with nc.Block() as block:
            @block.tensor
            def _(pe):
                mm_cols(pe, k, 0, k.N, k.Cn).then_inc(k.mm.sem, 1)

            @block.scalar
            def _(a):
                a.wait_ge(k.mm.sem, k.mm.at(1))
                for t in range(T):
                    a.activation(A0[:, t, :], k.ps[:, t, :], ACT.Copy)

            @block.vector
            def _(v):
                ch = Chain(v, k.dve_step)
                for t in range(T):
                    ch.link(v.tensor_scalar(wE[:, t, :], masks[:, t, 0, :], wt[:, t, 0:1], None, ALU.mult))
                    ch.link(v.scalar_tensor_tensor(wE[:, t, :], masks[:, t, 1, :], wt[:, t, 1:2], wE[:, t, :],
                                                   ALU.mult, ALU.add))
                ch.close()
        done((k.mm, 1))
        with nc.Block() as block:
            def walk(eng, step):
                for u in range(2):
                    step(u, u, 0)
                with eng.Fori(1, E // 2) as j:
                    for u in range(2):
                        step(j * 2 + u, u, j)

            @block.sync
            def _(sp):
                def step(e, u, j):
                    if later(e, 2):
                        sp.wait_ge(k.heads.sem, k.heads.at(-1) + e)
                    for q, m in enumerate((i_["L3_gnn_Wl"], i_["L3_gnn_Wr"])):
                        for l in range(2):
                            sp.dma_start(W[u][2 * l + q][:], m[bass.ds(e, 1), l].rearrange(
                                "a (k p) n -> p (a k) n", p=P)).then_inc(k.slot[u].sem, 16)
                    sp.dma_start(b0[u][:], i_["sage_b0"][bass.ds(e, 1)].rearrange("a p m -> p (a m)")
                                 ).then_inc(k.slot[u].sem, 16)
                    sp.dma_start(b1[u][:], i_["sage_b1"][bass.ds(e, 1), :].to_broadcast([P, D])
                                 ).then_inc(k.slot[u].sem, 16)
                walk(sp, step)

            @block.tensor
            def _(pe):
                def step(e, u, j):
                    pe.wait_ge(k.slot[u].sem, k.slot[u].at(96) + j * 96)
                    if later(e, 1):
                        pe.wait_ge(k.heads.sem, k.heads.at(0) + e)
                    for t in range(T):
                        for w, x in ((W[u][0], A0), (W[u][1], k.NT)):
                            for f in range(T):
                                m = pe.matmul(k.ps[:, t, :], w[:, f, t * P:(t + 1) * P], x[:, f, :],
                                              start=(f == 0 and x is A0), stop=(f == T - 1 and x is not A0))
                        m.then_inc(k.mm.sem, 1)
                    pe.wait_ge(k.copied.sem, k.copied.at(1) + e)
                    for t in range(T):
                        for f in range(T):
                            m = pe.matmul(k.ps[:, T + t, :], H1[:, f, t * P:(t + 1) * P], W[u][2][:, f, :],
                                          start=(f == 0), stop=(f == T - 1))
                        m.then_inc(k.tp.sem, 1)
                    mm_rows(pe, k, 0, H1, W[u][3], stop=False)
                    pe.wait_ge(k.ready.sem, k.ready.at(1) + e)
                    for t in range(T):
                        for s in range(T):
                            m = pe.matmul(k.ps[:, t, :], k.Cn[:, s, t * P:(t + 1) * P], PR[:, s, :],
                                          start=False, stop=(s == T - 1))
                        m.then_inc(k.out.sem, 1)
                walk(pe, step)

            @block.scalar
            def _(a):
                def step(e, u, j):
                    for t in range(T):
                        a.wait_ge(k.mm.sem, k.mm.at(t + 1) + e * T)
                        m = a.activation(H1[:, t, :], k.ps[:, t, :], ACT.Relu, bias=b0[u][:, t:t + 1])
                    m.then_inc(k.copied.sem, 1)
                walk(a, step)

            @block.vector
            def _(v):
                ch = Chain(v, k.dve_step)

                def step(e, u, j):
                    ch.n, ch.loop = 2 * T * u, j * (4 * T)
                    for t in range(T):
                        v.wait_ge(k.tp.sem, k.tp.at(t + 1) + e * T)
                        m = v.tensor_copy(PR[:, t, :], k.ps[:, T + t, :])
                    m.then_inc(k.ready.sem, 1)
                    for t in range(T):
                        v.wait_ge(k.out.sem, k.out.at(t + 1) + e * T)
                        ch.link(v.tensor_tensor(o[:, t, :], k.ps[:, t, :], b1[u][:], ALU.add))
                        ch.link(v.tensor_scalar(o[:, t, :], o[:, t, :], 0.0, wE[:, t, bass.ds(e, 1)],
                                                ALU.max, ALU.mult))
                        m = v.tensor_tensor(k.X[:, t, :], k.X[:, t, :], o[:, t, :], ALU.add)
                    m.then_inc(k.heads.sem, 1)
                    v.wait_ge(k.heads.sem, k.heads.at(1) + e)
                walk(v, step)
                ch.close(2 * T * E)
        done((k.heads, E), (k.slot[0], 48 * E), (k.slot[1], 48 * E), (k.mm, T * E), (k.copied, E), (k.ready, E),
             (k.tp, T * E), (k.out, T * E))



def program(nc, i, y):
    with ExitStack() as c:
        k = Kernel(nc, i)
        (k.loaded, k.mm, k.ready, k.copied, k.maxed, k.exped, k.probs, k.tp, k.av, k.heads, k.out, k.gathered,
         k.dve_step, k.pool_step) = [Ticker(c.enter_context(nc.semaphore(n))) for n in (
             "loaded", "mm", "ready", "copied", "maxed", "exped", "probs", "tp", "av", "heads", "out", "gathered",
             "dve_step", "pool_step")]
        k.slot = [Ticker(c.enter_context(nc.semaphore(f"slot{j}"))) for j in range(4)]
        k.pool_slot = [Ticker(c.enter_context(nc.semaphore(f"pool_slot{j}"))) for j in range(4)]
        k.pool_stored = [Ticker(c.enter_context(nc.semaphore(f"pool_stored{j}"))) for j in range(2)]
        k.turned = [Ticker(c.enter_context(nc.semaphore(f"turned{j}"))) for j in range(2)]
        k.stored = [Ticker(c.enter_context(nc.semaphore(f"stored{j}"))) for j in range(2)]
        k.ps = c.enter_context(nc.psum_tensor("ps", [P, 8, 512], F32))
        k.psb = k.ps[:].bitcast(BF16)
        k.X, k.N, k.NT, k.Cn = [sb(c, k, n, [P, T, D]) for n in ("X", "N", "NT", "Cn")]
        k.ident, k.ones, k.before = [sb(c, k, n, [P, P]) for n in ("ident", "ones", "before")]
        k.identb = sb(c, k, "identb", [P, P], BF16)
        k.zrow, k.ramp_f = sb(c, k, "zrow", [P, N]), sb(c, k, "ramp_f", [P, N])
        k.ramp, k.ramp_i = sb(c, k, "ramp", [P, N], F16), sb(c, k, "ramp_i", [P, N], I32)
        k.node_i, k.node_f = sb(c, k, "node_i", [P, T], I32), sb(c, k, "node_f", [P, T])
        k.src_i, k.own = sb(c, k, "src_i", [P, EA], I32), sb(c, k, "own", [P, EA], I32)
        k.ew, k.zero16 = sb(c, k, "ew", [P, EB]), sb(c, k, "zero16", [P, N], BF16)
        k.src_f, k.dst_f = sb(c, k, "src_f", [P, EA]), sb(c, k, "dst_f", [P, EA])
        k.ea = sb(c, k, "ea", [P, EA, 2])
        k.inv_deg, k.has_out = sb(c, k, "inv_deg", [P, T]), sb(c, k, "has_out", [P, T])
        k.eps = sb(c, k, "eps", [P, 1])
        G0, G3 = (N + EXPERTS * (P - 1)) // P, (2 * N + EXPERTS * (P - 1)) // P
        k.xl_d = nc.dram_tensor("xl_d", (N, D + 1), F32).ap()
        k.edges_d = nc.dram_tensor("edges_d", (EB * P, WORDS), F32).ap()
        k.rows_d = nc.dram_tensor("rows_d", (N, D), F32).ap()
        k.at_d, k.val_d = nc.dram_tensor("at_d", (N,), I32).ap(), nc.dram_tensor("val_d", (N,), F32).ap()
        spread, result = [nc.dram_tensor(n, (G3 * P, D), F32).ap() for n in ("spread_d", "result_d")]

        with ExitStack() as c0:
            k.C, k.no_edge = [sb(c0, k, n, [P, T, D]) for n in ("C", "no_edge")]
            constants(k)
            with ExitStack() as c_edges:
                edge_slots(k, c_edges)
                adjacency(k)

            layernorm(k, k.X, k.N, k.NT)
            attention(k, dict(Wq=i["L0_gnn_Wq"], Wk=i["L0_gnn_Wk"], Wv=i["L0_gnn_Wv"], Wo=i["L0_gnn_Wo"], bq=i["g_bq"],
                                         bk=i["g_bk"], bv=i["L0_gnn_bv"], bo=i["L0_gnn_bo"]), k.no_edge, k.X, k.X)
        layernorm(k, k.X, k.N, k.NT)
        with ExitStack() as c1:
            O = sb(c1, k, "O", [P, T, D])
            attention(k, dict(Wq=i["L0_ffn_Wq"], Wk=i["L0_ffn_Wk"], Wv=i["L0_ffn_Wv"], Wo=i["L0_ffn_Wo"], bq=i["f_bq"],
                                         bk=i["f_bk"], bv=i["L0_ffn_bv"], bo=i["L0_ffn_bo"]), None, k.N, O)
            with ExitStack() as c2:
                gb = [sb(c2, k, "gb", [P, D]) for _ in range(2)]
                load(k, ((gb[0][:], bcast(i["L0_ffn_ln1_g"])), (gb[1][:], bcast(i["L0_ffn_ln1_b"]))))
                layernorm(k, O, k.N, k.NT, passes=(gb,))
        routed_ffn(k, k.NT, k.N, i["L0_ffn_gate_W"], i["L0_ffn_gate_b"], "top1", 1, G0,
                   dict(W1=i["L0_ffn_W1"], W2=i["L0_ffn_W2"], b1=i["l0b1"], b2=i["L0_ffn_b2"]),
                   2048, False, spread, result)

        layernorm(k, k.X, k.N, k.NT)
        gat(k)
        layernorm(k, k.X, k.N, k.NT)
        positional_ffn(k)

        layernorm(k, k.X, k.N, k.NT)
        graph_conv(k)
        layernorm(k, k.X, k.N, k.NT)
        expert_choice_ffn(k)

        layernorm(k, k.X, k.N, k.NT)
        sage(k)
        layernorm(k, k.X, k.N, k.NT)
        routed_ffn(k, k.NT, k.N, i["router_wT"], None, "top2", 2, G3,
                   dict(Wg=i["L3_ffn_w_gate"], Wu=i["L3_ffn_w_up"], Wd=i["L3_ffn_w_down"]), 1024, True,
                   spread, result)
        store(k, y)


def store(k, y):
    with k.nc.Block() as block:
        @block.sync
        def _(sp):
            sp.dma_start(rows_of(y), k.X[:]).then_inc(k.stored[0].sem, 16)
            sp.wait_ge(k.stored[0].sem, k.stored[0].at(16))



def kernel(**inputs):
    import concourse.bacc as bacc
    from concourse.bass_utils import run_bass_kernel_spmd

    given = {n: np.asarray(a) for n, a in inputs.items()}

    def columns(v, tiles):
        return np.ascontiguousarray(np.swapaxes(v.reshape(*v.shape[:-1], tiles, P), -1, -2))

    def turned(w):
        return np.ascontiguousarray(np.swapaxes(w, -1, -2))

    laid = {
        "g_bq": columns(given["L0_gnn_bq"], T), "g_bk": columns(given["L0_gnn_bk"], T),
        "f_bq": columns(given["L0_ffn_bq"], T), "f_bk": columns(given["L0_ffn_bk"], T),
        "l0b1": columns(given["L0_ffn_b1"], 16), "attn_b": columns(given["L1_ffn_attn_b"], T),
        "attn_wT": turned(given["L1_ffn_attn_w"]), "next_wT": turned(given["L1_ffn_next_w"]),
        "fc1T": turned(given["L1_ffn_fc1_w"]), "fc2T": turned(given["L1_ffn_fc2_w"]),
        "l2b1": columns(given["L2_ffn_b1"], 2), "l2b2": columns(given["L2_ffn_b2"], T),
        "sb1": columns(given["L2_ffn_sb1"], 2),
        "sage_b0": columns(given["L3_gnn_bl"][:, 0], T), "sage_b1": np.ascontiguousarray(given["L3_gnn_bl"][:, 1]),
        "router_wT": turned(given["L3_ffn_router_w"]),
    }
    unused = {"L0_gnn_bq", "L0_gnn_bk", "L0_ffn_bq", "L0_ffn_bk", "L0_ffn_b1", "L1_ffn_attn_b", "L1_ffn_attn_w",
              "L1_ffn_next_w", "L1_ffn_fc1_w", "L1_ffn_fc2_w", "L2_ffn_b1",
              "L2_ffn_b2", "L2_ffn_sb1", "L3_gnn_bl", "L3_ffn_router_w", "L1_ffn_gate_w"}
    laid.update({n: np.ascontiguousarray(a) for n, a in given.items() if n not in unused})
    nc = bacc.Bacc("TRN2", target_bir_lowering=False, num_devices=1)
    i = {n: nc.dram_tensor(n, a.shape, mybir.dt.from_np(a.dtype), kind="ExternalInput").ap()
         for n, a in laid.items()}
    y = nc.dram_tensor("y", (N, D), F32, kind="ExternalOutput").ap()
    program(nc, i, y)
    return run_bass_kernel_spmd(nc, [laid], core_ids=[0]).results[0]["y"]
```

```python
from contextlib import ExitStack

import concourse.bass as bass
import numpy as np
from concourse import mybir

F32 = mybir.dt.float32
F16 = mybir.dt.float16
BF16 = mybir.dt.bfloat16
I32 = mybir.dt.int32
U32 = mybir.dt.uint32
ALU = mybir.AluOpType
ACT = mybir.ActivationFunctionType
AX = mybir.AxisListType

P = 128
N = 512
D = 512
T = N // P
EDGES = 8704
ET = EDGES // P
EB = ET + T
EA = EB + T
WORDS = 8
HEADS = 8
HD = D // HEADS
EXPERTS = 8
NEG = -1e30
EPS = 1e-5
FAR = 2.0 ** 50
DEEP = 8
EX_SCALE = 16384.0


class Ticker:

    def __init__(self, sem):
        self.sem, self.base = sem, 0

    def at(self, n):
        return self.base + n


class Kernel:

    def __init__(self, nc, inputs):
        self.nc, self.i, self.uid = nc, inputs, 0


class Chain:

    def __init__(self, eng, ticker):
        self.eng, self.t, self.n, self.loop = eng, ticker, 0, 0

    def link(self, ins):
        self.n += 1
        ins.then_inc(self.t.sem, 1)
        self.eng.wait_ge(self.t.sem, self.t.at(self.n) + self.loop)

    def close(self, total=None):
        self.t.base += self.n if total is None else total


def later(step, first):
    return not isinstance(step, int) or step >= first


def rows_of(w):
    return w.rearrange("(k p) n -> p k n", p=P)


def bcast(v, n=P):
    return v.rearrange("(a d) -> a d", a=1).to_broadcast([n, v.shape[0]])


def sb(c, k, name, shape, dt=F32):
    k.uid += 1
    return c.enter_context(k.nc.sbuf_tensor(f"{name}_{k.uid}", shape, dt))


def done(*pairs):
    for ticker, n in pairs:
        ticker.base += n



def constants(k):
    with k.nc.Block() as block:
        @block.gpsimd
        def _(gp):
            ch = Chain(gp, k.pool_step)
            gp.memset(k.ident[:], 0.0)
            gp.memset(k.ones[:], 1.0)
            gp.memset(k.eps[:], EPS)
            ch.link(gp.memset(k.zrow[:], 0.0))
            gp.affine_select(out=k.ident[:], in_=k.ident[:], compare_op=ALU.not_equal, fill=1.0,
                             base=0, pattern=[[-1, P]], channel_multiplier=1)
            gp.affine_select(out=k.before[:], in_=k.ones[:], compare_op=ALU.is_gt, fill=0.0,
                             base=0, pattern=[[1, P]], channel_multiplier=-1)
            gp.iota(k.ramp_i[:], pattern=[[1, N]], base=0, channel_multiplier=0)
            ch.link(gp.iota(k.node_i[:], pattern=[[P, T]], base=0, channel_multiplier=1))
            ch.close()

        @block.sync
        def _(sp):
            sp.dma_start(k.X[:], rows_of(k.i["x"])).then_inc(k.loaded.sem, 16)
            sp.wait_ge(k.loaded.sem, k.loaded.at(16))
    done((k.loaded, 16))
    with k.nc.Block() as block:
        @block.vector
        def _(v):
            v.tensor_copy(k.ramp_f[:], k.ramp_i[:])
            v.tensor_copy(k.ramp[:], k.ramp_i[:])
            v.tensor_copy(k.node_f[:], k.node_i[:])
            v.tensor_copy(k.identb[:], k.ident[:])
            v.memset(k.zero16[:], 0.0)


def edge_slots(k, c0):
    nc = k.nc
    k.drawn_src, k.drawn_dst = sb(c0, k, "drawn_src", [P, ET]), sb(c0, k, "drawn_dst", [P, ET])
    k.drawn_ea = ea = sb(c0, k, "drawn_ea", [P, ET, 2])
    k.slots = slot = sb(c0, k, "slots", [P, ET], I32)
    k.payload = pay = sb(c0, k, "payload", [P, ET, WORDS])
    with ExitStack() as c:
        src_i, dst_i = sb(c, k, "src_r", [P, ET], I32), sb(c, k, "dst_r", [P, ET], I32)
        ew = sb(c, k, "ew_r", [P, ET])
        dst = sb(c, k, "dst", [P, ET])
        ge = sb(c, k, "ge", [P, T + 1, ET])
        m, rank = sb(c, k, "m", [P, T, ET]), sb(c, k, "rank", [P, T, ET])
        tot, off, n_b, tiles, end = [sb(c, k, n, [P, T]) for n in ("tot", "off", "n_b", "tiles", "end")]
        junk, starts = sb(c, k, "junk", [P, ET]), sb(c, k, "starts", [P, ET])
        slot_f = sb(c, k, "slot_f", [P, ET])
        own = sb(c, k, "own", [P, EA])
        zero = sb(c, k, "zero", [P, EB * WORDS])
        with nc.Block() as block:
            @block.sync
            def _(sp):
                for to, frm in ((src_i[:], k.i["src"].rearrange("(p j) -> p j", p=P)),
                                (dst_i[:], k.i["dst"].rearrange("(p j) -> p j", p=P)),
                                (ea[:], k.i["edge_attr_2"].rearrange("(p j) c -> p j c", p=P)),
                                (ew[:], k.i["edge_weight"].rearrange("(p j) -> p j", p=P))):
                    sp.dma_start(to, frm).then_inc(k.loaded.sem, 16)
                sp.wait_ge(k.ready.sem, k.ready.at(1))
                sp.dma_start(k.edges_d.rearrange("(p j) c -> p (j c)", p=P), zero[:]).then_inc(k.stored[0].sem, 16)
                sp.wait_ge(k.stored[0].sem, k.stored[0].at(16))

            @block.tensor
            def _(pe):
                pe.wait_ge(k.ready.sem, k.ready.at(2))
                pe.matmul(k.ps[:, 0, 0:T], k.before[:], tot[:], start=True, stop=True)
                pe.matmul(k.ps[:, 1, 0:T], k.ones[:], tot[:], start=True, stop=True).then_inc(k.mm.sem, 1)

            @block.vector
            def _(v):
                ch = Chain(v, k.dve_step)
                v.memset(zero[:], 0.0).then_inc(k.ready.sem, 1)
                v.memset(pay[:], 0.0)
                ch.link(v.tensor_scalar(starts[:], k.ramp_f[:, 0:ET], float(P), None, ALU.mult))
                v.wait_ge(k.loaded.sem, k.loaded.at(64))
                v.tensor_copy(k.drawn_src[:], src_i[:])
                v.tensor_copy(k.drawn_dst[:], dst_i[:])
                ch.link(v.tensor_copy(dst[:], dst_i[:]))
                for b in range(T + 1):
                    last = v.tensor_scalar(ge[:, b, :], dst[:], float(P * b), None, ALU.is_ge)
                ch.link(last)
                ch.link(v.tensor_tensor(m[:], ge[:, 0:T, :], ge[:, 1:T + 1, :], ALU.subtract))
                v.tensor_reduce(tot[:], m[:], AX.X, ALU.add).then_inc(k.ready.sem, 1)
                for b in range(T):
                    last = v.tensor_tensor_scan(rank[:, b, :], k.ones[:, 0:ET], m[:, b, :], 0.0, ALU.mult, ALU.add)
                ch.link(last)
                v.wait_ge(k.mm.sem, k.mm.at(1))
                v.tensor_copy(off[:], k.ps[:, 0, 0:T])
                ch.link(v.tensor_copy(n_b[:], k.ps[:, 1, 0:T]))
                for b in range(T):
                    last = v.tensor_scalar(junk[:], starts[:], n_b[:, b:b + 1], None, ALU.is_lt, ALU.add,
                                           accum_out=tiles[:, b:b + 1])
                    ch.link(last)
                ch.link(v.tensor_tensor_scan(end[:], k.ones[:, 0:T], tiles[:], 0.0, ALU.mult, ALU.add))
                ch.link(v.tensor_tensor(tiles[:], end[:], tiles[:], ALU.subtract))
                ch.link(v.scalar_tensor_tensor(off[:], tiles[:], float(P), off[:], ALU.mult, ALU.add))
                ch.link(v.tensor_tensor(rank[:], rank[:], m[:], ALU.subtract))
                for b in range(T):
                    ch.link(v.scalar_tensor_tensor(rank[:, b, :], rank[:, b, :], off[:, b:b + 1], m[:, b, :],
                                                   ALU.add, ALU.mult))
                ch.link(v.tensor_tensor(slot_f[:], rank[:, 0, :], rank[:, 1, :], ALU.add))
                ch.link(v.tensor_tensor(slot_f[:], slot_f[:], rank[:, 2, :], ALU.add))
                ch.link(v.tensor_tensor(slot_f[:], slot_f[:], rank[:, 3, :], ALU.add))
                ch.link(v.tensor_copy(slot[:], slot_f[:]))
                ch.link(v.tensor_scalar(dst[:], dst[:], 1.0, None, ALU.add))
                for b in range(1, T):
                    ch.link(v.scalar_tensor_tensor(dst[:], ge[:, b, :], -float(P), dst[:], ALU.mult, ALU.add))
                v.tensor_copy(pay[:, :, 0], src_i[:])
                v.tensor_copy(pay[:, :, 1], dst[:])
                v.tensor_copy(pay[:, :, 2:4], ea[:])
                v.tensor_copy(pay[:, :, 4], ew[:])
                ch.link(v.memset(own[:], 0.0))
                for b in range(T - 1):
                    ch.link(v.scalar_tensor_tensor(own[:, 0:EB], k.ramp_f[:, 0:EB], end[:, b:b + 1], own[:, 0:EB],
                                                   ALU.is_ge, ALU.add))
                ch.link(v.tensor_copy(own[:, EB:EA], k.ramp_f[:, 0:T]))
                v.tensor_copy(k.own[:], own[:])
                v.tensor_copy(k.src_f[:, EB:EA], k.node_f[:])
                for t in range(T):
                    v.tensor_copy(k.dst_f[:, EB + t:EB + t + 1], k.node_f[:, 0:1])
                ch.close()
        done((k.loaded, 64), (k.stored[0], 16), (k.ready, 2), (k.mm, 1))


def split3(v, ch, parts, value, rest):
    ch.link(v.tensor_copy(parts[0], value))
    ch.link(v.tensor_tensor(rest, value, parts[0], ALU.subtract))
    ch.link(v.tensor_copy(parts[1], rest))
    ch.link(v.tensor_tensor(rest, rest, parts[1], ALU.subtract))
    ch.link(v.tensor_copy(parts[2], rest))


def clear_banks(pe, k, banks):
    for b in banks:
        m = pe.matmul(k.ps[:, b, :], k.zero16[:, 0:P], k.zero16[:], start=True, stop=True)
    return m


def dst_tiles(eng, k, i, n=4):
    return k.nc.values_load_multi_w_load_instructions(
        k.own[0:1, bass.ds(i, n)], engines=(eng.engine,), min_val=0, max_val=T - 1,
        skip_runtime_bounds_check_because="a sum of three comparisons, and 0..3 for the self loops")[1]


def adjacency(k):
    nc = k.nc
    with ExitStack() as c:
        parts = sb(c, k, "parts", [P, ET, 7], BF16)
        rest = sb(c, k, "rest", [P, ET, 2])
        oh_s = [sb(c, k, "oh_s", [P, N], BF16) for _ in range(2)]
        oh_d = [sb(c, k, "oh_d", [P, N], BF16) for _ in range(2)]
        sums = sb(c, k, "sums", [P, T, 7])
        inv = sb(c, k, "inv", [P, T])
        diag = sb(c, k, "diag", [P, T, P])
        back = sb(c, k, "back", [P, EB, WORDS])
        with nc.Block() as block:
            @block.gpsimd
            def _(gp):
                for j in range(ET):
                    gp.indirect_dma_start(k.edges_d,
                                          bass.IndirectOffsetOnAxis(ap=k.slots[:, j:j + 1].bitcast(U32), axis=0),
                                          k.payload[:, j, :], None).then_inc(k.gathered.sem, 16)

            @block.vector
            def _(v):
                ch = Chain(v, k.dve_step)
                v.memset(parts[:, :, 6:7], 1.0)
                split3(v, ch, [parts[:, :, 2 * j:2 * j + 2] for j in range(3)], k.drawn_ea[:], rest[:])
                ch.close()

                def step(i, u):
                    if later(i, 2):
                        v.wait_ge(k.mm.sem, k.mm.at(i - 1))
                    v.tensor_scalar(oh_s[u][:], k.ramp[:], k.drawn_src[:, bass.ds(i, 1)], None, ALU.is_equal)
                    v.tensor_scalar(oh_d[u][:], k.ramp[:], k.drawn_dst[:, bass.ds(i, 1)], None,
                                    ALU.is_equal).then_inc(k.ready.sem, 1)
                for u in range(2):
                    step(u, u)
                with v.Fori(1, ET // 2) as j:
                    for u in range(2):
                        step(j * 2 + u, u)

            @block.tensor
            def _(pe):
                def step(i, u, first=False, last=False):
                    pe.wait_ge(k.ready.sem, k.ready.at(i + 1))
                    for t in range(T):
                        pe.matmul(k.ps[:, t, :], oh_s[u][:, t * P:(t + 1) * P], oh_d[u][:],
                                  start=first, stop=last)
                    for t in range(T):
                        m = pe.matmul(k.ps[:, T + t, 0:7], oh_d[u][:, t * P:(t + 1) * P],
                                      parts[:, bass.ds(i, 1), :].rearrange("p a c -> p (a c)"),
                                      start=first, stop=last)
                    m.then_inc(k.mm.sem, 1)
                step(0, 0, first=True)
                step(1, 1)
                with pe.Fori(1, ET // 2 - 1) as j:
                    for u in range(2):
                        step(j * 2 + u, u)
                step(ET - 2, 0)
                step(ET - 1, 1, last=True)
        done((k.mm, ET), (k.ready, ET))
        with nc.Block() as block:
            @block.sync
            def _(sp):
                sp.wait_ge(k.gathered.sem, k.gathered.at(16 * ET))
                sp.dma_start(back[:], k.edges_d.rearrange("(j p) c -> p j c", p=P)).then_inc(k.loaded.sem, 16)

            @block.scalar
            def _(a):
                for t in range(T):
                    a.activation(k.C[:, t, :], k.ps[:, t, :], ACT.Copy).then_inc(k.copied.sem, 1)

            @block.vector
            def _(v):
                ch = Chain(v, k.dve_step)
                for t in range(T):
                    last = v.tensor_copy(sums[:, t, :], k.ps[:, T + t, 0:7])
                ch.link(last)
                v.tensor_scalar(k.inv_deg[:], sums[:, :, 6], 1.0, None, ALU.min)
                ch.link(v.tensor_scalar(inv[:], sums[:, :, 6], 1.0, None, ALU.max))
                ch.link(v.reciprocal(inv[:], inv[:]))
                ch.link(v.tensor_tensor(k.inv_deg[:], k.inv_deg[:], inv[:], ALU.mult))
                mean = k.ea[:, EB:EA, :]
                ch.link(v.tensor_tensor(mean, sums[:, :, 0:2], sums[:, :, 2:4], ALU.add))
                ch.link(v.tensor_tensor(mean, mean, sums[:, :, 4:6], ALU.add))
                for t in range(T):
                    v.tensor_scalar(k.ea[:, EB + t, :], k.ea[:, EB + t, :], inv[:, t:t + 1], None, ALU.mult)
                for t in range(T):
                    last = v.tensor_scalar(diag[:, t, :], k.ident[:], k.inv_deg[:, t:t + 1], None, ALU.mult)
                last.then_inc(k.ready.sem, 1)
                v.wait_ge(k.mm.sem, k.mm.at(1))
                v.wait_ge(k.copied.sem, k.copied.at(T))
                for t in range(T):
                    v.tensor_tensor(k.Cn[:, t, :], k.C[:, t, :], k.ps[:, T, :], ALU.mult)
                    v.tensor_scalar(k.no_edge[:, t, :], k.C[:, t, :], 0.0, NEG, ALU.is_equal, ALU.mult)
                ch.link(v.tensor_reduce(k.has_out[:], k.C[:], AX.X, ALU.max))
                ch.link(v.tensor_scalar(k.has_out[:], k.has_out[:], 0.0, None, ALU.is_gt))
                v.wait_ge(k.loaded.sem, k.loaded.at(16))
                v.tensor_copy(k.src_f[:, 0:EB], back[:, :, 0])
                v.tensor_scalar(k.dst_f[:, 0:EB], back[:, :, 1], -1.0, None, ALU.add)
                v.tensor_copy(k.ea[:, 0:EB, :], back[:, :, 2:4])
                ch.link(v.tensor_copy(k.ew[:], back[:, :, 4]))
                ch.link(v.tensor_copy(k.src_i[:], k.src_f[:]))
                ch.close()

            @block.tensor
            def _(pe):
                pe.wait_ge(k.ready.sem, k.ready.at(1))
                for t in range(T):
                    m = pe.matmul(k.ps[:, T, t * P:(t + 1) * P], k.ones[:], diag[:, t, :], start=True, stop=True)
                m.then_inc(k.mm.sem, 1)
        done((k.mm, 1), (k.ready, 1), (k.copied, T), (k.loaded, 16), (k.gathered, 16 * ET))



def layernorm(k, x, rows, cols, gain=None, relu=False, early=None):
    nc = k.nc
    with ExitStack() as c:
        stats = sb(c, k, "stats", [P, T, 6])
        mv = sb(c, k, "mv", [P, T, 2])
        rstd = sb(c, k, "rstd", [P, T])
        with nc.Block() as block:
            if early is not None:
                @block.sync
                def _(sp):
                    early(sp)

            @block.vector
            def _(v):
                ch = Chain(v, k.dve_step)
                for t in range(T):
                    last = v.bn_stats(stats[:, t, :], x[:, t, :])
                ch.link(last)
                for t in range(T):
                    last = v.bn_aggr(mv[:, t, :], stats[:, t, :])
                last.then_inc(k.ready.sem, 1)
                v.wait_ge(k.copied.sem, k.copied.at(1))
                ch.link(v.reciprocal(rstd[:], rstd[:]))
                steps = [lambda t: v.tensor_scalar(rows[:, t, :], x[:, t, :], mv[:, t, 0:1], rstd[:, t:t + 1],
                                                   ALU.subtract, ALU.mult)]
                if gain:
                    steps += [lambda t: v.tensor_tensor(rows[:, t, :], rows[:, t, :], gain[0][:], ALU.mult),
                              lambda t: v.tensor_tensor(rows[:, t, :], rows[:, t, :], gain[1][:], ALU.add)]
                if relu:
                    steps += [lambda t: v.tensor_scalar(rows[:, t, :], rows[:, t, :], 0.0, None, ALU.max)]
                for step in steps[:-1]:
                    for t in range(T):
                        last = step(t)
                    ch.link(last)
                for t in range(T):
                    steps[-1](t).then_inc(k.tp.sem, 1)
                for f in (1, 3):
                    v.wait_ge(k.mm.sem, k.mm.at(f + 1))
                    v.tensor_copy(cols[:, f, :], k.ps[:, f, :])
                ch.close()

            @block.scalar
            def _(a):
                a.wait_ge(k.ready.sem, k.ready.at(1))
                a.activation(rstd[:], mv[:, :, 1], ACT.Sqrt, bias=k.eps[:, 0:1]).then_inc(k.copied.sem, 1)
                for f in (0, 2):
                    a.wait_ge(k.mm.sem, k.mm.at(f + 1))
                    a.activation(cols[:, f, :], k.ps[:, f, :], ACT.Copy)

            @block.tensor
            def _(pe):
                for t in range(T):
                    pe.wait_ge(k.tp.sem, k.tp.at(t + 1))
                    for f in range(T):
                        m = pe.transpose(k.ps[:, f, t * P:(t + 1) * P], rows[:, t, f * P:(f + 1) * P], k.ident[:])
                        if t == T - 1:
                            m.then_inc(k.mm.sem, 1)
        done((k.ready, 1), (k.copied, 1), (k.mm, T), (k.tp, T))


def mm_rows(pe, k, bank, cols, w, start=True, stop=True):
    for t in range(T):
        for f in range(T):
            m = pe.matmul(k.ps[:, bank + t, :], cols[:, f, t * P:(t + 1) * P], w[:, f, :],
                          start=start and f == 0, stop=stop and f == T - 1)
    return m


def mm_cols(pe, k, bank, w, cols, start=True, stop=True):
    for t in range(T):
        for f in range(T):
            m = pe.matmul(k.ps[:, bank + t, :], w[:, f, t * P:(t + 1) * P], cols[:, f, :],
                          start=start and f == 0, stop=stop and f == T - 1)
    return m



def attention(k, w, mask, base, out):
    nc = k.nc
    with ExitStack() as c:
        W = [sb(c, k, f"w{j}", [P, T, D]) for j in range(4)]
        QT, KT, V, OT = [sb(c, k, n, [P, T, D]) for n in ("qt", "kt", "v", "ot")]
        bq, bk = sb(c, k, "bq", [P, T]), sb(c, k, "bk", [P, T])
        bv, bo = sb(c, k, "bv", [P, D]), sb(c, k, "bo", [P, D])
        E = [sb(c, k, "e", [P, T, N]) for _ in range(2)]
        PT = sb(c, k, "pt", [P, T, N])
        mx, den = sb(c, k, "mx", [P, 2, T]), sb(c, k, "den", [P, 2, T])

        def weights(sp):
            for dst, src in ((bq[:], w["bq"]), (bk[:], w["bk"]), (bv[:], bcast(w["bv"])), (bo[:], bcast(w["bo"]))):
                sp.dma_start(dst, src).then_inc(k.loaded.sem, 16)
            for j, m in enumerate((w["Wq"], w["Wk"], w["Wv"], w["Wo"])):
                sp.dma_start(W[j][:], rows_of(m)).then_inc(k.slot[j].sem, 16)
        layernorm(k, k.X, k.N, k.NT, early=weights)
        with nc.Block() as block:
            @block.tensor
            def _(pe):
                pe.wait_ge(k.slot[0].sem, k.slot[0].at(16))
                mm_cols(pe, k, 0, W[0], k.NT).then_inc(k.mm.sem, 1)
                pe.wait_ge(k.slot[1].sem, k.slot[1].at(16))
                mm_cols(pe, k, 4, W[1], k.NT).then_inc(k.mm.sem, 1)
                pe.wait_ge(k.slot[2].sem, k.slot[2].at(16))
                pe.wait_ge(k.copied.sem, k.copied.at(1))
                mm_rows(pe, k, 0, k.NT, W[2]).then_inc(k.mm.sem, 1)

            @block.vector
            def _(v):
                v.wait_ge(k.loaded.sem, k.loaded.at(64))
                v.wait_ge(k.mm.sem, k.mm.at(1))
                for t in range(T):
                    m = v.tensor_scalar(QT[:, t, :], k.ps[:, t, :], bq[:, t:t + 1], HD ** -0.5, ALU.add, ALU.mult)
                m.then_inc(k.copied.sem, 1)
                for t in range(T):
                    v.tensor_tensor(out[:, t, :], base[:, t, :], bo[:], ALU.add)
                v.wait_ge(k.mm.sem, k.mm.at(3))
                for t in range(T):
                    v.tensor_tensor(V[:, t, :], k.ps[:, t, :], bv[:], ALU.add)

            @block.scalar
            def _(a):
                a.wait_ge(k.loaded.sem, k.loaded.at(64))
                a.wait_ge(k.mm.sem, k.mm.at(2))
                for t in range(T):
                    a.activation(KT[:, t, :], k.ps[:, T + t, :], ACT.Identity, bias=bk[:, t:t + 1])
        done((k.loaded, 64), (k.mm, 3), (k.copied, 1), (k.slot[0], 16), (k.slot[1], 16), (k.slot[2], 16))

        with nc.Block() as block:
            @block.tensor
            def _(pe):
                def scores(h):
                    lo, f = (h % 2) * HD, h // 2
                    for t in range(T):
                        if h:
                            pe.wait_ge(k.ready.sem, k.ready.at(T * (h - 1) + t + 1))
                        pe.matmul(k.ps[:, t, :], QT[lo:lo + HD, f, t * P:(t + 1) * P], KT[lo:lo + HD, f, :],
                                  start=True, stop=True).then_inc(k.mm.sem, 1)

                def weigh(h):
                    lo, f = (h % 2) * HD, h // 2
                    pe.wait_ge(k.probs.sem, k.probs.at(h + 1))
                    for m in range(T):
                        if h or m >= 2:
                            n = T * h + m - 2
                            q = k.turned[m % 2]
                            pe.wait_ge(q.sem, q.at(n // 2 + 1))
                        for t in range(T):
                            i = pe.transpose(k.ps[:, 4 + m % 2, t * P:(t + 1) * P],
                                             E[h % 2][:, t, m * P:(m + 1) * P], k.ident[:])
                        i.then_inc(k.tp.sem, 1)
                    if h % 2 == 0 and h >= 4:
                        pe.wait_ge(k.heads.sem, k.heads.at(h // 2 - 1))
                    for m in range(T):
                        q = k.turned[m % 2]
                        pe.wait_ge(q.sem, q.at(2 * h + m // 2 + 1))
                        i = pe.matmul(k.ps[lo:lo + HD, 6 + f % 2, :], V[:, m, h * HD:(h + 1) * HD], PT[:, m, :],
                                      start=(m == 0), stop=(m == T - 1))
                    i.then_inc(k.av.sem, 1)
                scores(0)
                for h in range(HEADS):
                    if h + 1 < HEADS:
                        scores(h + 1)
                    weigh(h)
                pe.wait_ge(k.slot[3].sem, k.slot[3].at(16))
                pe.wait_ge(k.heads.sem, k.heads.at(HEADS // 2))
                mm_rows(pe, k, 0, OT, W[3]).then_inc(k.mm.sem, 1)

            @block.vector
            def _(v):
                ch = Chain(v, k.dve_step)

                def maxima(h):
                    s = h % 2
                    if h >= 2:
                        v.wait_ge(k.tp.sem, k.tp.at(T * (h - 1)))
                    for t in range(T):
                        v.wait_ge(k.mm.sem, k.mm.at(T * h + t + 1))
                        last = v.tensor_tensor_reduce(E[s][:, t, :], k.ps[:, t, :],
                                                      mask[:, t, :] if mask is not None else k.zrow[:],
                                                      1.0, -3e38, ALU.add, ALU.max, mx[:, s, t:t + 1])
                        last.then_inc(k.ready.sem, 1)
                    v.wait_ge(k.ready.sem, k.ready.at(T * (h + 1)))
                    v.tensor_scalar(mx[:, s, :], mx[:, s, :], -1.0, None, ALU.mult).then_inc(k.maxed.sem, 1)

                def norm(h):
                    s = h % 2
                    v.wait_ge(k.exped.sem, k.exped.at(h + 1))
                    ch.link(v.reciprocal(den[:, s, :], den[:, s, :]))
                    if mask is not None:
                        ch.link(v.tensor_tensor(den[:, s, :], den[:, s, :], k.has_out[:], ALU.mult))
                    for t in range(T):
                        last = v.tensor_scalar(E[s][:, t, :], E[s][:, t, :], den[:, s, t:t + 1], None, ALU.mult)
                    last.then_inc(k.probs.sem, 1)

                def turn(h):
                    for m in (1, 3):
                        v.wait_ge(k.tp.sem, k.tp.at(T * h + m + 1))
                        if h:
                            v.wait_ge(k.av.sem, k.av.at(h))
                        v.tensor_copy(PT[:, m, :], k.ps[:, 5, :]).then_inc(k.turned[1].sem, 1)
                maxima(0)
                for h in range(HEADS):
                    norm(h)
                    if h + 1 < HEADS:
                        maxima(h + 1)
                    turn(h)
                v.wait_ge(k.mm.sem, k.mm.at(T * HEADS + 1))
                for t in range(T):
                    v.tensor_tensor(out[:, t, :], out[:, t, :], k.ps[:, t, :], ALU.add)
                ch.close()

            @block.scalar
            def _(a):
                for h in range(HEADS):
                    s = h % 2
                    a.wait_ge(k.maxed.sem, k.maxed.at(h + 1))
                    for t in range(T):
                        i = a.activation(E[s][:, t, :], E[s][:, t, :], ACT.Exp, bias=mx[:, s, t:t + 1],
                                         accum_out=den[:, s, t:t + 1])
                    i.then_inc(k.exped.sem, 1)
                    for m in (0, 2):
                        a.wait_ge(k.tp.sem, k.tp.at(T * h + m + 1))
                        if h:
                            a.wait_ge(k.av.sem, k.av.at(h))
                        a.activation(PT[:, m, :], k.ps[:, 4, :], ACT.Copy).then_inc(k.turned[0].sem, 1)
                    if h % 2:
                        a.wait_ge(k.av.sem, k.av.at(h + 1))
                        a.activation(OT[:, h // 2, :], k.ps[:, 6 + (h // 2) % 2, :],
                                     ACT.Copy).then_inc(k.heads.sem, 1)
        done((k.mm, T * HEADS + 1), (k.ready, T * HEADS), (k.maxed, HEADS), (k.exped, HEADS), (k.probs, HEADS),
             (k.tp, T * HEADS), (k.turned[0], 2 * HEADS), (k.turned[1], 2 * HEADS), (k.av, HEADS),
             (k.heads, HEADS // 2), (k.slot[3], 16))



def routing(k, c, cols, gate, bias, width, how, choices):
    nc = k.nc
    g = sb(c, k, "gate", [P, T, width])
    gb = sb(c, k, "gate_b", [P, width])
    lg = sb(c, k, "lg", [P, T, 8])
    mx = sb(c, k, "lmx", [P, T])
    sm = sb(c, k, "lsm", [P, T])
    top = sb(c, k, "top", [P, T, 8])
    at = sb(c, k, "at", [P, T, 8], U32)
    atf = sb(c, k, "atf", [P, T, 8])
    masks = sb(c, k, "masks", [P, T, choices, 8])
    wt = sb(c, k, "wt", [P, T, choices])
    with nc.Block() as block:
        @block.sync
        def _(sp):
            sp.dma_start(g[:], rows_of(gate)).then_inc(k.loaded.sem, 16)
            if bias is not None:
                sp.dma_start(gb[:], bcast(bias)).then_inc(k.loaded.sem, 16)

        @block.tensor
        def _(pe):
            pe.wait_ge(k.loaded.sem, k.loaded.at(32 if bias is not None else 16))
            for t in range(T):
                for f in range(T):
                    m = pe.matmul(k.ps[:, t, 0:width], cols[:, f, t * P:(t + 1) * P], g[:, f, :],
                                  start=(f == 0), stop=(f == T - 1))
            m.then_inc(k.mm.sem, 1)

        @block.vector
        def _(v):
            ch = Chain(v, k.dve_step)
            if width < 8:
                ch.link(v.memset(lg[:], NEG))
            v.wait_ge(k.mm.sem, k.mm.at(1))
            for t in range(T):
                if bias is not None:
                    last = v.tensor_tensor(lg[:, t, 0:width], k.ps[:, t, 0:width], gb[:], ALU.add)
                else:
                    last = v.tensor_copy(lg[:, t, 0:width], k.ps[:, t, 0:width])
            ch.link(last)
            if how != "top2":
                ch.link(v.tensor_reduce(mx[:], lg[:], AX.X, ALU.max))
                ch.link(v.tensor_scalar(mx[:], mx[:], -1.0, None, ALU.mult))
                for t in range(T):
                    last = v.tensor_scalar(lg[:, t, :], lg[:, t, :], mx[:, t:t + 1], None, ALU.add)
                last.then_inc(k.ready.sem, 1)
                v.wait_ge(k.copied.sem, k.copied.at(1))
                ch.link(v.tensor_reduce(sm[:], lg[:], AX.X, ALU.add))
                ch.link(v.reciprocal(sm[:], sm[:]))
                for t in range(T):
                    last = v.tensor_scalar(lg[:, t, :], lg[:, t, :], sm[:, t:t + 1], None, ALU.mult)
                ch.link(last)
            for t in range(T):
                last = v.max(top[:, t, :], lg[:, t, :])
            ch.link(last)
            for t in range(T):
                last = v.max_index(at[:, t, :], top[:, t, :], lg[:, t, :])
            ch.link(last)
            ch.link(v.tensor_copy(atf[:], at[:]))
            for t in range(T):
                for q in range(choices):
                    last = v.tensor_scalar(masks[:, t, q, :], k.ramp_f[:, 0:8], atf[:, t, q:q + 1], None,
                                           ALU.is_equal)
            ch.link(last)
            if how != "top2":
                ch.link(v.tensor_copy(wt[:], top[:, :, 0:choices]))
            else:
                v.tensor_tensor(sm[:], top[:, :, 1], top[:, :, 0], ALU.subtract).then_inc(k.ready.sem, 1)
                v.wait_ge(k.copied.sem, k.copied.at(1))
                ch.link(v.tensor_scalar(sm[:], mx[:], 1.0, None, ALU.add))
                ch.link(v.reciprocal(wt[:, :, 0], sm[:]))
                ch.link(v.tensor_tensor(wt[:, :, 1], wt[:, :, 0], mx[:], ALU.mult))
            ch.close()

        @block.scalar
        def _(a):
            a.wait_ge(k.ready.sem, k.ready.at(1))
            if how != "top2":
                a.activation(lg[:], lg[:], ACT.Exp).then_inc(k.copied.sem, 1)
            else:
                a.activation(mx[:], sm[:], ACT.Exp).then_inc(k.copied.sem, 1)
    done((k.loaded, 32 if bias is not None else 16), (k.mm, 1), (k.ready, 1), (k.copied, 1))
    return masks, wt


def empty_slots(k, granules, spread):
    def fill(sp):
        for g in range(granules):
            sp.dma_start(spread[g * P:(g + 1) * P, :], k.zrow[:]).then_inc(k.stored[1].sem, 16)
        sp.wait_ge(k.stored[1].sem, k.stored[1].at(16 * granules))
    return fill


def dispatch(k, c, masks, choices, granules, rows, spread):
    nc = k.nc
    m = sb(c, k, "m", [P, T, EXPERTS])
    pos = sb(c, k, "pos", [P, T, EXPERTS])
    n_e = sb(c, k, "n_e", [P, EXPERTS])
    g_e = sb(c, k, "g_e", [P, EXPERTS])
    end = sb(c, k, "end", [P, EXPERTS])
    own = sb(c, k, "own", [P, granules + 1])
    own_i = sb(c, k, "own_i", [P, granules + 1], I32)
    pick = sb(c, k, "pick", [P, T, EXPERTS])
    slot_f = sb(c, k, "slot_f", [P, T, choices])
    slot = sb(c, k, "slot", [P, T, choices], I32)
    with nc.Block() as block:
        @block.vector
        def _(v):
            ch = Chain(v, k.dve_step)
            if choices == 1:
                v.tensor_copy(m[:], masks[:, :, 0, :]).then_inc(k.ready.sem, 1)
            else:
                v.tensor_tensor(m[:], masks[:, :, 0, :], masks[:, :, 1, :], ALU.add).then_inc(k.ready.sem, 1)
            v.wait_ge(k.mm.sem, k.mm.at(1))
            for t in range(T):
                v.tensor_copy(pos[:, t, :], k.ps[:, t, 0:EXPERTS])
            ch.link(v.tensor_copy(n_e[:], k.ps[:, T, 0:EXPERTS]))
            ch.link(v.tensor_scalar(g_e[:], n_e[:], 0.0, None, ALU.is_gt))
            for j in range(1, T):
                ch.link(v.scalar_tensor_tensor(g_e[:], n_e[:], float(P * j), g_e[:], ALU.is_gt, ALU.add))
            ch.link(v.tensor_tensor_scan(end[:], k.ones[:, 0:EXPERTS], g_e[:], 0.0, ALU.mult, ALU.add))
            ch.link(v.tensor_tensor(g_e[:], end[:], g_e[:], ALU.subtract))
            for t in range(T):
                last = v.scalar_tensor_tensor(pos[:, t, :], g_e[:], float(P), pos[:, t, :], ALU.mult, ALU.add)
            ch.link(last)
            for q in range(choices):
                ch.link(v.tensor_tensor(pick[:], masks[:, :, q, :], pos[:], ALU.mult))
                ch.link(v.tensor_reduce(slot_f[:, :, q], pick[:], AX.X, ALU.add))
            v.tensor_copy(slot[:], slot_f[:]).then_inc(k.copied.sem, 1)
            ch.link(v.memset(own[:], 0.0))
            for e in range(EXPERTS):
                ch.link(v.scalar_tensor_tensor(own[:], k.ramp_f[:, 0:granules + 1], end[:, e:e + 1], own[:],
                                               ALU.is_ge, ALU.add))
            ch.link(v.tensor_scalar(own[:], own[:], float(EXPERTS - 1), None, ALU.min))
            ch.link(v.tensor_copy(own[:, granules:granules + 1], end[:, EXPERTS - 1:EXPERTS]))
            ch.link(v.tensor_copy(own_i[:], own[:]))
            ch.close()

        @block.tensor
        def _(pe):
            pe.wait_ge(k.ready.sem, k.ready.at(1))
            for t in range(T):
                for s in range(t + 1):
                    pe.matmul(k.ps[:, t, 0:EXPERTS], k.before[:] if s == t else k.ones[:], m[:, s, :],
                              start=(s == 0), stop=(s == t))
            for s in range(T):
                i = pe.matmul(k.ps[:, T, 0:EXPERTS], k.ones[:], m[:, s, :], start=(s == 0), stop=(s == T - 1))
            i.then_inc(k.mm.sem, 1)

        @block.gpsimd
        def _(gp):
            gp.wait_ge(k.copied.sem, k.copied.at(1))
            for q in range(choices):
                for t in range(T):
                    gp.indirect_dma_start(spread, bass.IndirectOffsetOnAxis(ap=slot[:, t, q:q + 1].bitcast(U32), axis=0),
                                          rows[:, t, :], None).then_inc(k.gathered.sem, 16)
            gp.wait_ge(k.gathered.sem, k.gathered.at(16 * T * choices))
    done((k.ready, 1), (k.mm, 1), (k.copied, 1), (k.gathered, 16 * T * choices))
    return slot, own_i


def experts(k, c, granules, own, spread, result, w, hidden, gated):
    nc = k.nc
    HT = hidden // P
    ins = 2 if gated else 1
    least = N * ins // P
    half = hidden // 2
    W1 = [[sb(c, k, "w1", [P, T, hidden]) for _ in range(ins)] for _ in range(2)]
    W2 = [sb(c, k, "w2", [P, HT, D]) for _ in range(2)]
    b1 = [sb(c, k, "b1", [P, HT]) for _ in range(2)]
    b2 = [sb(c, k, "b2", [P, D]) for _ in range(2)]
    tok = [sb(c, k, "tok", [P, D]) for _ in range(2)]
    tokT = sb(c, k, "tokT", [P, T, P])
    hT = sb(c, k, "hT", [P, HT, P])
    act = sb(c, k, "act", [P, T * P]) if gated else None
    y = [sb(c, k, "y", [P, D]) for _ in range(2)]
    QT_ = HT // T
    first = [k.slot[u] for u in range(2)]
    second = [k.slot[2 + u] for u in range(2)]
    third = [k.slot[4 + u] for u in range(2)]
    n_first, n_second, n_third = (48, 32, 16) if gated else (48, 16, 32)

    def walk(eng, step):
        step(0, 0, 0)
        step(1, 1, 0)
        with eng.Fori(1, granules // 2) as j:
            for u in range(2):
                step(j * 2 + u, u, j)
        if granules % 2:
            step(granules - 1, 0, granules // 2)

    def used_granules(eng):
        return eng.value_load(own[0:1, granules:granules + 1], min_val=least, max_val=granules)

    with nc.Block() as block:
        @block.sync
        def _(sp):
            used = used_granules(sp)

            def loads(g, u, j):
                e = sp.value_load(own[0:1, bass.ds(g, 1)], min_val=0, max_val=EXPERTS - 1)
                src = ((w["Wg"], w["Wu"]) if gated else (w["W1"],))
                if later(g, 2):
                    sp.wait_ge(k.heads.sem, k.heads.at(-1) + g)
                sp.dma_start(tok[u][:], spread[bass.ds(g * P, P), :]).then_inc(first[u].sem, 16)
                if not gated:
                    sp.dma_start(b1[u][:], w["b1"][bass.ds(e, 1)].rearrange("a p m -> p (a m)")
                                 ).then_inc(first[u].sem, 16)
                for at, ticker in ((0, first[u]), (half, second[u])):
                    for q in range(ins):
                        sp.dma_start(W1[u][q][:, :, at:at + half], src[q][bass.ds(e, 1)].rearrange(
                            "a (k p) n -> p (a k) n", p=P)[:, :, at:at + half]).then_inc(ticker.sem, 16)
                sp.dma_start(W2[u][:], (w["Wd"] if gated else w["W2"])[bass.ds(e, 1)].rearrange(
                    "a (k p) n -> p (a k) n", p=P)).then_inc(third[u].sem, 16)
                if not gated:
                    sp.dma_start(b2[u][:], w["b2"][bass.ds(e, 1), :].to_broadcast([P, D])
                                 ).then_inc(third[u].sem, 16)

            def step(g, u, j):
                if not later(g, least):
                    return loads(g, u, j)
                with sp.If(g < used):
                    loads(g, u, j)
                with sp.Else():
                    sp.wait_ge(k.heads.sem, k.heads.at(-1) + g)
                    sp.sem_inc(first[u].sem, n_first)
                    sp.sem_inc(second[u].sem, n_second)
                    sp.sem_inc(third[u].sem, n_third)
            walk(sp, step)

        @block.tensor
        def _(pe):
            used = used_granules(pe)

            def products(g, u, j):
                pe.wait_ge(first[u].sem, first[u].at(n_first) + j * n_first)
                for f in range(T):
                    m = pe.transpose(k.ps[:, 0, f * P:(f + 1) * P], tok[u][:, f * P:(f + 1) * P], k.ident[:])
                m.then_inc(k.tp.sem, 1)
                pe.wait_ge(k.turned[0].sem, k.turned[0].at(1) + g)
                for q in range(QT_):
                    if q == QT_ // 2:
                        pe.wait_ge(second[u].sem, second[u].at(n_second) + j * n_second)
                    for i in range(ins):
                        b = 1 + (q * ins + i) % 4
                        lag = q * ins + i - 4
                        if lag >= 0:
                            pe.wait_ge(k.copied.sem, k.copied.at(lag // ins + 1) + g * QT_)
                        for s in range(T):
                            for f in range(T):
                                m = pe.matmul(k.ps[:, b, s * P:(s + 1) * P],
                                              W1[u][i][:, f, (q * T + s) * P:(q * T + s + 1) * P],
                                              tokT[:, f, :], start=(f == 0), stop=(f == T - 1))
                    m.then_inc(k.mm.sem, 1)
                pe.wait_ge(third[u].sem, third[u].at(n_third) + j * n_third)
                if later(g, 2):
                    pe.wait_ge(k.heads.sem, k.heads.at(-1) + g)
                for s in range(HT):
                    if s % T == 0:
                        pe.wait_ge(k.copied.sem, k.copied.at(s // T + 1) + g * QT_)
                    m = pe.matmul(k.ps[:, 5 + u, :], hT[:, s, :], W2[u][:, s, :], start=(s == 0), stop=(s == HT - 1))
                m.then_inc(k.out.sem, 1)

            def step(g, u, j):
                if not later(g, least):
                    return products(g, u, j)
                with pe.If(g < used):
                    products(g, u, j)
                with pe.Else():
                    pe.wait_ge(k.out.sem, k.out.at(0) + g)
                    pe.sem_inc(k.tp.sem, 1)
                    pe.sem_inc(k.mm.sem, QT_)
                    pe.sem_inc(k.out.sem, 1)
            walk(pe, step)

        @block.scalar
        def _(a):
            used = used_granules(a)
            signal = k.exped if gated else k.copied

            def hidden_tiles(g, u, j):
                if later(g, 1):
                    a.wait_ge(k.out.sem, k.out.at(0) + g)
                for q in range(QT_):
                    a.wait_ge(k.mm.sem, k.mm.at(q + 1) + g * QT_)
                    if gated:
                        if q or later(g, 1):
                            a.wait_ge(k.copied.sem, k.copied.at(q) + g * QT_)
                        a.activation(act[:], k.ps[:, 1 + (q * 2) % 4, :], ACT.Silu).then_inc(k.exped.sem, 1)
                    else:
                        for s in range(T):
                            i = a.activation(hT[:, q * T + s, :], k.ps[:, 1 + q % 4, s * P:(s + 1) * P],
                                             ACT.Gelu_apprx_tanh, bias=b1[u][:, q * T + s:q * T + s + 1])
                        i.then_inc(k.copied.sem, 1)

            def step(g, u, j):
                if not later(g, least):
                    return hidden_tiles(g, u, j)
                with a.If(g < used):
                    hidden_tiles(g, u, j)
                with a.Else():
                    a.wait_ge(signal.sem, signal.at(0) + g * QT_)
                    a.sem_inc(signal.sem, QT_)
            walk(a, step)

        @block.vector
        def _(v):
            used = used_granules(v)

            def rows_of_granule(g, u, j):
                v.wait_ge(k.tp.sem, k.tp.at(1) + g)
                if later(g, 1):
                    v.wait_ge(k.mm.sem, k.mm.at(0) + g * QT_)
                v.tensor_copy(tokT[:].rearrange("p k n -> p (k n)"), k.ps[:, 0, :]).then_inc(k.turned[0].sem, 1)
                if gated:
                    if later(g, 1):
                        v.wait_ge(k.out.sem, k.out.at(0) + g)
                    for q in range(QT_):
                        v.wait_ge(k.exped.sem, k.exped.at(q + 1) + g * QT_)
                        v.tensor_tensor(hT[:, q * T:(q + 1) * T, :].rearrange("p k n -> p (k n)"), act[:],
                                        k.ps[:, 1 + (q * 2 + 1) % 4, :], ALU.mult).then_inc(k.copied.sem, 1)
                v.wait_ge(k.out.sem, k.out.at(1) + g)
                if later(g, 2):
                    v.wait_ge(k.pool_stored[u].sem, k.pool_stored[u].at(0) + j * 16)
                if gated:
                    v.tensor_copy(y[u][:], k.ps[:, 5 + u, :]).then_inc(k.heads.sem, 1)
                else:
                    v.tensor_tensor(y[u][:], k.ps[:, 5 + u, :], b2[u][:], ALU.add).then_inc(k.heads.sem, 1)

            def step(g, u, j):
                if not later(g, least):
                    return rows_of_granule(g, u, j)
                with v.If(g < used):
                    rows_of_granule(g, u, j)
                with v.Else():
                    v.wait_ge(k.heads.sem, k.heads.at(0) + g)
                    v.sem_inc(k.turned[0].sem, 1)
                    if gated:
                        v.sem_inc(k.copied.sem, QT_)
                    v.sem_inc(k.heads.sem, 1)
            walk(v, step)

        @block.gpsimd
        def _(gp):
            def step(g, u, j):
                gp.wait_ge(k.heads.sem, k.heads.at(1) + g)
                gp.dma_start(result[bass.ds(g * P, P), :], y[u][:]).then_inc(k.pool_stored[u].sem, 16)
            for g in range(granules):
                step(g, g % 2, g // 2)
            for u in range(2):
                gp.wait_ge(k.pool_stored[u].sem, k.pool_stored[u].at(16 * ((granules + 1 - u) // 2)))
    n0, n1 = (granules + 1) // 2, granules // 2
    done(*[(t[u], n * (n0, n1)[u]) for t, n in ((first, n_first), (second, n_second), (third, n_third))
           for u in range(2)],
         (k.tp, granules), (k.turned[0], granules),
         (k.mm, QT_ * granules), (k.copied, QT_ * granules), (k.out, granules), (k.heads, granules),
         (k.pool_stored[0], 16 * n0), (k.pool_stored[1], 16 * n1), (k.exped, QT_ * granules if gated else 0))


def combine(k, c, slot, wt, choices, result):
    with k.nc.Block() as block:
        back = [sb(c, k, "back", [P, T, D]) for _ in range(choices)]

        @block.gpsimd
        def _(gp):
            for q in range(choices):
                for t in range(T):
                    gp.indirect_dma_start(back[q][:, t, :], None, result,
                                          bass.IndirectOffsetOnAxis(ap=slot[:, t, q:q + 1].bitcast(U32), axis=0)
                                          ).then_inc(k.gathered.sem, 16)

        @block.vector
        def _(v):
            ch = Chain(v, k.dve_step)
            v.wait_ge(k.gathered.sem, k.gathered.at(16 * T * choices))
            for q in range(choices):
                for t in range(T):
                    last = v.scalar_tensor_tensor(k.X[:, t, :], back[q][:, t, :], wt[:, t, q:q + 1], k.X[:, t, :],
                                                  ALU.mult, ALU.add)
                ch.link(last)
            ch.close()
    done((k.gathered, 16 * T * choices))


def routed_ffn(k, cols, rows, gate, bias, how, choices, granules, w, hidden, gated, spread, result):
    spread, result = spread[0:granules * P, :], result[0:granules * P, :]
    with ExitStack() as c:
        masks, wt = routing(k, c, cols, gate, bias, EXPERTS, how, choices)
        slot, own = dispatch(k, c, masks, choices, granules, rows, spread)
        with ExitStack() as c2:
            experts(k, c2, granules, own, spread, result, w, hidden, gated)
        combine(k, c, slot, wt, choices, result)



def gat_setup(k, c):
    nc = k.nc
    a_part, w_part = (0, 0, 1, 0, 2, 1), (0, 1, 0, 2, 0, 1)
    G4 = 4 * P
    k.oht = sb(c, k, "oht", [P, EA * P], BF16)
    k.eaT = sb(c, k, "eaT", [P, EA * P], BF16)
    k.we = sb(c, k, "we", [P, 3, D], BF16)
    k.dst_far = sb(c, k, "dst_far", [P, EA])
    k.pick = sb(c, k, "pick", [P, EA, 3 * T])
    with ExitStack() as c2:
        oh = sb(c2, k, "oh", [P, EA, P], BF16)
        eap = sb(c2, k, "eap", [P, EA, 12], BF16)
        p3 = [sb(c2, k, "p3", [P, EA, 2], BF16) for _ in range(3)]
        rest, own_f = sb(c2, k, "rest", [P, EA, 2]), sb(c2, k, "own_f", [P, EA])
        w_in, w_rest = sb(c2, k, "w_in", [2, 3, D]), sb(c2, k, "w_rest", [2, 3, D])
        w3 = [sb(c2, k, "w3", [2, 3, D], BF16) for _ in range(3)]
        with nc.Block() as block:
            @block.sync
            def _(sp):
                sp.dma_start(w_in[:], k.i["L1_gnn_We"].rearrange("l c n -> c l n")).then_inc(k.loaded.sem, 16)
                sp.wait_ge(k.ready.sem, k.ready.at(2))
                for j in range(6):
                    sp.dma_start(k.we[2 * j:2 * j + 2, :, :], w3[w_part[j]][:]).then_inc(k.stored[0].sem, 16)
                sp.wait_ge(k.stored[0].sem, k.stored[0].at(96))

            @block.gpsimd
            def _(gp):
                gp.memset(k.we[:], 0.0).then_inc(k.ready.sem, 1)
                gp.memset(k.eaT[:], 0.0).then_inc(k.maxed.sem, 1)

            @block.vector
            def _(v):
                ch = Chain(v, k.dve_step)
                split3(v, ch, [p[:] for p in p3], k.ea[:], rest[:])
                for j in range(6):
                    last = v.tensor_copy(eap[:, :, 2 * j:2 * j + 2], p3[a_part[j]][:])
                last.then_inc(k.probs.sem, 1)
                with v.Fori(0, EA // 4) as j:
                    for u in range(4):
                        i = j * 4 + u
                        m = v.tensor_scalar(oh[:, bass.ds(i, 1), :].rearrange("p a n -> p (a n)"), k.ramp[:, 0:P],
                                            k.dst_f[:, bass.ds(i, 1)], None, ALU.is_equal)
                    m.then_inc(k.copied.sem, 1)
                v.wait_ge(k.loaded.sem, k.loaded.at(16))
                split3(v, ch, [w[:] for w in w3], w_in[:], w_rest[:])
                v.tensor_copy(w_rest[:, 0, 0:1], w3[0][:, 0, 0:1]).then_inc(k.ready.sem, 1)
                ch.link(v.tensor_copy(own_f[:], k.own[:]))
                v.tensor_scalar(k.dst_far[:], k.dst_f[:], -FAR, None, ALU.mult)
                for b in range(T):
                    for q in range(3):
                        v.tensor_scalar(k.pick[:, :, 3 * b + q], own_f[:], float(b), None, ALU.is_equal)
                ch.close()

            @block.tensor
            def _(pe):
                pe.wait_ge(k.probs.sem, k.probs.at(1))
                for q in range(EA // 4):
                    if q >= 2:
                        pe.wait_ge(k.turned[0].sem, k.turned[0].at(q - 1))
                        pe.wait_ge(k.turned[1].sem, k.turned[1].at(q - 1))
                    for u in range(4):
                        m = pe.transpose(k.psb[0:12, q % 2, u * P:(u + 1) * P], eap[:, 4 * q + u, :], k.identb[:])
                    m.then_inc(k.mm.sem, 1)
                    pe.wait_ge(k.copied.sem, k.copied.at(q + 1))
                    for u in range(4):
                        m = pe.transpose(k.psb[:, 2 + q % 2, u * P:(u + 1) * P], oh[:, 4 * q + u, :], k.identb[:])
                    m.then_inc(k.tp.sem, 1)

            @block.scalar
            def _(a):
                a.wait_ge(k.maxed.sem, k.maxed.at(1))
                for q in range(EA // 4):
                    a.wait_ge(k.mm.sem, k.mm.at(q + 1))
                    a.activation(k.eaT[0:12, q * G4:(q + 1) * G4], k.psb[0:12, q % 2, 0:G4],
                                 ACT.Copy).then_inc(k.turned[0].sem, 1)
                    a.wait_ge(k.tp.sem, k.tp.at(q + 1))
                    a.activation(k.oht[:, q * G4:(q + 1) * G4], k.psb[:, 2 + q % 2, 0:G4],
                                 ACT.Copy).then_inc(k.turned[1].sem, 1)
        done((k.loaded, 16), (k.copied, EA // 4), (k.ready, 2), (k.stored[0], 96), (k.maxed, 1), (k.probs, 1),
             (k.mm, EA // 4), (k.tp, EA // 4), (k.turned[0], EA // 4), (k.turned[1], EA // 4))


def per_edge(pe, k, bank, table):
    h = EA // 2
    for i in range(EA):
        m = pe.matmul(k.ps[:, bank + i // h, i % h * 12:(i % h + 1) * 12], k.oht[:, i * P:(i + 1) * P],
                      table[:].rearrange("p a c -> p (a c)"), start=True, stop=True)
        if i % h == h - 1:
            m.then_inc(k.tp.sem, 1)


def pick_own(v, ch, k, bank, me, prod):
    h = EA // 2
    for half in range(2):
        v.wait_ge(k.tp.sem, k.tp.at(half + 1))
        ch.link(v.tensor_tensor(prod[:, half * h:(half + 1) * h, :], k.ps[:, bank + half, 0:h * 12].rearrange(
            "p (i c) -> p i c", c=12), k.pick[:, half * h:(half + 1) * h, :], ALU.mult))
    ch.link(v.tensor_reduce(me[:], prod[:], AX.X, ALU.add))


def walk_edges(eng, k, step, lag=0):
    def own(i, n):
        return None if lag is None else dst_tiles(eng, k, i - lag if later(i, 1) else i, n)

    def at(tiles, u):
        return None if lag is None or u < 0 else tiles[u:]
    rounds = EA // DEEP
    tiles = own(0, DEEP)
    for u in range(DEEP):
        step(u, u, 0, at(tiles, u - (lag or 0)))
    with eng.Fori(1, rounds) as j:
        tiles = own(j * DEEP, DEEP)
        for u in range(DEEP):
            step(j * DEEP + u, u, j, at(tiles, u))
    first = rounds * DEEP
    tiles = own(first, EA - first + (lag or 0))
    for u in range(EA - first):
        step(first + u, u, rounds, at(tiles, u))
    return tiles


def gat_layer(k, l, norm_before, rows_in, cols_in):
    nc = k.nc
    W1 = D + 1
    XL, H2, att, b_out, eac, L, sdot, me, M, prod, mc, mrest, mp, hi16, XP, ap = (k.gat[n] for n in (
        "XL", "H2", "att", "b_out", "eac", "L", "sdot", "me", "M", "prod", "mc", "mrest", "mp", "hi16", "XP", "ap"))
    with ExitStack() as c:
        with ExitStack() as c2:
            W = [sb(c2, k, "w", [P, T, D]) for _ in range(2)]
            bl, br = sb(c2, k, "bl", [P, D]), sb(c2, k, "br", [P, D])
            web = sb(c2, k, "web", [P, 2, D])

            def weights(sp):
                for dst, src in ((bl[:], bcast(k.i["L1_gnn_bl"][l])), (br[:], bcast(k.i["L1_gnn_br"][l])),
                                 (att[:], bcast(k.i["L1_gnn_att"][l])), (b_out[:], bcast(k.i["L1_gnn_b_out"][l])),
                                 (web[:, 0, :], bcast(k.i["L1_gnn_We"][l, 0])),
                                 (web[:, 1, :], bcast(k.i["L1_gnn_We"][l, 1]))):
                    sp.dma_start(dst, src).then_inc(k.loaded.sem, 16)
                for j, m in enumerate((k.i["L1_gnn_Wl"], k.i["L1_gnn_Wr"])):
                    sp.dma_start(W[j][:], rows_of(m[l])).then_inc(k.slot[j].sem, 16)
            norm_before(weights)
            XR = sb(c2, k, "xr", [P, T, W1])
            wc = sb(c2, k, "wc", [P, 2])
            junk = sb(c2, k, "junk", [P, D])
            with nc.Block() as block:
                @block.sync
                def _(sp):
                    for j, m in enumerate((k.i["L1_gnn_gamma"], k.i["L1_gnn_beta"])):
                        sp.dma_start(k.gat["gb"][j][:], bcast(m[l])).then_inc(k.stored[1].sem, 16)
                    sp.wait_ge(k.probs.sem, k.probs.at(1))
                    sp.dma_start(k.xl_d.rearrange("(k p) n -> p k n", p=P), XL[:]).then_inc(k.stored[0].sem, 16)
                    sp.wait_ge(k.stored[0].sem, k.stored[0].at(16))
                    sp.wait_ge(k.stored[1].sem, k.stored[1].at(32))

                @block.tensor
                def _(pe):
                    for j in range(2):
                        pe.wait_ge(k.slot[j].sem, k.slot[j].at(16))
                        mm_rows(pe, k, 4 * j, cols_in, W[j]).then_inc(k.mm.sem, 1)
                    pe.wait_ge(k.ready.sem, k.ready.at(1))
                    per_edge(pe, k, 0, ap)

                @block.vector
                def _(v):
                    ch = Chain(v, k.dve_step)
                    v.wait_ge(k.loaded.sem, k.loaded.at(96))
                    for q in range(2):
                        ch.link(v.scalar_tensor_tensor(junk[:], web[:, q, :], 0.2, att[:], ALU.mult, ALU.mult,
                                                       accum_out=wc[:, q:q + 1]))
                    ch.link(v.tensor_scalar(eac[:], k.ea[:, :, 0], wc[:, 0:1], None, ALU.mult))
                    v.memset(M[:], -NEG)
                    ch.link(v.scalar_tensor_tensor(eac[:], k.ea[:, :, 1], wc[:, 1:2], eac[:], ALU.mult, ALU.add))
                    for j, (x, b) in enumerate(((XL, bl), (XR, br))):
                        v.wait_ge(k.mm.sem, k.mm.at(j + 1))
                        for t in range(T):
                            last = v.tensor_tensor(x[:, t, 0:D], k.ps[:, 4 * j + t, :], b[:], ALU.add)
                        ch.link(last)
                        for t in range(T):
                            last = v.scalar_tensor_tensor(junk[:], x[:, t, 0:D], 0.2, att[:], ALU.mult, ALU.mult,
                                                          accum_out=x[:, t, D:W1])
                            if t < T - 1:
                                ch.link(last)
                        last.then_inc(k.probs.sem, 1)
                        v.wait_ge(k.probs.sem, k.probs.at(j + 1))
                    split3(v, ch, [ap[:, :, q] for q in range(3)], XR[:, :, D], mrest[:])
                    v.tensor_copy(mrest[:, 0:1], ap[:, 0, 0:1]).then_inc(k.ready.sem, 1)
                    split3(v, ch, [XP[:, q] for q in range(3)], XR[:, :, 0:D], XR[:, :, 0:D])
                    pick_own(v, ch, k, 0, me, prod)
                    ch.link(v.tensor_tensor(eac[:], eac[:], me[:], ALU.add))
                    ch.close()
            done((k.loaded, 96), (k.slot[0], 16), (k.slot[1], 16), (k.stored[0], 16), (k.stored[1], 32), (k.mm, 2), (k.probs, 2),
                 (k.ready, 1), (k.tp, 2))

        with ExitStack() as c2:
            G = [sb(c2, k, "g", [P, W1]) for _ in range(DEEP)]
            r = [sb(c2, k, "r", [P, D]) for _ in range(DEEP)]
            pen = [sb(c2, k, "pen", [P, P], BF16) for _ in range(DEEP)]
            junk = [sb(c2, k, "junk", [P, D]) for _ in range(2)]
            att8 = sb(c2, k, "att8", [P, D])

            with nc.Block() as block:
                @block.gpsimd
                def _(gp):
                    for i in range(EA):
                        if i >= DEEP:
                            gp.wait_ge(k.mm.sem, k.mm.at(i - DEEP + 1))
                            gp.wait_ge(k.probs.sem, k.probs.at(i - DEEP + 1))
                        gp.indirect_dma_start(G[i % DEEP][:], None, k.xl_d,
                                              bass.IndirectOffsetOnAxis(ap=k.src_i[:, i:i + 1].bitcast(U32), axis=0)
                                              ).then_inc(k.pool_slot[i % DEEP].sem, 16)

                @block.tensor
                def _(pe):
                    def step(i, u, j, own):
                        if later(i, DEEP):
                            reader = k.turned[0] if u % 2 else k.copied
                            pe.wait_ge(reader.sem, reader.at(u // 2 + 1 - DEEP // 2) + j * (DEEP // 2))
                        pe.matmul(k.ps[:, u, :], k.eaT[:, bass.ds(i * P, P)], k.we[:, l, :],
                                  start=True, stop=False)
                        for q in range(3):
                            m = pe.matmul(k.ps[:, u, :], k.oht[:, bass.ds(i * P, P)],
                                          XP[:, q, bass.ds(own[0], 1), :].rearrange("p a n -> p (a n)"),
                                          start=False, stop=(q == 2 and u % 2 == 1))
                        if u % 2 == 0:
                            pe.wait_ge(k.pool_slot[u].sem, k.pool_slot[u].at(16) + j * 16)
                            m = pe.matmul(k.ps[:, u, :], k.ident[:], G[u][:, 0:D], start=False, stop=True)
                        m.then_inc(k.mm.sem, 1)
                    walk_edges(pe, k, step)

                @block.scalar
                def _(a):
                    def step(i, u, j, own):
                        if later(i, DEEP):
                            a.wait_ge(k.maxed.sem, k.maxed.at(1 - DEEP) + i)
                        a.activation(pen[u][:], k.ramp[:, 0:P], ACT.Square, scale=FAR,
                                     bias=k.dst_far[:, bass.ds(i, 1)]).then_inc(k.exped.sem, 1)
                        if u % 2 == 0:
                            a.wait_ge(k.mm.sem, k.mm.at(1) + i)
                            a.activation(r[u][:], k.ps[:, u, :], ACT.Relu, scale=0.8).then_inc(k.copied.sem, 1)
                    walk_edges(a, k, step, None)

                @block.vector
                def _(v):
                    ch = Chain(v, k.dve_step)
                    ch.link(v.tensor_scalar(att8[:], att[:], 0.8, None, ALU.mult))

                    def dot(i, u, j):
                        if u % 2:
                            v.wait_ge(k.turned[0].sem, k.turned[0].at(u // 2 + 1) + j * (DEEP // 2))
                            m = v.scalar_tensor_tensor(junk[u % 2][:], r[u][:], 0.0, att8[:], ALU.max, ALU.mult,
                                                       accum_out=sdot[:, bass.ds(i, 1)])
                        else:
                            v.wait_ge(k.copied.sem, k.copied.at(u // 2 + 1) + j * (DEEP // 2))
                            m = v.scalar_tensor_tensor(junk[u % 2][:], r[u][:], 1.0, att[:], ALU.mult, ALU.mult,
                                                       accum_out=sdot[:, bass.ds(i, 1)])
                        m.then_inc(k.dve_step.sem, 1)

                    def logit(i, u):
                        v.wait_ge(k.dve_step.sem, k.dve_step.at(1) + i)
                        v.scalar_tensor_tensor(L[:, bass.ds(i - 1, 1)], G[u][:, D:W1], eac[:, bass.ds(i - 1, 1)],
                                               sdot[:, bass.ds(i - 1, 1)], ALU.add, ALU.add).then_inc(k.probs.sem, 1)

                    def lowest(i, u, own):
                        v.wait_ge(k.probs.sem, k.probs.at(-1) + i)
                        v.wait_ge(k.exped.sem, k.exped.at(-1) + i)
                        if later(i, 3):
                            v.wait_ge(k.maxed.sem, k.maxed.at(-2) + i)
                        low = M[:, bass.ds(own * P, P)]
                        v.scalar_tensor_tensor(low, pen[u][:], L[:, bass.ds(i - 2, 1)], low, ALU.subtract, ALU.min
                                               ).then_inc(k.maxed.sem, 1)

                    def step(i, u, j, own):
                        if u % 2:
                            v.wait_ge(k.mm.sem, k.mm.at(1) + i)
                            v.wait_ge(k.pool_slot[u].sem, k.pool_slot[u].at(16) + j * 16)
                            v.tensor_tensor(r[u][:], k.ps[:, u, :], G[u][:, 0:D], ALU.add
                                            ).then_inc(k.turned[0].sem, 1)
                        if later(i, 2):
                            lowest(i, (u - 2) % DEEP, own[0])
                        dot(i, u, j)
                        if later(i, 1):
                            logit(i, (u - 1) % DEEP)
                    own = walk_edges(v, k, step, 2)
                    lowest(EA, (EA - 2) % DEEP, own[-2])
                    logit(EA, (EA - 1) % DEEP)
                    lowest(EA + 1, (EA - 1) % DEEP, own[-1])
                    ch.close(EA + 1)
            done(*[(k.pool_slot[u], 16 * ((EA - u + DEEP - 1) // DEEP)) for u in range(DEEP)], (k.mm, EA),
                 (k.copied, EA // 2), (k.probs, EA), (k.turned[0], EA // 2), (k.maxed, EA), (k.exped, EA))

        with nc.Block() as block:
            @block.tensor
            def _(pe):
                for t in range(T):
                    m = pe.transpose(k.ps[:, 0, t * P:(t + 1) * P], M[:, t * P:(t + 1) * P], k.ident[:])
                m.then_inc(k.mm.sem, 1)
                pe.wait_ge(k.ready.sem, k.ready.at(1))
                per_edge(pe, k, 1, mp)

            @block.vector
            def _(v):
                ch = Chain(v, k.dve_step)
                v.wait_ge(k.mm.sem, k.mm.at(1))
                ch.link(v.tensor_reduce(mc[:], k.ps[:, 0, :].rearrange("p (t n) -> p t n", t=T), AX.X, ALU.min))
                split3(v, ch, [mp[:, :, q] for q in range(3)], mc[:], mrest[:])
                v.tensor_copy(mrest[:, 0:1], mc[:, 0:1]).then_inc(k.ready.sem, 1)
                pick_own(v, ch, k, 1, me, prod)
                ch.link(v.tensor_tensor(L[:], L[:], me[:], ALU.add))
                v.tensor_scalar(L[:], L[:], 0.0, None, ALU.min).then_inc(k.ready.sem, 1)
                v.wait_ge(k.copied.sem, k.copied.at(1))
                ch.link(v.tensor_scalar(me[:], me[:], EX_SCALE, None, ALU.mult))
                ch.link(v.tensor_copy(hi16[:], me[:]))
                ch.link(v.tensor_copy(L[:], hi16[:]))
                ch.link(v.tensor_tensor(me[:], me[:], L[:], ALU.subtract))
                ch.close()

            @block.scalar
            def _(a):
                a.wait_ge(k.ready.sem, k.ready.at(2))
                a.activation(me[:], L[:], ACT.Exp).then_inc(k.copied.sem, 1)
        done((k.mm, 1), (k.tp, 2), (k.ready, 2), (k.copied, 1))

        with ExitStack() as c2:
            os_ = [sb(c2, k, "os", [P, N], F16) for _ in range(DEEP)]
            dh = [sb(c2, k, "dh", [P, P], F16) for _ in range(DEEP)]
            dl = [sb(c2, k, "dl", [P, P], F16) for _ in range(DEEP)]
            pen = [sb(c2, k, "pen", [P, P], BF16) for _ in range(DEEP)]
            A, AT = sb(c2, k, "A", [P, T, N]), sb(c2, k, "AT", [P, T, N])
            den = sb(c2, k, "den", [P, T])
            with nc.Block() as block:
                @block.vector
                def _(v):
                    def step(i, u, j, own):
                        if later(i, DEEP):
                            v.wait_ge(k.mm.sem, k.mm.at(1 - DEEP) + i)
                        col = bass.ds(i, 1)
                        v.tensor_scalar(os_[u][:], k.ramp[:], k.src_f[:, col], None, ALU.is_equal)
                        v.tensor_scalar(dl[u][:], k.ramp[:, 0:P], k.dst_f[:, col], me[:, col], ALU.is_equal,
                                        ALU.mult).then_inc(k.ready.sem, 1)
                    walk_edges(v, k, step, None)

                @block.scalar
                def _(a):
                    def pen_of(i, u):
                        if later(i, DEEP):
                            a.wait_ge(k.mm.sem, k.mm.at(1 - DEEP) + i)
                        a.activation(pen[u][:], k.ramp[:, 0:P], ACT.Square, scale=FAR,
                                     bias=k.dst_far[:, bass.ds(i, 1)]).then_inc(k.exped.sem, 1)

                    def half_of(i, u):
                        a.wait_ge(k.exped.sem, k.exped.at(1) + i)
                        a.activation(dh[u][:], pen[u][:], ACT.Relu, scale=-1.0,
                                     bias=L[:, bass.ds(i, 1)]).then_inc(k.copied.sem, 1)

                    def step(i, u, j, own):
                        pen_of(i, u)
                        if later(i, 1):
                            half_of(i - 1, (u - 1) % DEEP)
                    walk_edges(a, k, step, None)
                    half_of(EA - 1, (EA - 1) % DEEP)

                @block.tensor
                def _(pe):
                    clear_banks(pe, k, range(T))

                    def step(i, u, j, own):
                        pe.wait_ge(k.ready.sem, k.ready.at(1) + i)
                        pe.wait_ge(k.copied.sem, k.copied.at(1) + i)
                        for half in (dh, dl):
                            m = pe.matmul(k.ps[:, bass.ds(own[0], 1), :].rearrange("p a n -> p (a n)"), half[u][:],
                                          os_[u][:], start=False, stop=True, skip_group_check=True)
                        m.then_inc(k.mm.sem, 1)
                    walk_edges(pe, k, step)
            done((k.mm, EA), (k.ready, EA), (k.copied, EA), (k.exped, EA))
            with nc.Block() as block:
                @block.scalar
                def _(a):
                    for t in range(T):
                        i = a.activation(A[:, t, :], k.ps[:, t, :], ACT.Copy, accum_out=den[:, t:t + 1])
                    i.then_inc(k.copied.sem, 1)
                    for f in (0, 2):
                        a.wait_ge(k.tp.sem, k.tp.at(f + 1))
                        i = a.activation(AT[:, f, :], k.ps[:, f, :], ACT.Copy)
                    i.then_inc(k.copied.sem, 1)

                @block.tensor
                def _(pe):
                    pe.wait_ge(k.copied.sem, k.copied.at(1))
                    for f in range(T):
                        for t in range(T):
                            m = pe.transpose(k.ps[:, f, t * P:(t + 1) * P], A[:, t, f * P:(f + 1) * P], k.ident[:])
                        m.then_inc(k.tp.sem, 1)
                    pe.wait_ge(k.copied.sem, k.copied.at(2))
                    pe.wait_ge(k.ready.sem, k.ready.at(1))
                    for t in range(T):
                        for s in range(T):
                            m = pe.matmul(k.ps[:, T + t, :], AT[:, s, t * P:(t + 1) * P], XL[:, s, 0:D],
                                          start=(s == 0), stop=(s == T - 1))
                        m.then_inc(k.mm.sem, 1)

                @block.vector
                def _(v):
                    ch = Chain(v, k.dve_step)
                    for t in range(T):
                        v.tensor_tensor(H2[:, t, :], rows_in[:, t, :], b_out[:], ALU.add)
                    v.wait_ge(k.copied.sem, k.copied.at(1))
                    ch.link(v.tensor_scalar(den[:], den[:], 1e-16 * EX_SCALE, None, ALU.add))
                    ch.link(v.reciprocal(den[:], den[:]))
                    for f in (1, 3):
                        v.wait_ge(k.tp.sem, k.tp.at(f + 1))
                        m = v.tensor_copy(AT[:, f, :], k.ps[:, f, :])
                    m.then_inc(k.ready.sem, 1)
                    for t in range(T):
                        v.wait_ge(k.mm.sem, k.mm.at(t + 1))
                        v.scalar_tensor_tensor(H2[:, t, :], k.ps[:, T + t, :], den[:, t:t + 1], H2[:, t, :],
                                               ALU.mult, ALU.add)
                    ch.close()
            done((k.copied, 2), (k.mm, T), (k.tp, T), (k.ready, 1))


def gat(k):
    with ExitStack() as c:
        gat_setup(k, c)
        k.gat = {n: sb(c, k, n, *shape) for n, shape in dict(
            XL=([P, T, D + 1],), H2=([P, T, D],), att=([P, D],), b_out=([P, D],), eac=([P, EA],), L=([P, EA],),
            sdot=([P, EA],), me=([P, EA],), M=([P, N],), prod=([P, EA, 12],), mc=([P, T],), mrest=([P, T],),
            mp=([P, T, 3], BF16), hi16=([P, EA], F16),
            XP=([P, 3, T, D], BF16),
            ap=([P, T, 3], BF16),
        ).items()}
        k.gat["gb"] = gb = [sb(c, k, "gb", [P, D]) for _ in range(2)]

        def first(early):
            layernorm(k, k.X, k.N, k.NT, early=early)

        def later_ones(early):
            layernorm(k, k.gat["H2"], k.N, k.NT, gain=gb, relu=True, early=early)
        for l in range(3):
            gat_layer(k, l, later_ones if l else first, k.N, k.NT)
        later_ones(None)
        with k.nc.Block() as block:
            @block.vector
            def _(v):
                v.tensor_tensor(k.X[:], k.X[:], k.N[:], ALU.add)


def load(k, pairs):
    with k.nc.Block() as block:
        @block.sync
        def _(sp):
            for dst, src in pairs:
                sp.dma_start(dst, src).then_inc(k.loaded.sem, 16)
            sp.wait_ge(k.loaded.sem, k.loaded.at(16 * len(pairs)))
    done((k.loaded, 16 * len(pairs)))



def positional_ffn(k):
    nc, i_ = k.nc, k.i
    FF = 2048
    HT = FF // P
    SL = 64

    def by_expert(x, m):
        return x.rearrange("p (e m t) -> p e m t", e=EXPERTS, m=2)[:, :, m, :]

    def by_token(x, m):
        return x.rearrange("p (m e t) -> p e m t", e=EXPERTS, m=2)[:, :, m, :]

    with ExitStack() as c:
        XA = sb(c, k, "xa", [P, T, N])
        nb = sb(c, k, "nb", [P, D])
        W1 = [sb(c, k, "w1", [P, T, FF]) for _ in range(2)]
        YT = k.NT
        with ExitStack() as c2:
            gb = [sb(c2, k, "gb", [P, D]) for _ in range(2)]
            N2, N2T = sb(c2, k, "n2", [P, T, D]), sb(c2, k, "n2t", [P, T, D])
            W = sb(c2, k, "w", [P, T, D])
            ab = sb(c2, k, "ab", [P, T])

            def gains(sp):
                for j, m in enumerate((i_["L1_ffn_ln_g"], i_["L1_ffn_ln_b"])):
                    sp.dma_start(gb[j][:], bcast(m)).then_inc(k.stored[0].sem, 16)
                sp.wait_ge(k.stored[0].sem, k.stored[0].at(32))

            def weights(sp):
                sp.dma_start(ab[:], i_["attn_b"]).then_inc(k.loaded.sem, 16)
                sp.dma_start(nb[:], bcast(i_["L1_ffn_next_b"])).then_inc(k.loaded.sem, 16)
                sp.dma_start(W[:], rows_of(i_["attn_wT"])).then_inc(k.loaded.sem, 16)
                for u in range(2):
                    sp.dma_start(W1[u][:], rows_of(i_["fc1T"][u])).then_inc(k.slot[u].sem, 16)
            layernorm(k, k.X, k.N, k.NT, early=gains)
            done((k.stored[0], 32))
            layernorm(k, k.N, N2, N2T, gain=gb, early=weights)
            with nc.Block() as block:
                @block.tensor
                def _(pe):
                    pe.wait_ge(k.loaded.sem, k.loaded.at(48))
                    mm_cols(pe, k, 0, W, N2T).then_inc(k.mm.sem, 1)

                @block.vector
                def _(v):
                    v.wait_ge(k.mm.sem, k.mm.at(1))
                    for t in range(T):
                        for m in range(2):
                            v.scalar_tensor_tensor(by_expert(XA[:, t, :], m), by_token(k.ps[:, t, :], m),
                                                   ab[:, t:t + 1], by_token(k.NT[:, t, :], m), ALU.add, ALU.add)
            done((k.mm, 1), (k.loaded, 48))

        with ExitStack() as c2:
            W2 = [sb(c2, k, "w2", [P, HT, D]) for _ in range(2)]
            b1, b2 = sb(c2, k, "b1", [P, FF]), sb(c2, k, "b2", [P, D])
            h = sb(c2, k, "h", [P, FF])
            hT = k.N[:].rearrange("p a (b n) -> p (a b) n", n=P)
            yb = sb(c2, k, "yb", [P, D])
            PAIRS = EXPERTS // 2
            with nc.Block() as block:
                @block.sync
                def _(sp):
                    for j in range(PAIRS):
                        for u in range(2):
                            if j:
                                sp.wait_ge(k.mm.sem, k.mm.at(2 * j - 1 + u))
                                sp.dma_start(W1[u][:], rows_of(i_["fc1T"][2 * j + u])).then_inc(k.slot[u].sem, 16)
                        for u in range(2):
                            if j:
                                sp.wait_ge(k.out.sem, k.out.at(2 * j - 1 + u))
                            sp.dma_start(W2[u][:], rows_of(i_["fc2T"][2 * j + u])).then_inc(k.slot[2 + u].sem, 16)
                    sp.wait_ge(k.mm.sem, k.mm.at(2 * PAIRS))
                    sp.dma_start(XA[:], rows_of(i_["next_wT"])).then_inc(k.loaded.sem, 16)

                @block.gpsimd
                def _(gp):
                    for j in range(PAIRS):
                        if j:
                            gp.wait_ge(k.heads.sem, k.heads.at(j))
                        for u in range(2):
                            o = slice(u * SL, (u + 1) * SL)
                            gp.dma_start(b1[o, :], bcast(i_["L1_ffn_fc1_b"][2 * j + u], SL)
                                         ).then_inc(k.gathered.sem, 16)
                            gp.dma_start(b2[o, :], bcast(i_["L1_ffn_fc2_b"][2 * j + u], SL)
                                         ).then_inc(k.gathered.sem, 16)

                @block.tensor
                def _(pe):
                    def turn_y(j):
                        pe.wait_ge(k.heads.sem, k.heads.at(j + 1))
                        if j:
                            pe.wait_ge(k.probs.sem, k.probs.at(j))
                        for f in range(T):
                            m = pe.transpose(k.ps[:, 7, f * P:(f + 1) * P], yb[:, f * P:(f + 1) * P], k.ident[:])
                        m.then_inc(k.av.sem, 1)

                    for j in range(PAIRS):
                        for u in range(2):
                            e = 2 * j + u
                            pe.wait_ge(k.slot[u].sem, k.slot[u].at(16 * (j + 1)))
                            for q in range(T):
                                for f in range(T):
                                    m = pe.matmul(k.ps[u * SL:(u + 1) * SL, q, :], XA[:, f, e * SL:(e + 1) * SL],
                                                  W1[u][:, f, q * 512:(q + 1) * 512],
                                                  start=(f == 0), stop=(f == T - 1))
                            m.then_inc(k.mm.sem, 1)
                        if j:
                            turn_y(j - 1)
                        for q in range(T):
                            n = T * j + q
                            pe.wait_ge(k.ready.sem, k.ready.at(n + 1))
                            if n >= 2:
                                pe.wait_ge(k.copied.sem, k.copied.at(n - 1))
                            for s in range(T):
                                m = pe.transpose(k.ps[:, 4 + q % 2, s * P:(s + 1) * P],
                                                 h[:, (T * q + s) * P:(T * q + s + 1) * P], k.ident[:])
                            m.then_inc(k.tp.sem, 1)
                        pe.wait_ge(k.copied.sem, k.copied.at(T * (j + 1)))
                        for u in range(2):
                            pe.wait_ge(k.slot[2 + u].sem, k.slot[2 + u].at(16 * (j + 1)))
                            for s in range(HT):
                                m = pe.matmul(k.ps[u * SL:(u + 1) * SL, 6, :], hT[:, s, u * SL:(u + 1) * SL],
                                              W2[u][:, s, :], start=(s == 0), stop=(s == HT - 1))
                            m.then_inc(k.out.sem, 1)
                    turn_y(PAIRS - 1)

                @block.scalar
                def _(a):
                    for n in range(T * PAIRS):
                        q = n % T
                        a.wait_ge(k.tp.sem, k.tp.at(n + 1))
                        if n >= T:
                            a.wait_ge(k.out.sem, k.out.at(2 * (n // T)))
                        a.activation(hT[:, T * q:T * q + T, :].rearrange("p s n -> p (s n)"), k.ps[:, 4 + q % 2, :],
                                     ACT.Gelu).then_inc(k.copied.sem, 1)

                @block.vector
                def _(v):
                    def spread_y(j):
                        v.wait_ge(k.av.sem, k.av.at(j + 1))
                        for u in range(2):
                            for m in range(2):
                                at = m * 256 + (2 * j + u) * 32
                                i = v.tensor_copy(YT[:, :, at:at + 32], k.ps[:, 7, :].rearrange(
                                    "p (f u m t) -> p u m f t", f=T, u=2, m=2)[:, u, m])
                        i.then_inc(k.probs.sem, 1)

                    for j in range(PAIRS):
                        v.wait_ge(k.mm.sem, k.mm.at(2 * j + 2))
                        v.wait_ge(k.gathered.sem, k.gathered.at(64 * (j + 1)))
                        for q in range(T):
                            if j:
                                v.wait_ge(k.tp.sem, k.tp.at(T * (j - 1) + q + 1))
                            v.tensor_tensor(h[:, q * 512:(q + 1) * 512], k.ps[:, q, :], b1[:, q * 512:(q + 1) * 512],
                                            ALU.add).then_inc(k.ready.sem, 1)
                        if j:
                            spread_y(j - 1)
                        v.wait_ge(k.out.sem, k.out.at(2 * j + 2))
                        v.tensor_tensor(yb[:], k.ps[:, 6, :], b2[:], ALU.add).then_inc(k.heads.sem, 1)
                    spread_y(PAIRS - 1)
            done((k.slot[0], 16 * PAIRS), (k.slot[1], 16 * PAIRS), (k.slot[2], 16 * PAIRS), (k.slot[3], 16 * PAIRS),
                 (k.gathered, 64 * PAIRS), (k.mm, 2 * PAIRS), (k.tp, T * PAIRS), (k.ready, T * PAIRS),
                 (k.copied, T * PAIRS), (k.out, 2 * PAIRS), (k.heads, PAIRS), (k.av, PAIRS), (k.probs, PAIRS))

        W, o = XA, sb(c, k, "o", [P, T, D])
        with nc.Block() as block:
            @block.tensor
            def _(pe):
                pe.wait_ge(k.loaded.sem, k.loaded.at(16))
                mm_rows(pe, k, 0, YT, W).then_inc(k.mm.sem, 1)

            @block.vector
            def _(v):
                v.wait_ge(k.mm.sem, k.mm.at(1))
                for t in range(T):
                    v.tensor_tensor(o[:, t, :], k.ps[:, t, :], nb[:], ALU.add).then_inc(k.ready.sem, 1)
                for t in range(T):
                    v.wait_ge(k.copied.sem, k.copied.at(t + 1))
                    v.tensor_tensor(k.X[:, t, :], k.X[:, t, :], o[:, t, :], ALU.add)

            @block.scalar
            def _(a):
                for t in range(T):
                    a.wait_ge(k.ready.sem, k.ready.at(t + 1))
                    a.activation(o[:, t, :], o[:, t, :], ACT.Gelu).then_inc(k.copied.sem, 1)
        done((k.mm, 1), (k.ready, T), (k.copied, T), (k.loaded, 16))



def graph_conv(k):
    nc = k.nc
    with ExitStack() as c:
        W, bias = sb(c, k, "w", [P, T, D]), sb(c, k, "bias", [P, D])
        sup = sb(c, k, "sup", [P, T, D])
        AT = sb(c, k, "at", [P, T, N])
        rest = sb(c, k, "rest", [P, EB])
        wp = [sb(c, k, "wp", [P, EB], BF16) for _ in range(3)]
        wf = [sb(c, k, "wf", [P, EB]) for _ in range(3)]
        os_ = [sb(c, k, "os", [P, N], BF16) for _ in range(4)]
        dw = [[sb(c, k, "dw", [P, P], BF16) for _ in range(3)] for _ in range(4)]

        def weights(sp):
            sp.dma_start(W[:], rows_of(k.i["L2_gnn_weight"])).then_inc(k.loaded.sem, 16)
            sp.dma_start(bias[:], bcast(k.i["L2_gnn_bias"])).then_inc(k.loaded.sem, 16)
        layernorm(k, k.X, k.N, k.NT, early=weights)
        with nc.Block() as block:
            @block.tensor
            def _(pe):
                pe.wait_ge(k.loaded.sem, k.loaded.at(32))
                mm_rows(pe, k, 4, k.NT, W).then_inc(k.mm.sem, 1)

            @block.vector
            def _(v):
                ch = Chain(v, k.dve_step)
                split3(v, ch, [w[:] for w in wp], k.ew[:], rest[:])
                for q in range(3):
                    v.tensor_copy(wf[q][:], wp[q][:])
                ch.close()

            @block.scalar
            def _(a):
                a.wait_ge(k.mm.sem, k.mm.at(1))
                for t in range(T):
                    a.activation(sup[:, t, :], k.ps[:, T + t, :], ACT.Copy)
        done((k.mm, 1), (k.loaded, 32))
        with nc.Block() as block:
            @block.vector
            def _(v):
                def step(i, u):
                    if later(i, 4):
                        v.wait_ge(k.mm.sem, k.mm.at(-3) + i)
                    col = bass.ds(i, 1)
                    v.tensor_scalar(os_[u][:], k.ramp[:], k.src_f[:, col], None, ALU.is_equal)
                    for q in range(3):
                        m = v.tensor_scalar(dw[u][q][:], k.ramp[:, 0:P], k.dst_f[:, col], wf[q][:, col],
                                            ALU.is_equal, ALU.mult)
                    m.then_inc(k.ready.sem, 1)
                for u in range(4):
                    step(u, u)
                with v.Fori(1, EB // 4) as j:
                    for u in range(4):
                        step(j * 4 + u, u)

            @block.tensor
            def _(pe):
                clear_banks(pe, k, range(T))
                with pe.Fori(0, EB // 4) as j:
                    own = dst_tiles(pe, k, j * 4)
                    for u in range(4):
                        i, b = j * 4 + u, own[u]
                        pe.wait_ge(k.ready.sem, k.ready.at(1) + i)
                        for q in range(3):
                            m = pe.matmul(k.ps[:, bass.ds(b, 1), :].rearrange("p a n -> p (a n)"), dw[u][q][:],
                                          os_[u][:], start=False, stop=True, skip_group_check=True)
                        m.then_inc(k.mm.sem, 1)
        done((k.mm, EB), (k.ready, EB))
        with nc.Block() as block:
            @block.scalar
            def _(a):
                for t in range(T):
                    m = a.activation(AT[:, t, :], k.ps[:, t, :], ACT.Copy)
                m.then_inc(k.copied.sem, 1)

            @block.tensor
            def _(pe):
                pe.wait_ge(k.copied.sem, k.copied.at(1))
                mm_rows(pe, k, 4, AT, sup).then_inc(k.mm.sem, 1)

            @block.vector
            def _(v):
                ch = Chain(v, k.dve_step)
                for t in range(T):
                    last = v.tensor_tensor(k.X[:, t, :], k.X[:, t, :], bias[:], ALU.add)
                ch.link(last)
                v.wait_ge(k.mm.sem, k.mm.at(1))
                for t in range(T):
                    v.tensor_tensor(k.X[:, t, :], k.X[:, t, :], k.ps[:, T + t, :], ALU.add)
                ch.close()
        done((k.mm, 1), (k.copied, 1))



def expert_choice_ffn(k):
    nc, i_ = k.nc, k.i
    E, CAP, FF = 16, 32, 256
    HT = FF // P
    GE = P // CAP
    with ExitStack() as c:
        g = sb(c, k, "g", [P, T, E])
        sw1, sw2 = sb(c, k, "sw1", [P, T, FF]), sb(c, k, "sw2", [P, HT, D])
        sb1, sb2 = sb(c, k, "sb1", [P, HT]), sb(c, k, "sb2", [P, D])
        lg = sb(c, k, "lg", [P, T, E])
        mx, sm = sb(c, k, "mx", [P, T]), sb(c, k, "sm", [P, T])
        pr = sb(c, k, "pr", [E, N])
        val, at = sb(c, k, "val", [E, CAP]), sb(c, k, "at", [E, CAP], U32)
        at_c, atf_c, val_c = sb(c, k, "at_c", [P, T], I32), sb(c, k, "atf_c", [P, T]), sb(c, k, "val_c", [P, T])
        shT = sb(c, k, "shT", [P, HT, N])
        tok, tokT = sb(c, k, "tok", [P, T, D]), sb(c, k, "tokT", [P, T, N])
        y = sb(c, k, "y", [P, T, D])
        b1, b2 = sb(c, k, "b1", [P, E // GE, FF]), sb(c, k, "b2", [P, E // GE, D])
        back = sb(c, k, "back", [P, T, N])

        def weights(sp):
            pairs = ((g[:], rows_of(i_["L2_ffn_gate_w"])), (sw1[:], rows_of(i_["L2_ffn_sw1"])),
                     (sw2[:], i_["L2_ffn_sw2"].rearrange("(k p) n -> p k n", p=P)), (sb1[:], i_["sb1"]),
                     (sb2[:], bcast(i_["L2_ffn_sb2"])),
                     *[(b[e % GE * CAP:(e % GE + 1) * CAP, e // GE, :], bcast(m[e], CAP))
                       for b, m in ((b1, i_["L2_ffn_b1"]), (b2, i_["L2_ffn_b2"])) for e in range(E)])
            for dst, src in pairs:
                sp.dma_start(dst, src).then_inc(k.slot[0].sem, 16)
            sp.wait_ge(k.slot[0].sem, k.slot[0].at(16 * len(pairs)))
        layernorm(k, k.X, k.N, k.NT, early=weights)
        done((k.slot[0], 16 * (5 + 2 * E)))
        with nc.Block() as block:
            @block.tensor
            def _(pe):
                for t in range(T):
                    for f in range(T):
                        m = pe.matmul(k.ps[:, t, 0:E], k.NT[:, f, t * P:(t + 1) * P], g[:, f, :],
                                      start=(f == 0), stop=(f == T - 1))
                m.then_inc(k.mm.sem, 1)
                for s in range(HT):
                    for f in range(T):
                        m = pe.matmul(k.ps[:, T + s, :], sw1[:, f, s * P:(s + 1) * P], k.NT[:, f, :],
                                      start=(f == 0), stop=(f == T - 1))
                m.then_inc(k.mm.sem, 1)
                pe.wait_ge(k.ready.sem, k.ready.at(2))
                for t in range(T):
                    m = pe.transpose(k.ps[0:E, 6, t * P:(t + 1) * P], lg[:, t, :], k.ident[:])
                m.then_inc(k.mm.sem, 1)

            @block.vector
            def _(v):
                ch = Chain(v, k.dve_step)
                v.wait_ge(k.mm.sem, k.mm.at(1))
                ch.link(v.tensor_reduce(mx[:], k.ps[:, 0:T, 0:E], AX.X, ALU.max))
                for t in range(T):
                    m = v.tensor_scalar(lg[:, t, :], k.ps[:, t, 0:E], mx[:, t:t + 1], None, ALU.subtract)
                m.then_inc(k.ready.sem, 1)
                v.wait_ge(k.copied.sem, k.copied.at(1))
                ch.link(v.tensor_reduce(sm[:], lg[:], AX.X, ALU.add))
                ch.link(v.reciprocal(sm[:], sm[:]))
                for t in range(T):
                    m = v.tensor_scalar(lg[:, t, :], lg[:, t, :], sm[:, t:t + 1], None, ALU.mult)
                m.then_inc(k.ready.sem, 1)
                v.wait_ge(k.mm.sem, k.mm.at(3))
                ch.link(v.tensor_copy(pr[:], k.ps[0:E, 6, :]))
                for q in range(CAP // 8):
                    o = slice(8 * q, 8 * q + 8)
                    ch.link(v.max(val[:, o], pr[:]))
                    ch.link(v.max_index(at[:, o], val[:, o], pr[:]))
                    if q < CAP // 8 - 1:
                        ch.link(v.match_replace(pr[:], val[:, o], pr[:], -1.0))
                v.tensor_copy(sm[0:E, 0:1], val[:, 0:1]).then_inc(k.ready.sem, 1)
                v.wait_ge(k.loaded.sem, k.loaded.at(64))
                ch.link(v.tensor_copy(atf_c[:], at_c[:]))
                for t in range(T):
                    v.tensor_scalar(back[:, t, :], k.ramp_f[:], atf_c[:, t:t + 1], val_c[:, t:t + 1],
                                    ALU.is_equal, ALU.mult)
                ch.close()

            @block.scalar
            def _(a):
                a.wait_ge(k.ready.sem, k.ready.at(1))
                a.activation(lg[:], lg[:], ACT.Exp).then_inc(k.copied.sem, 1)
                a.wait_ge(k.mm.sem, k.mm.at(2))
                for s in range(HT):
                    a.activation(shT[:, s, :], k.ps[:, T + s, :], ACT.Gelu_apprx_tanh, bias=sb1[:, s:s + 1])

            @block.sync
            def _(sp):
                sp.dma_start(rows_of(k.rows_d), k.N[:]).then_inc(k.stored[0].sem, 16)
                sp.wait_ge(k.ready.sem, k.ready.at(3))
                sp.dma_start(k.at_d.rearrange("(e j) -> e j", e=E), at[:].bitcast(I32)).then_inc(k.loaded.sem, 16)
                sp.dma_start(k.val_d.rearrange("(e j) -> e j", e=E), val[:]).then_inc(k.loaded.sem, 16)
                sp.wait_ge(k.loaded.sem, k.loaded.at(32))
                with nc.allow_non_contiguous_dma(reason="512 words"):
                    sp.dma_start(at_c[:], k.at_d.rearrange("(t p) -> p t", p=P)).then_inc(k.loaded.sem, 16)
                    sp.dma_start(val_c[:], k.val_d.rearrange("(t p) -> p t", p=P)).then_inc(k.loaded.sem, 16)

            @block.gpsimd
            def _(gp):
                gp.wait_ge(k.loaded.sem, k.loaded.at(64))
                gp.wait_ge(k.stored[0].sem, k.stored[0].at(16))
                for t in range(T):
                    gp.indirect_dma_start(tok[:, t, :], None, k.rows_d,
                                          bass.IndirectOffsetOnAxis(ap=at_c[:, t:t + 1].bitcast(U32), axis=0)
                                          ).then_inc(k.gathered.sem, 16)
                gp.wait_ge(k.gathered.sem, k.gathered.at(16 * T))
        done((k.mm, 3), (k.ready, 3), (k.copied, 1), (k.loaded, 64), (k.gathered, 16 * T), (k.stored[0], 16))

        def turn(src, dst):
            with nc.Block() as block:
                @block.tensor
                def _(pe):
                    for f in range(T):
                        for t in range(T):
                            m = pe.transpose(k.ps[:, f, t * P:(t + 1) * P], src[:, t, f * P:(f + 1) * P], k.ident[:])
                        m.then_inc(k.mm.sem, 1)

                @block.vector
                def _(v):
                    for f in (0, 2):
                        v.wait_ge(k.mm.sem, k.mm.at(f + 1))
                        v.tensor_copy(dst[:, f, :], k.ps[:, f, :])

                @block.scalar
                def _(a):
                    for f in (1, 3):
                        a.wait_ge(k.mm.sem, k.mm.at(f + 1))
                        a.activation(dst[:, f, :], k.ps[:, f, :], ACT.Copy)
            done((k.mm, T))

        turn(tok, tokT)
        with ExitStack() as c2:
            W1 = [sb(c2, k, "w1", [P, GE * T, FF]) for _ in range(2)]
            W2 = [sb(c2, k, "w2", [P, GE * HT, D]) for _ in range(2)]
            h = [sb(c2, k, "h", [P, FF]) for _ in range(2)]
            hT = [sb(c2, k, "hT", [P, HT, P]) for _ in range(2)]
            GROUPS = E // GE
            with nc.Block() as block:
                @block.sync
                def _(sp):
                    for g in range(GROUPS):
                        e = slice(g * GE, (g + 1) * GE)
                        if g >= 2:
                            sp.wait_ge(k.mm.sem, k.mm.at(g - 1))
                        sp.dma_start(W1[g % 2][:], i_["L2_ffn_w1"][e].rearrange("e (k p) n -> p (e k) n", p=P)
                                     ).then_inc(k.slot[g % 2].sem, 16)
                        if g >= 2:
                            sp.wait_ge(k.out.sem, k.out.at(g - 1))
                        sp.dma_start(W2[g % 2][:], i_["L2_ffn_w2"][e].rearrange("e (k p) n -> p (e k) n", p=P)
                                     ).then_inc(k.slot[2 + g % 2].sem, 16)

                @block.tensor
                def _(pe):
                    def first(g):
                        pe.wait_ge(k.slot[g % 2].sem, k.slot[g % 2].at(16 * (g // 2 + 1)))
                        if g >= 2:
                            pe.wait_ge(k.ready.sem, k.ready.at(g - 1))
                        for q in range(GE):
                            e = g * GE + q
                            for f in range(T):
                                m = pe.matmul(k.ps[q * CAP:(q + 1) * CAP, g % 2, 0:FF],
                                              tokT[:, f, e * CAP:(e + 1) * CAP], W1[g % 2][:, q * T + f, :],
                                              start=(f == 0), stop=(f == T - 1))
                        m.then_inc(k.mm.sem, 1)

                    def second(g):
                        pe.wait_ge(k.exped.sem, k.exped.at(g + 1))
                        for s in range(HT):
                            m = pe.transpose(k.ps[:, 2 + g % 2, s * P:(s + 1) * P], h[g % 2][:, s * P:(s + 1) * P],
                                             k.ident[:])
                        m.then_inc(k.tp.sem, 1)
                        pe.wait_ge(k.turned[0].sem, k.turned[0].at(g + 1))
                        pe.wait_ge(k.slot[2 + g % 2].sem, k.slot[2 + g % 2].at(16 * (g // 2 + 1)))
                        if g >= 2:
                            pe.wait_ge(k.heads.sem, k.heads.at(g - 1))
                        for q in range(GE):
                            for s in range(HT):
                                m = pe.matmul(k.ps[q * CAP:(q + 1) * CAP, 4 + g % 2, :],
                                              hT[g % 2][:, s, q * CAP:(q + 1) * CAP], W2[g % 2][:, q * HT + s, :],
                                              start=(s == 0), stop=(s == HT - 1))
                        m.then_inc(k.out.sem, 1)
                    for g in range(GROUPS + 1):
                        if g < GROUPS:
                            first(g)
                        if g:
                            second(g - 1)

                @block.vector
                def _(v):
                    for g in range(GROUPS + 1):
                        if g < GROUPS:
                            v.wait_ge(k.mm.sem, k.mm.at(g + 1))
                            if g >= 2:
                                v.wait_ge(k.tp.sem, k.tp.at(g - 1))
                            v.tensor_tensor(h[g % 2][:], k.ps[:, g % 2, 0:FF], b1[:, g, :], ALU.add
                                            ).then_inc(k.ready.sem, 1)
                        if g:
                            v.wait_ge(k.out.sem, k.out.at(g))
                            v.tensor_tensor(y[:, g - 1, :], k.ps[:, 4 + (g - 1) % 2, :], b2[:, g - 1, :], ALU.add
                                            ).then_inc(k.heads.sem, 1)

                @block.scalar
                def _(a):
                    for g in range(GROUPS):
                        a.wait_ge(k.ready.sem, k.ready.at(g + 1))
                        a.activation(h[g % 2][:], h[g % 2][:], ACT.Gelu_apprx_tanh).then_inc(k.exped.sem, 1)
                        a.wait_ge(k.tp.sem, k.tp.at(g + 1))
                        if g >= 2:
                            a.wait_ge(k.out.sem, k.out.at(g - 1))
                        a.activation(hT[g % 2][:].rearrange("p s n -> p (s n)"), k.ps[:, 2 + g % 2, 0:HT * P],
                                     ACT.Copy).then_inc(k.turned[0].sem, 1)
            done((k.mm, GROUPS), (k.ready, GROUPS), (k.exped, GROUPS), (k.tp, GROUPS), (k.turned[0], GROUPS),
                 (k.out, GROUPS), (k.heads, GROUPS), *[(k.slot[u], 16 * GROUPS // 2) for u in range(4)])
        with nc.Block() as block:
            @block.tensor
            def _(pe):
                for t in range(T):
                    for s in range(HT):
                        pe.matmul(k.ps[:, T + t, :], shT[:, s, t * P:(t + 1) * P], sw2[:, s, :],
                                  start=(s == 0), stop=False)
                    for s in range(T):
                        m = pe.matmul(k.ps[:, T + t, :], back[:, s, t * P:(t + 1) * P], y[:, s, :],
                                      start=False, stop=(s == T - 1))
                    m.then_inc(k.mm.sem, 1)

            @block.vector
            def _(v):
                ch = Chain(v, k.dve_step)
                for t in range(T):
                    last = v.tensor_tensor(k.X[:, t, :], k.X[:, t, :], sb2[:], ALU.add)
                ch.link(last)
                for t in range(T):
                    v.wait_ge(k.mm.sem, k.mm.at(t + 1))
                    v.tensor_tensor(k.X[:, t, :], k.X[:, t, :], k.ps[:, T + t, :], ALU.add)
                ch.close()
        done((k.mm, T))



def sage(k):
    nc, i_ = k.nc, k.i
    E = 4
    with ExitStack() as c:
        masks, wt = routing(k, c, k.NT, i_["L3_gnn_gate_W"], i_["L3_gnn_gate_b"], E, "gates", 2)
        wE = sb(c, k, "wE", [P, T, 8])
        A0 = sb(c, k, "A0", [P, T, N])
        H1, PR, o = [sb(c, k, n, [P, T, D]) for n in ("H1", "PR", "o")]
        W = [[sb(c, k, "w", [P, T, D]) for _ in range(4)] for _ in range(2)]
        b0 = [sb(c, k, "b0", [P, T]) for _ in range(2)]
        b1 = [sb(c, k, "b1", [P, D]) for _ in range(2)]

        def weights(sp, e, u):
            for q, m in enumerate((i_["L3_gnn_Wl"], i_["L3_gnn_Wr"])):
                for l in range(2):
                    sp.dma_start(W[u][2 * l + q][:], m[bass.ds(e, 1), l].rearrange(
                        "a (k p) n -> p (a k) n", p=P)).then_inc(k.slot[u].sem, 16)
            sp.dma_start(b0[u][:], i_["sage_b0"][bass.ds(e, 1)].rearrange("a p m -> p (a m)")
                         ).then_inc(k.slot[u].sem, 16)
            sp.dma_start(b1[u][:], i_["sage_b1"][bass.ds(e, 1), :].to_broadcast([P, D])
                         ).then_inc(k.slot[u].sem, 16)
        with nc.Block() as block:
            @block.sync
            def _(sp):
                for u in range(2):
                    weights(sp, u, u)

            @block.tensor
            def _(pe):
                mm_cols(pe, k, 0, k.N, k.Cn).then_inc(k.mm.sem, 1)

            @block.scalar
            def _(a):
                a.wait_ge(k.mm.sem, k.mm.at(1))
                for t in range(T):
                    a.activation(A0[:, t, :], k.ps[:, t, :], ACT.Copy)

            @block.vector
            def _(v):
                ch = Chain(v, k.dve_step)
                for t in range(T):
                    ch.link(v.tensor_scalar(wE[:, t, :], masks[:, t, 0, :], wt[:, t, 0:1], None, ALU.mult))
                    ch.link(v.scalar_tensor_tensor(wE[:, t, :], masks[:, t, 1, :], wt[:, t, 1:2], wE[:, t, :],
                                                   ALU.mult, ALU.add))
                ch.close()
        done((k.mm, 1))
        with nc.Block() as block:
            def walk(eng, step):
                for u in range(2):
                    step(u, u, 0)
                with eng.Fori(1, E // 2) as j:
                    for u in range(2):
                        step(j * 2 + u, u, j)

            @block.sync
            def _(sp):
                for e in range(2, E):
                    sp.wait_ge(k.heads.sem, k.heads.at(e - 1))
                    weights(sp, e, e % 2)

            @block.tensor
            def _(pe):
                def step(e, u, j):
                    pe.wait_ge(k.slot[u].sem, k.slot[u].at(96) + j * 96)
                    if later(e, 1):
                        pe.wait_ge(k.heads.sem, k.heads.at(0) + e)
                    for t in range(T):
                        for w, x in ((W[u][0], A0), (W[u][1], k.NT)):
                            for f in range(T):
                                m = pe.matmul(k.ps[:, t, :], w[:, f, t * P:(t + 1) * P], x[:, f, :],
                                              start=(f == 0 and x is A0), stop=(f == T - 1 and x is not A0))
                        m.then_inc(k.mm.sem, 1)
                    pe.wait_ge(k.copied.sem, k.copied.at(1) + e)
                    for t in range(T):
                        for f in range(T):
                            m = pe.matmul(k.ps[:, T + t, :], H1[:, f, t * P:(t + 1) * P], W[u][2][:, f, :],
                                          start=(f == 0), stop=(f == T - 1))
                        m.then_inc(k.tp.sem, 1)
                    mm_rows(pe, k, 0, H1, W[u][3], stop=False)
                    pe.wait_ge(k.ready.sem, k.ready.at(1) + e)
                    for t in range(T):
                        for s in range(T):
                            m = pe.matmul(k.ps[:, t, :], k.Cn[:, s, t * P:(t + 1) * P], PR[:, s, :],
                                          start=False, stop=(s == T - 1))
                        m.then_inc(k.out.sem, 1)
                walk(pe, step)

            @block.scalar
            def _(a):
                def step(e, u, j):
                    for t in range(T):
                        a.wait_ge(k.mm.sem, k.mm.at(t + 1) + e * T)
                        m = a.activation(H1[:, t, :], k.ps[:, t, :], ACT.Relu, bias=b0[u][:, t:t + 1])
                    m.then_inc(k.copied.sem, 1)
                walk(a, step)

            @block.vector
            def _(v):
                ch = Chain(v, k.dve_step)

                def step(e, u, j):
                    ch.n, ch.loop = 2 * T * u, j * (4 * T)
                    for t in range(T):
                        v.wait_ge(k.tp.sem, k.tp.at(t + 1) + e * T)
                        m = v.tensor_copy(PR[:, t, :], k.ps[:, T + t, :])
                    m.then_inc(k.ready.sem, 1)
                    for t in range(T):
                        v.wait_ge(k.out.sem, k.out.at(t + 1) + e * T)
                        ch.link(v.tensor_tensor(o[:, t, :], k.ps[:, t, :], b1[u][:], ALU.add))
                        ch.link(v.tensor_scalar(o[:, t, :], o[:, t, :], 0.0, wE[:, t, bass.ds(e, 1)],
                                                ALU.max, ALU.mult))
                        m = v.tensor_tensor(k.X[:, t, :], k.X[:, t, :], o[:, t, :], ALU.add)
                    m.then_inc(k.heads.sem, 1)
                    v.wait_ge(k.heads.sem, k.heads.at(1) + e)
                walk(v, step)
                ch.close(2 * T * E)
        done((k.heads, E), (k.slot[0], 48 * E), (k.slot[1], 48 * E), (k.mm, T * E), (k.copied, E), (k.ready, E),
             (k.tp, T * E), (k.out, T * E))



def program(nc, i, y):
    with ExitStack() as c:
        k = Kernel(nc, i)
        (k.loaded, k.mm, k.ready, k.copied, k.maxed, k.exped, k.probs, k.tp, k.av, k.heads, k.out, k.gathered,
         k.dve_step, k.pool_step) = [Ticker(c.enter_context(nc.semaphore(n))) for n in (
             "loaded", "mm", "ready", "copied", "maxed", "exped", "probs", "tp", "av", "heads", "out", "gathered",
             "dve_step", "pool_step")]
        k.slot = [Ticker(c.enter_context(nc.semaphore(f"slot{j}"))) for j in range(6)]
        k.pool_slot = [Ticker(c.enter_context(nc.semaphore(f"pool_slot{j}"))) for j in range(DEEP)]
        k.pool_stored = [Ticker(c.enter_context(nc.semaphore(f"pool_stored{j}"))) for j in range(2)]
        k.turned = [Ticker(c.enter_context(nc.semaphore(f"turned{j}"))) for j in range(2)]
        k.stored = [Ticker(c.enter_context(nc.semaphore(f"stored{j}"))) for j in range(2)]
        k.ps = c.enter_context(nc.psum_tensor("ps", [P, 8, 512], F32))
        k.psb = k.ps[:].bitcast(BF16)
        k.X, k.N, k.NT, k.Cn = [sb(c, k, n, [P, T, D]) for n in ("X", "N", "NT", "Cn")]
        k.ident, k.ones, k.before = [sb(c, k, n, [P, P]) for n in ("ident", "ones", "before")]
        k.identb = sb(c, k, "identb", [P, P], BF16)
        k.zrow, k.ramp_f = sb(c, k, "zrow", [P, N]), sb(c, k, "ramp_f", [P, N])
        k.ramp, k.ramp_i = sb(c, k, "ramp", [P, N], F16), sb(c, k, "ramp_i", [P, N], I32)
        k.node_i, k.node_f = sb(c, k, "node_i", [P, T], I32), sb(c, k, "node_f", [P, T])
        k.src_i, k.own = sb(c, k, "src_i", [P, EA], I32), sb(c, k, "own", [P, EA], I32)
        k.ew, k.zero16 = sb(c, k, "ew", [P, EB]), sb(c, k, "zero16", [P, N], BF16)
        k.src_f, k.dst_f = sb(c, k, "src_f", [P, EA]), sb(c, k, "dst_f", [P, EA])
        k.ea = sb(c, k, "ea", [P, EA, 2])
        k.inv_deg, k.has_out = sb(c, k, "inv_deg", [P, T]), sb(c, k, "has_out", [P, T])
        k.eps = sb(c, k, "eps", [P, 1])
        G0, G3 = (N + EXPERTS * (P - 1)) // P, (2 * N + EXPERTS * (P - 1)) // P
        k.xl_d = nc.dram_tensor("xl_d", (N, D + 1), F32).ap()
        k.edges_d = nc.dram_tensor("edges_d", (EB * P, WORDS), F32).ap()
        k.rows_d = nc.dram_tensor("rows_d", (N, D), F32).ap()
        k.at_d, k.val_d = nc.dram_tensor("at_d", (N,), I32).ap(), nc.dram_tensor("val_d", (N,), F32).ap()
        spread, result = [nc.dram_tensor(n, (G3 * P, D), F32).ap() for n in ("spread_d", "result_d")]

        with ExitStack() as c0:
            k.C, k.no_edge = [sb(c0, k, n, [P, T, D]) for n in ("C", "no_edge")]
            constants(k)
            with ExitStack() as c_edges:
                edge_slots(k, c_edges)
                adjacency(k)

            attention(k, dict(Wq=i["L0_gnn_Wq"], Wk=i["L0_gnn_Wk"], Wv=i["L0_gnn_Wv"], Wo=i["L0_gnn_Wo"], bq=i["g_bq"],
                                         bk=i["g_bk"], bv=i["L0_gnn_bv"], bo=i["L0_gnn_bo"]), k.no_edge, k.X, k.X)
        with ExitStack() as c1:
            O = sb(c1, k, "O", [P, T, D])
            attention(k, dict(Wq=i["L0_ffn_Wq"], Wk=i["L0_ffn_Wk"], Wv=i["L0_ffn_Wv"], Wo=i["L0_ffn_Wo"], bq=i["f_bq"],
                                         bk=i["f_bk"], bv=i["L0_ffn_bv"], bo=i["L0_ffn_bo"]), None, k.N, O)
            with ExitStack() as c2:
                gb = [sb(c2, k, "gb", [P, D]) for _ in range(2)]
                load(k, ((gb[0][:], bcast(i["L0_ffn_ln1_g"])), (gb[1][:], bcast(i["L0_ffn_ln1_b"]))))
                layernorm(k, O, k.N, k.NT, gain=gb, early=empty_slots(k, G0, spread))
                done((k.stored[1], 16 * G0))
        routed_ffn(k, k.NT, k.N, i["L0_ffn_gate_W"], i["L0_ffn_gate_b"], "top1", 1, G0,
                   dict(W1=i["L0_ffn_W1"], W2=i["L0_ffn_W2"], b1=i["l0b1"], b2=i["L0_ffn_b2"]),
                   2048, False, spread, result)

        gat(k)
        positional_ffn(k)

        graph_conv(k)
        expert_choice_ffn(k)

        layernorm(k, k.X, k.N, k.NT)
        sage(k)
        layernorm(k, k.X, k.N, k.NT, early=empty_slots(k, G3, spread))
        done((k.stored[1], 16 * G3))
        routed_ffn(k, k.NT, k.N, i["router_wT"], None, "top2", 2, G3,
                   dict(Wg=i["L3_ffn_w_gate"], Wu=i["L3_ffn_w_up"], Wd=i["L3_ffn_w_down"]), 1024, True,
                   spread, result)
        store(k, y)


def store(k, y):
    with k.nc.Block() as block:
        @block.sync
        def _(sp):
            sp.dma_start(rows_of(y), k.X[:]).then_inc(k.stored[0].sem, 16)
            sp.wait_ge(k.stored[0].sem, k.stored[0].at(16))



def kernel(**inputs):
    import concourse.bacc as bacc
    from concourse.bass_utils import run_bass_kernel_spmd

    given = {n: np.asarray(a) for n, a in inputs.items()}

    def columns(v, tiles):
        return np.ascontiguousarray(np.swapaxes(v.reshape(*v.shape[:-1], tiles, P), -1, -2))

    def turned(w):
        return np.ascontiguousarray(np.swapaxes(w, -1, -2))

    laid = {
        "g_bq": columns(given["L0_gnn_bq"], T), "g_bk": columns(given["L0_gnn_bk"], T),
        "f_bq": columns(given["L0_ffn_bq"], T), "f_bk": columns(given["L0_ffn_bk"], T),
        "l0b1": columns(given["L0_ffn_b1"], 16), "attn_b": columns(given["L1_ffn_attn_b"], T),
        "attn_wT": turned(given["L1_ffn_attn_w"]), "next_wT": turned(given["L1_ffn_next_w"]),
        "fc1T": turned(given["L1_ffn_fc1_w"]), "fc2T": turned(given["L1_ffn_fc2_w"]),
        "sb1": columns(given["L2_ffn_sb1"], 2),
        "sage_b0": columns(given["L3_gnn_bl"][:, 0], T), "sage_b1": np.ascontiguousarray(given["L3_gnn_bl"][:, 1]),
        "router_wT": turned(given["L3_ffn_router_w"]),
    }
    unused = {"L0_gnn_bq", "L0_gnn_bk", "L0_ffn_bq", "L0_ffn_bk", "L0_ffn_b1", "L1_ffn_attn_b", "L1_ffn_attn_w",
              "L1_ffn_next_w", "L1_ffn_fc1_w", "L1_ffn_fc2_w", "L1_ffn_gate_w", "L2_ffn_sb1", "L3_gnn_bl",
              "L3_ffn_router_w"}
    laid.update({n: np.ascontiguousarray(a) for n, a in given.items() if n not in unused})
    nc = bacc.Bacc("TRN2", target_bir_lowering=False, num_devices=1)
    i = {n: nc.dram_tensor(n, a.shape, mybir.dt.from_np(a.dtype), kind="ExternalInput").ap()
         for n, a in laid.items()}
    y = nc.dram_tensor("y", (N, D), F32, kind="ExternalOutput").ap()
    program(nc, i, y)
    return run_bass_kernel_spmd(nc, [laid], core_ids=[0]).results[0]["y"]
```
